# Optimizing a Trainium2 kernel written in Bass

```python
import numpy as np
import jax
import jax.numpy as jnp

def _softmax(x, axis=-1):
    return jax.nn.softmax(x, axis=axis)

def _gelu(x):
    return jax.nn.gelu(x, approximate=True)

def _silu(x):
    return jax.nn.silu(x)

def _sigmoid(x):
    return jax.nn.sigmoid(x)

def _layernorm(x, axis=-1, eps=1e-05):
    m = jnp.mean(x, axis=axis, keepdims=True)
    v = jnp.var(x, axis=axis, keepdims=True)
    return (x - m) / jnp.sqrt(v + eps)

def _scatter_add(tgt, idx, src, axis=0):
    return tgt.at[idx].add(src)

def _segment_sum(src, seg, n):
    return jax.ops.segment_sum(src, seg, n)
kernel_name = 'mk_sandwich_d1_jaxref_r8_29bc3e'

def setup_inputs(seed: int=0):
    np.random.seed(seed)
    _w = jnp.asarray

    def _L0_attn_setup():
        import jax, jax.numpy as jnp
        import numpy as np
        D_MODEL = 512
        D_XB = 128
        D_INNER = 512
        HEADDIM = 128
        DSTATE = 128
        NHEADS = D_INNER // HEADDIM
        DCONV = 4
        INTER = 1792
        EPS = 1e-05
        CHUNK = 128

        def rmsnorm(x, w):
            return x * jax.lax.rsqrt(jnp.mean(x * x, axis=-1, keepdims=True) + EPS) * w

        def silu(x):
            return x * jax.nn.sigmoid(x)

        def mamba2(x, w_in, conv_w, conv_b, A_log, D, dt_bias, w_out):
            B, L, _ = x.shape
            H, P, N = (NHEADS, HEADDIM, DSTATE)
            G = D_XB // P
            rep = H // G
            zxbcdt = x @ w_in.T
            z, xs, Bs, Cs, dt = jnp.split(zxbcdt, [D_INNER, D_INNER + D_XB, D_INNER + 2 * D_XB, 2 * D_INNER + 2 * D_XB], axis=-1)
            xBC = jnp.concatenate([xs, Bs, Cs], axis=-1)
            conv = jax.lax.conv_general_dilated(xBC.transpose(0, 2, 1), conv_w[:, None, :], (1,), [(DCONV - 1, 0)], feature_group_count=conv_w.shape[0])
            xBC = silu(conv.transpose(0, 2, 1) + conv_b)
            xs, Bs, Cs = jnp.split(xBC, [D_XB, 2 * D_XB], axis=-1)
            dt = jax.nn.softplus(dt + dt_bias)
            A = -jnp.exp(A_log)
            xh = jnp.repeat(xs.reshape(B, L, G, P), rep, axis=2)
            Bh = jnp.repeat(Bs.reshape(B, L, G, N), rep, axis=2)
            Ch = Cs.reshape(B, L, H, N)
            c, Q = (L // CHUNK, CHUNK)
            a = (dt * A).reshape(B, c, Q, H).transpose(0, 1, 3, 2)
            dtc = dt.reshape(B, c, Q, H).transpose(0, 1, 3, 2)
            Xc = xh.reshape(B, c, Q, H, P).transpose(0, 1, 3, 2, 4)
            Bc = Bh.reshape(B, c, Q, H, N).transpose(0, 1, 3, 2, 4)
            Cc = Ch.reshape(B, c, Q, H, N).transpose(0, 1, 3, 2, 4)
            cs = jnp.cumsum(a, axis=-1)
            tri = jnp.tril(jnp.ones((Q, Q), bool))
            Ldec = jnp.where(tri, jnp.exp(cs[..., :, None] - cs[..., None, :]), 0.0)
            Xdt = Xc * dtc[..., None]
            att = jnp.einsum('bchqn,bchkn->bchqk', Cc, Bc) * Ldec
            Yd = jnp.einsum('bchqk,bchkp->bchqp', att, Xdt)
            dec_end = jnp.exp(cs[..., -1:] - cs)
            states = jnp.einsum('bchq,bchqn,bchqp->bchpn', dec_end, Bc, Xdt)
            g = jnp.exp(cs[..., -1])

            def step(S, inp):
                gk, st = inp
                return (gk[:, :, None, None] * S + st, S)
            S0 = jnp.zeros((B, H, P, N), x.dtype)
            _, prev = jax.lax.scan(step, S0, (g.transpose(1, 0, 2), states.transpose(1, 0, 2, 3, 4)))
            prev = prev.transpose(1, 0, 2, 3, 4)
            Yo = jnp.einsum('bchqn,bchpn,bchq->bchqp', Cc, prev, jnp.exp(cs))
            Y = (Yd + Yo).transpose(0, 1, 3, 2, 4).reshape(B, L, H, P)
            Y = Y + D[:, None] * xh
            y = Y.reshape(B, L, D_INNER) * silu(z)
            return y @ w_out.T
        key = jax.random.key(seed)
        ks = jax.random.split(key, 10)
        B, L = (2, 256)
        proj_out = 2 * D_INNER + 2 * D_XB + NHEADS
        conv_dim = 2 * D_XB + D_INNER
        return {'hidden_states': jax.random.normal(ks[0], (B, L, D_MODEL), jnp.float32), 'w_in': jax.random.normal(ks[1], (proj_out, D_MODEL), jnp.float32) * 0.02, 'conv_w': jax.random.normal(ks[2], (conv_dim, DCONV), jnp.float32) * 0.1, 'conv_b': jnp.zeros((conv_dim,), jnp.float32), 'A_log': jnp.log(jnp.arange(1, NHEADS + 1, dtype=jnp.float32)), 'D': jnp.ones((NHEADS,), jnp.float32), 'dt_bias': jax.random.normal(ks[3], (NHEADS,), jnp.float32) * 0.1, 'w_out': jax.random.normal(ks[4], (D_MODEL, D_INNER), jnp.float32) * 0.02, 'ln1_w': jnp.ones((D_MODEL,), jnp.float32), 'ln2_w': jnp.ones((D_MODEL,), jnp.float32), 'gate_w': jax.random.normal(ks[5], (INTER, D_MODEL), jnp.float32) * 0.02, 'up_w': jax.random.normal(ks[6], (INTER, D_MODEL), jnp.float32) * 0.02, 'down_w': jax.random.normal(ks[7], (D_MODEL, INTER), jnp.float32) * 0.02}
    _L0_attn_in = _L0_attn_setup()

    def _L0_ffn_setup():
        import jax, jax.numpy as jnp
        import numpy as np
        B_, S, D_IN, D_OUT = (4, 256, 512, 512)
        N, RANK, ALPHA = (8, 16, 32)
        SCALE = ALPHA / RANK
        key = jax.random.key(seed)
        kx, ka, kb, kw, kbias = jax.random.split(key, 5)
        x = jax.random.normal(kx, (B_, S, D_IN), dtype=jnp.float32)
        lora_A = jax.random.normal(ka, (N, RANK, D_IN), dtype=jnp.float32) * (1.0 / np.sqrt(D_IN))
        lora_B = jax.random.normal(kb, (N, D_OUT, RANK), dtype=jnp.float32) * (1.0 / np.sqrt(RANK))
        W = jax.random.normal(kw, (D_OUT, D_IN), dtype=jnp.float32) * (1.0 / np.sqrt(D_IN))
        bias = jax.random.normal(kbias, (D_OUT,), dtype=jnp.float32) * 0.01
        lora_weights = jnp.full((N,), 1.0 / N, dtype=jnp.float32)
        return {'x': x, 'lora_A': lora_A, 'lora_B': lora_B, 'W': W, 'bias': bias, 'lora_weights': lora_weights}
    _L0_ffn_in = _L0_ffn_setup()
    _d = {'L0_attn_hidden_states': _L0_attn_in['hidden_states'], 'L0_attn_w_in': _L0_attn_in['w_in'], 'L0_attn_conv_w': _L0_attn_in['conv_w'], 'L0_attn_conv_b': _L0_attn_in['conv_b'], 'L0_attn_A_log': _L0_attn_in['A_log'], 'L0_attn_D': _L0_attn_in['D'], 'L0_attn_dt_bias': _L0_attn_in['dt_bias'], 'L0_attn_w_out': _L0_attn_in['w_out'], 'L0_attn_ln1_w': _L0_attn_in['ln1_w'], 'L0_attn_ln2_w': _L0_attn_in['ln2_w'], 'L0_attn_gate_w': _L0_attn_in['gate_w'], 'L0_attn_up_w': _L0_attn_in['up_w'], 'L0_attn_down_w': _L0_attn_in['down_w'], 'L0_ffn_lora_A': _L0_ffn_in['lora_A'], 'L0_ffn_lora_B': _L0_ffn_in['lora_B'], 'L0_ffn_W': _L0_ffn_in['W'], 'L0_ffn_bias': _L0_ffn_in['bias'], 'L0_ffn_lora_weights': _L0_ffn_in['lora_weights']}
    _x0 = _d['L0_attn_hidden_states']
    _d['L0_attn_hidden_states'] = jax.random.normal(jax.random.fold_in(jax.random.key(seed), 1), (2, 1024, 512), dtype=_x0.dtype)
    del _x0
    return _d

def reference(L0_attn_hidden_states, L0_attn_w_in, L0_attn_conv_w, L0_attn_conv_b, L0_attn_A_log, L0_attn_D, L0_attn_dt_bias, L0_attn_w_out, L0_attn_ln1_w, L0_attn_ln2_w, L0_attn_gate_w, L0_attn_up_w, L0_attn_down_w, L0_ffn_lora_A, L0_ffn_lora_B, L0_ffn_W, L0_ffn_bias, L0_ffn_lora_weights):

    def _L0_attn_ref(hidden_states, w_in, conv_w, conv_b, A_log, D, dt_bias, w_out, ln1_w, ln2_w, gate_w, up_w, down_w):
        import jax, jax.numpy as jnp
        import numpy as np
        D_MODEL = 512
        D_XB = 128
        D_INNER = 512
        HEADDIM = 128
        DSTATE = 128
        NHEADS = D_INNER // HEADDIM
        DCONV = 4
        INTER = 1792
        EPS = 1e-05
        CHUNK = 128

        def rmsnorm(x, w):
            return x * jax.lax.rsqrt(jnp.mean(x * x, axis=-1, keepdims=True) + EPS) * w

        def silu(x):
            return x * jax.nn.sigmoid(x)

        def mamba2(x, w_in, conv_w, conv_b, A_log, D, dt_bias, w_out):
            B, L, _ = x.shape
            H, P, N = (NHEADS, HEADDIM, DSTATE)
            G = D_XB // P
            rep = H // G
            zxbcdt = x @ w_in.T
            z, xs, Bs, Cs, dt = jnp.split(zxbcdt, [D_INNER, D_INNER + D_XB, D_INNER + 2 * D_XB, 2 * D_INNER + 2 * D_XB], axis=-1)
            xBC = jnp.concatenate([xs, Bs, Cs], axis=-1)
            conv = jax.lax.conv_general_dilated(xBC.transpose(0, 2, 1), conv_w[:, None, :], (1,), [(DCONV - 1, 0)], feature_group_count=conv_w.shape[0])
            xBC = silu(conv.transpose(0, 2, 1) + conv_b)
            xs, Bs, Cs = jnp.split(xBC, [D_XB, 2 * D_XB], axis=-1)
            dt = jax.nn.softplus(dt + dt_bias)
            A = -jnp.exp(A_log)
            xh = jnp.repeat(xs.reshape(B, L, G, P), rep, axis=2)
            Bh = jnp.repeat(Bs.reshape(B, L, G, N), rep, axis=2)
            Ch = Cs.reshape(B, L, H, N)
            c, Q = (L // CHUNK, CHUNK)
            a = (dt * A).reshape(B, c, Q, H).transpose(0, 1, 3, 2)
            dtc = dt.reshape(B, c, Q, H).transpose(0, 1, 3, 2)
            Xc = xh.reshape(B, c, Q, H, P).transpose(0, 1, 3, 2, 4)
            Bc = Bh.reshape(B, c, Q, H, N).transpose(0, 1, 3, 2, 4)
            Cc = Ch.reshape(B, c, Q, H, N).transpose(0, 1, 3, 2, 4)
            cs = jnp.cumsum(a, axis=-1)
            tri = jnp.tril(jnp.ones((Q, Q), bool))
            Ldec = jnp.where(tri, jnp.exp(cs[..., :, None] - cs[..., None, :]), 0.0)
            Xdt = Xc * dtc[..., None]
            att = jnp.einsum('bchqn,bchkn->bchqk', Cc, Bc) * Ldec
            Yd = jnp.einsum('bchqk,bchkp->bchqp', att, Xdt)
            dec_end = jnp.exp(cs[..., -1:] - cs)
            states = jnp.einsum('bchq,bchqn,bchqp->bchpn', dec_end, Bc, Xdt)
            g = jnp.exp(cs[..., -1])

            def step(S, inp):
                gk, st = inp
                return (gk[:, :, None, None] * S + st, S)
            S0 = jnp.zeros((B, H, P, N), x.dtype)
            _, prev = jax.lax.scan(step, S0, (g.transpose(1, 0, 2), states.transpose(1, 0, 2, 3, 4)))
            prev = prev.transpose(1, 0, 2, 3, 4)
            Yo = jnp.einsum('bchqn,bchpn,bchq->bchqp', Cc, prev, jnp.exp(cs))
            Y = (Yd + Yo).transpose(0, 1, 3, 2, 4).reshape(B, L, H, P)
            Y = Y + D[:, None] * xh
            y = Y.reshape(B, L, D_INNER) * silu(z)
            return y @ w_out.T
        res = hidden_states
        h = rmsnorm(hidden_states, ln1_w)
        h = res + mamba2(h, w_in, conv_w, conv_b, A_log, D, dt_bias, w_out)
        res = h
        h2 = rmsnorm(h, ln2_w)
        mlp = silu(h2 @ gate_w.T) * (h2 @ up_w.T) @ down_w.T
        return res + mlp

    def _L0_ffn_ref(x, lora_A, lora_B, W, bias, lora_weights):
        import jax, jax.numpy as jnp
        import numpy as np
        B_, S, D_IN, D_OUT = (4, 256, 512, 512)
        N, RANK, ALPHA = (8, 16, 32)
        SCALE = ALPHA / RANK
        h = jnp.einsum('bsd,nrd->nbsr', x, lora_A)
        coef = (SCALE * lora_weights)[:, None, None]
        lora_out = jnp.einsum('nbsr,nor->bso', h, lora_B * coef)
        base = jnp.einsum('bsd,od->bso', x, W) + bias
        return base + lora_out
    x = L0_attn_hidden_states
    x = x + _layernorm(_L0_attn_ref(_layernorm(x, axis=-1), L0_attn_w_in, L0_attn_conv_w, L0_attn_conv_b, L0_attn_A_log, L0_attn_D, L0_attn_dt_bias, L0_attn_w_out, L0_attn_ln1_w, L0_attn_ln2_w, L0_attn_gate_w, L0_attn_up_w, L0_attn_down_w), axis=-1)
    x = x + _layernorm(_L0_ffn_ref(_layernorm(x, axis=-1), L0_ffn_lora_A, L0_ffn_lora_B, L0_ffn_W, L0_ffn_bias, L0_ffn_lora_weights), axis=-1)
    return x

_drawn_inputs = setup_inputs


def setup_inputs(seed=0):
    import zlib

    import numpy as np

    out = dict(_drawn_inputs(seed))
    spreads = {'L0_attn_conv_b': (0.0, 0.8),
     'L0_attn_D': (1.0, 0.6),
     'L0_attn_ln1_w': (1.0, 0.6),
     'L0_attn_ln2_w': (1.0, 0.6),
     'L0_ffn_lora_weights': (0.125, 0.2)}
    factors = {'L0_attn_w_in': 8.0,
     'L0_attn_conv_w': 8.0,
     'L0_attn_A_log': 8.0,
     'L0_attn_dt_bias': 8.0,
     'L0_attn_w_out': 8.0,
     'L0_ffn_bias': 8.0,
     'L0_attn_gate_w': 64.0,
     'L0_attn_up_w': 64.0,
     'L0_attn_down_w': 64.0}
    for name, (base, spread) in spreads.items():
        noise = np.random.default_rng([zlib.crc32(name.encode()), seed]).standard_normal(out[name].shape)
        drawn = base * np.exp(spread * noise) if base else spread * noise
        out[name] = jnp.asarray(drawn.astype(out[name].dtype))
    for name, factor in factors.items():
        out[name] = (out[name] * factor).astype(out[name].dtype)
    return out
```

```python
from contextlib import ExitStack

import concourse.bass as bass
from concourse import mybir

F32 = mybir.dt.float32
F32R = mybir.dt.float32r
ALU = mybir.AluOpType
ACT = mybir.ActivationFunctionType

P = 128
EPS = 1e-5
BATCH, SEQ, D_MODEL = 2, 1024, 512
HEADS, STATE, TAPS = 4, 128, 4
D_INNER = 512
D_PROJ = 2 * D_INNER + 2 * P + HEADS
INTER = 1792
RANKS = 128
LORA_SCALE = 2.0

KD = D_MODEL // P
TILES = 4
BT = TILES * P
BLOCKS = BATCH * SEQ // BT
CPB = TILES // BATCH
CW = CPB * P
FT = INTER // P
ORDER = [b * CPB + c for c in range(CPB) for b in range(BATCH)]

CONV = 2 + HEADS
IN_GROUPS = [("dt", 2 * D_INNER + 2 * P, 0)] + \
    [("conv", D_INNER + P, 1), ("conv", D_INNER, 0)] + \
    [("conv", D_INNER + 2 * P + P * h, 2 + h) for h in range(HEADS)] + \
    [("z", P * h, h) for h in range(HEADS)]
NG = len(IN_GROUPS)
IN_AT = [[0, 1], [2, 3], [4, 5], [6, 7], [8, 9], [10]]
EV_AT = [[0, 1], [2, 3], [4, 5], [6], [7, 8, 9], [10]]
CONV_AT = [[], [1], [2, 3], [4, 5], [6], []]
STEPS = TILES + 2
SEED = 2


class Signal:

    def __init__(self, nc, ctx, name, per, seeded=True):
        self.sem = ctx.enter_context(nc.semaphore(name))
        self.per = per
        self.base = SEED if seeded else 0

    def at(self, block, n=None):
        return (block + self.base) * self.per + (self.per if n is None else n)

    def seed(self, engine):
        engine.sem_inc(self.sem, self.base * self.per)


def waits_apart(engine, passed):
    engine.sem_inc(passed, 1)


def sandwich_program(nc, x, w_in, w_out, conv_w, conv_b, a_log, d_skip, dt_bias, ln1, ln2, gate, up, down,
                     lora_a, lora_b, w_ffn, ffn_bias, lora_coef, h_scratch, out):
    state_space_phase(nc, x, w_in, w_out, conv_w, conv_b, a_log, d_skip, dt_bias, ln1, h_scratch)
    mlp_phase(nc, x, ln2, gate, up, down, lora_a, lora_b, w_ffn, ffn_bias, lora_coef, h_scratch, out)


def split_passes(hi_l, lo_l, hi_r, lo_r):
    return [(hi_l, hi_r), (hi_l, lo_r), (lo_l, hi_r)]


def state_space_phase(nc, x, w_in, w_out, conv_w, conv_b, a_log, d_skip, dt_bias, ln1, h_scratch):
    with ExitStack() as ctx:
        def sb(name, shape, dt=F32):
            return ctx.enter_context(nc.sbuf_tensor(name, shape, dt))

        def psum(name):
            return ctx.enter_context(nc.psum_tensor(name, [P, 512], F32))

        def sig(name, per, seeded=True):
            return Signal(nc, ctx, name, per, seeded)

        NW = D_PROJ - HEADS
        wi_hi, wi_lo = sb("wi_hi", [P, KD, NW], F32R), sb("wi_lo", [P, KD, NW], F32R)
        wdt = sb("wdt", [P, KD, 2 * HEADS], F32R)
        wo_hi, wo_lo = sb("wo_hi", [P, HEADS, D_MODEL], F32R), sb("wo_lo", [P, HEADS, D_MODEL], F32R)
        xin = sb("xin", [P, TILES, D_MODEL])
        zt_hi, zt_lo = sb("zt_hi", [P, KD, BT], F32R), sb("zt_lo", [P, KD, BT], F32R)
        raw = sb("raw", [P, CONV, BATCH, TAPS - 1 + CW])
        cacc = sb("cacc", [P, CONV * BT])
        CX = CONV * BT
        cx = sb("cx", [P, 2 * CX])
        ZS = HEADS * BT
        zs = sb("zs", [P, 2 * ZS])
        xr = sb("xr", [P, TILES, D_MODEL])
        xb32 = sb("xb32", [P, 2, P])
        b_hi, b_lo = sb("b_hi", [P, P], F32R), sb("b_lo", [P, P], F32R)
        xb_hi, xb_lo = sb("xb_hi", [P, 2, 2, P], F32R), sb("xb_lo", [P, 2, 2, P], F32R)
        c_hi, c_lo = sb("c_hi", [P, HEADS, P], F32R), sb("c_lo", [P, HEADS, P], F32R)
        r_hi, r_lo = sb("r_hi", [P, HEADS, P], F32R), sb("r_lo", [P, HEADS, P], F32R)
        dec = sb("dec", [P, HEADS, P])
        ecs = sb("ecs", [P, HEADS, P])
        mdt = sb("mdt", [P, HEADS, P])
        att32 = sb("att32", [P, HEADS, P])
        att_hi, att_lo = sb("att_hi", [P, HEADS, P], F32R), sb("att_lo", [P, HEADS, P], F32R)
        cp32 = sb("cp32", [P, HEADS, P])
        cp_hi, cp_lo = sb("cp_hi", [P, HEADS, P], F32R), sb("cp_lo", [P, HEADS, P], F32R)
        xs32 = sb("xs32", [P, HEADS, P])
        xs_hi, xs_lo = sb("xs_hi", [P, HEADS, P], F32R), sb("xs_lo", [P, HEADS, P], F32R)
        state = sb("state", [P, BATCH, HEADS, P])
        s_hi, s_lo = sb("s_hi", [P, HEADS, P], F32R), sb("s_lo", [P, HEADS, P], F32R)
        y32 = sb("y32", [P, HEADS, P])
        y_hi, y_lo = sb("y_hi", [P, HEADS, P], F32R), sb("y_lo", [P, HEADS, P], F32R)
        ident, upper = sb("ident", [P, P]), sb("upper", [P, P])
        after_f, ones_f = xb32[:, 0, :], xb32[:, 1, :]
        after, ones = sb("after", [P, P], F32R), sb("ones", [P, P], F32R)
        ln1_sb, cw_sb, cb_sb = sb("ln1_sb", [P, KD]), sb("cw_sb", [P, CONV, TAPS]), sb("cb_sb", [P, CONV])
        head_sb = sb("head_sb", [P, 3, HEADS])
        neg_a = sb("neg_a", [P, HEADS])
        mhalf = sb("mhalf", [P, TILES])
        bn = sb("bn", [P, TILES, 6])
        mv = sb("mv", [P, TILES, 2])
        lt = sb("lt", [P, 6, TILES])
        lz = sb("lz", [P, 2, TILES])
        lnk = sb("lnk", [P, BLOCKS * 2 * TILES])
        DH = TILES * HEADS
        dtraw = sb("dtraw", [P, TILES, 2 * HEADS])
        dtt = sb("dtt", [P, 8, DH])
        dtv, a_hi, a_lo = sb("dtv", [P, DH]), sb("a_hi", [P, DH], F32R), sb("a_lo", [P, DH])
        wd = sb("wd", [P, HEADS])

        p_in = [psum("p_in0"), psum("p_in1")]
        p_tr, p_d, p_s, p_y, p_st, p_o = (psum(n) for n in ("p_tr", "p_d", "p_s", "p_y", "p_st", "p_o"))

        par_in, win_in, wout_in = (sig(n, 1, False) for n in ("par_in", "win_in", "wout_in"))
        x_in, xr_in = sig("x_in", 32, False), sig("xr_in", 32, False)
        h_out = sig("h_out", 16 * TILES, False)
        consts = sig("consts", 1, False)
        mask_made = sig("mask_made", 1, False)
        zeroed, win_scaled, w_hi_made, w_lo_made, neg_a_made = (
            sig(n, 1, False) for n in ("zeroed", "win_scaled", "w_hi_made", "w_lo_made", "neg_a_made"))
        dve = {n: sig(n, per) for n, per in dict(
            bn_made=TILES, mean_var=TILES, normed=TILES, zt_lo_made=TILES, tap=4 * CONV, hist=1,
            dt_abs=1, dt_step=14, dt_tail=4, dt_ready=1, xb_copied=4, xb_lo_made=4, wd_made=4, xs_made=4,
            t1=4, t2=4, att_made=4, s_lo_made=4, s_updated=4, y_gated=4, y_lo_made=4, xhat=4, h_made=4).items()}
        act = {n: sig(n, per) for n, per in dict(
            zt_hi_made=TILES, in_out=NG, silu_made=1, dt_exp=1, dec_made=4, ecs_made=4, c_hi_made=4, b_hi_made=4,
            xb_hi_made=4, att_hi_made=4, cp_hi_made=4, xs_hi_made=4, s_hi_made=4, y_hi_made=4).items()}
        pool = {n: sig(n, per) for n, per in dict(
            ln_step=11, ln_scale=1, r_made=4, mdt_made=4, c_lo_made=4, b_lo_made=4, att_lo_made=4, cp_made=4,
            cp_lo_made=4, xs_lo_made=4, s_decayed=4).items()}
        pe = {n: sig(n, per) for n, per in dict(
            zt_ps=TILES, in_ps=NG, d_ps=4, cs_ps=4, tr_ps=4, sc_ps=4, y_ps=4, st_ps=4, o_ps=4).items()}
        s = {**dve, **act, **pool, **pe}

        passed_pool, passed_vector = (ctx.enter_context(nc.semaphore(n)) for n in ("passed_pool", "passed_vector"))

        block = ctx.enter_context(nc.Block())

        def cxs(i, first, count):
            return cx[:, bass.ds((i % 2) * CX + first, count)]

        def c_of(i, u):
            return cxs(i, 2 * BT, HEADS * BT).rearrange("p (h t) -> p h t", h=HEADS)[:, :, u * P:(u + 1) * P]

        def z_of(i, u):
            v = zs[:, bass.ds((i % 2) * ZS, ZS)]
            return v.rearrange("p (h t) -> p h t", h=HEADS)[:, :, u * P:(u + 1) * P]

        def per_head(v):
            return v.rearrange("p (h o) -> p h o", o=1).broadcast_to([P, HEADS, P])

        def over_heads(v):
            return v.rearrange("p (o q) -> p o q", o=1).broadcast_to([P, HEADS, P])

        def flat(v):
            return v.rearrange("p h q -> p (h q)")

        x_blocks = x.rearrange("(b i c p) d -> b i p c d", b=BATCH, i=BLOCKS, c=CPB)

        @block.sync
        def _(sp):
            for t, src in ((ln1_sb, ln1), (cw_sb, conv_w), (cb_sb, conv_b), (head_sb, None)):
                if src is not None:
                    sp.dma_start(t[:], src).then_inc(par_in.sem, 16)
            for n, src in enumerate((a_log, d_skip, dt_bias)):
                sp.dma_start(head_sb[:, n, :], src).then_inc(par_in.sem, 16)

            def load(i, dst, signal):
                for b in range(BATCH):
                    src = x_blocks[b, bass.ds(i, 1)].rearrange("o p c d -> (o p) c d")
                    sp.dma_start(dst[:, b * CPB:(b + 1) * CPB, :], src).then_inc(signal.sem, 16)

            load(0, xin, x_in)
            for k in range(KD):
                sp.dma_start(cx[:, k * D_PROJ:(k + 1) * D_PROJ], w_in[k * P:(k + 1) * P, :]).then_inc(win_in.sem, 16)
            sp.dma_start(zs[:, 0:HEADS * D_MODEL].rearrange("p (h n) -> p h n", h=HEADS),
                         w_out.rearrange("(h p) n -> p h n", p=P)).then_inc(wout_in.sem, 16)
            load(0, xr, xr_in)

            def body(i, more):
                if more:
                    sp.wait_ge(s["zt_ps"].sem, s["zt_ps"].at(i))
                    load(i + 1, xin, x_in)
                for q in range(TILES):
                    u = ORDER[q]
                    sp.wait_ge(s["h_made"].sem, s["h_made"].at(i, q + 1))
                    sp.dma_start(h_scratch[bass.ds(i * TILES + u, 1)].rearrange("o p d -> (o p) d"),
                                 xr[:, u, :]).then_inc(h_out.sem, 16)
                sp.wait_ge(h_out.sem, h_out.at(i))
                if more:
                    load(i + 1, xr, xr_in)

            with nc.sync.Fori(0, BLOCKS - 1) as i:
                body(i, True)
            body(BLOCKS - 1, False)

        @block.tensor
        def _(t):
            for v in pe.values():
                v.seed(t)

            def turn(j, first):
                if first is not None:
                    t.wait_ge(s["xs_made"].sem, s["xs_made"].at(j - 1, first))
                for u in range(TILES):
                    t.wait_ge(s["normed"].sem, s["normed"].at(j, u + 1))
                    if u:
                        t.wait_ge(s["zt_lo_made"].sem, s["zt_lo_made"].at(j, u))
                    for k in range(KD):
                        ins = nc.tensor.transpose(p_tr[:, k * P:(k + 1) * P], xin[:, u, k * P:(k + 1) * P], ident[:, :])
                    ins.then_inc(s["zt_ps"].sem, 1)

            def project(j, groups):
                for g in groups:
                    kind, col, _ = IN_GROUPS[g]
                    if g == 0:
                        t.wait_ge(s["zt_lo_made"].sem, s["zt_lo_made"].at(j))
                    t.wait_ge(s["in_out"].sem, s["in_out"].at(j, max(g - 1, 0)))
                    bank = p_in[g % 2]
                    if kind == "dt":
                        for u in range(TILES):
                            n = 0
                            for w in (zt_hi, zt_lo):
                                for k in range(KD):
                                    ins = nc.tensor.matmul(bank[:, u * 2 * HEADS:(u + 1) * 2 * HEADS],
                                                           w[:, k, u * P:(u + 1) * P], wdt[:, k, :],
                                                           start=(n == 0), stop=(n == 2 * KD - 1))
                                    n += 1
                    else:
                        n = 0
                        for k in range(KD):
                            for l, r in split_passes(wi_hi, wi_lo, zt_hi, zt_lo):
                                ins = nc.tensor.matmul(bank[:, :], l[:, k, col:col + P], r[:, k, :],
                                                       start=(n == 0), stop=(n == 3 * KD - 1))
                                n += 1
                    ins.then_inc(s["in_ps"].sem, 1)

            def front(i, q, more):
                t.wait_ge(s["r_made"].sem, s["r_made"].at(i, q + 1))
                t.wait_ge(s["ecs_made"].sem, s["ecs_made"].at(i, q))
                nc.tensor.matmul(p_d[:, :], after[:, :], flat(r_hi[:, :, :]), start=True, stop=False)
                nc.tensor.matmul(p_d[:, :], after[:, :], flat(r_lo[:, :, :]), start=False, stop=True).then_inc(s["d_ps"].sem, 1)
                t.wait_ge(s["xb_copied"].sem, s["xb_copied"].at(i, q + 1))
                t.wait_ge(s["xs_made"].sem, s["xs_made"].at(i, q))
                for n in range(2):
                    ins = nc.tensor.transpose(p_tr[:, n * P:(n + 1) * P], xb32[:, n, :], ident[:, :])
                ins.then_inc(s["tr_ps"].sem, 1)
                t.wait_ge(s["c_hi_made"].sem, s["c_hi_made"].at(i, q + 1))
                t.wait_ge(s["c_lo_made"].sem, s["c_lo_made"].at(i, q + 1))
                t.wait_ge(s["b_hi_made"].sem, s["b_hi_made"].at(i, q + 1))
                t.wait_ge(s["b_lo_made"].sem, s["b_lo_made"].at(i, q + 1))
                t.wait_ge(s["t2"].sem, s["t2"].at(i, q))
                for n, (l, r) in enumerate(split_passes(b_hi, b_lo, c_hi, c_lo)):
                    ins = nc.tensor.matmul(p_s[:, :], l[:, :], flat(r[:, :, :]), start=(n == 0), stop=(n == 2))
                ins.then_inc(s["sc_ps"].sem, 1)
                t.wait_ge(s["dec_made"].sem, s["dec_made"].at(i, q + 1))
                nc.tensor.matmul(p_d[:, :], ones[:, :], flat(r_hi[:, :, :]), start=True, stop=False)
                nc.tensor.matmul(p_d[:, :], ones[:, :], flat(r_lo[:, :, :]), start=False, stop=True).then_inc(s["cs_ps"].sem, 1)

            def back(i, q):
                t.wait_ge(s["xs_hi_made"].sem, s["xs_hi_made"].at(i, q + 1))
                t.wait_ge(s["xs_lo_made"].sem, s["xs_lo_made"].at(i, q + 1))
                t.wait_ge(s["s_updated"].sem, s["s_updated"].at(i, q))
                for n, (l, r) in enumerate(split_passes(xb_hi, xb_lo, xs_hi, xs_lo)):
                    ins = nc.tensor.matmul(p_st[:, :], l[:, q % 2, 1, :], flat(r[:, :, :]), start=(n == 0), stop=(n == 2))
                ins.then_inc(s["st_ps"].sem, 1)
                t.wait_ge(s["att_hi_made"].sem, s["att_hi_made"].at(i, q + 1))
                t.wait_ge(s["att_lo_made"].sem, s["att_lo_made"].at(i, q + 1))
                t.wait_ge(s["y_gated"].sem, s["y_gated"].at(i, q))
                for n, (l, r) in enumerate(split_passes(xb_hi, xb_lo, att_hi, att_lo)):
                    nc.tensor.matmul(p_y[:, :], l[:, q % 2, 0, :], flat(r[:, :, :]), start=(n == 0), stop=False,
                                     skip_group_check=True)
                t.wait_ge(s["cp_hi_made"].sem, s["cp_hi_made"].at(i, q + 1))
                t.wait_ge(s["cp_lo_made"].sem, s["cp_lo_made"].at(i, q + 1))
                t.wait_ge(s["s_hi_made"].sem, s["s_hi_made"].at(i, q + 1))
                t.wait_ge(s["s_lo_made"].sem, s["s_lo_made"].at(i, q + 1))
                for h in range(HEADS):
                    for n, (l, r) in enumerate(split_passes(s_hi, s_lo, cp_hi, cp_lo)):
                        ins = nc.tensor.matmul(p_y[:, h * P:(h + 1) * P], l[:, h, :], r[:, h, :], start=False,
                                               stop=(h == HEADS - 1 and n == 2), skip_group_check=True)
                ins.then_inc(s["y_ps"].sem, 1)

            def output(i, q):
                t.wait_ge(s["y_hi_made"].sem, s["y_hi_made"].at(i, q + 1))
                t.wait_ge(s["y_lo_made"].sem, s["y_lo_made"].at(i, q + 1))
                t.wait_ge(s["h_made"].sem, s["h_made"].at(i, q))
                n = 0
                for h in range(HEADS):
                    for l, r in split_passes(y_hi, y_lo, wo_hi, wo_lo):
                        ins = nc.tensor.matmul(p_o[:, :], l[:, h, :], r[:, h, :], start=(n == 0), stop=(n == 3 * HEADS - 1))
                        n += 1
                ins.then_inc(s["o_ps"].sem, 1)

            def body(i, more):
                for step in range(STEPS):
                    if step < TILES:
                        front(i, step, more)
                    if step == 0 and more:
                        turn(i + 1, 1)
                    if more:
                        project(i + 1, IN_AT[step])
                    if 1 <= step <= TILES:
                        back(i, step - 1)
                    if step >= 2:
                        output(i, step - 2)

            t.wait_ge(consts.sem, consts.at(0, 5))
            turn(0, None)
            t.wait_ge(w_hi_made.sem, w_hi_made.at(0, 3))
            t.wait_ge(w_lo_made.sem, w_lo_made.at(0, 3))
            project(0, range(NG))
            with nc.tensor.Fori(0, BLOCKS - 1) as i:
                body(i, True)
            body(BLOCKS - 1, False)

        @block.scalar
        def _(a):
            for v in act.values():
                v.seed(a)

            def turn(j):
                for u in range(TILES):
                    a.wait_ge(s["zt_ps"].sem, s["zt_ps"].at(j, u + 1))
                    if u == 0:
                        a.wait_ge(s["in_ps"].sem, s["in_ps"].at(j - 1))
                    nc.scalar.copy(zt_hi[:, :, u * P:(u + 1) * P],
                                   p_tr[:, :].rearrange("p (k t) -> p k t", k=KD)).then_inc(s["zt_hi_made"].sem, 1)

            def evacuate(j, groups):
                for g in groups:
                    kind, _, n = IN_GROUPS[g]
                    a.wait_ge(s["in_ps"].sem, s["in_ps"].at(j, g + 1))
                    if kind == "dt":
                        a.wait_ge(s["dt_step"].sem, s["dt_step"].at(j - 1))
                        ins = nc.scalar.copy(dtraw[:, :, :].rearrange("p u e -> p (u e)"), p_in[g % 2][:, 0:TILES * 2 * HEADS])
                    elif kind == "conv":
                        a.wait_ge(s["hist"].sem, s["hist"].at(j - 1))
                        ins = nc.scalar.copy(raw[:, n, :, TAPS - 1:], p_in[g % 2][:, :].rearrange("p (b t) -> p b t", b=BATCH))
                    else:
                        ins = nc.scalar.activation(zs[:, bass.ds((j % 2) * ZS + n * BT, BT)], p_in[g % 2][:, :], ACT.Silu)
                    ins.then_inc(s["in_out"].sem, 1)

            def dt_exp(j):
                a.wait_ge(s["dt_abs"].sem, s["dt_abs"].at(j))
                nc.scalar.activation(dtt[:, 2, :], dtt[:, 1, :], ACT.Exp, scale=-1.0).then_inc(s["dt_exp"].sem, 1)

            def silu(j):
                a.wait_ge(s["tap"].sem, s["tap"].at(j))
                nc.scalar.activation(cxs(j, 0, CX), cacc[:, :], ACT.Silu).then_inc(s["silu_made"].sem, 1)

            def front(i, q):
                u = ORDER[q]
                a.wait_ge(s["sc_ps"].sem, s["sc_ps"].at(i, q))
                a.wait_ge(s["xb_copied"].sem, s["xb_copied"].at(i, q + 1))
                nc.scalar.copy(b_hi[:, :], xb32[:, 1, :]).then_inc(s["b_hi_made"].sem, 1)
                nc.scalar.copy(c_hi[:, :, :], c_of(i, u)).then_inc(s["c_hi_made"].sem, 1)
                a.wait_ge(s["d_ps"].sem, s["d_ps"].at(i, q + 1))
                a.wait_ge(s["t1"].sem, s["t1"].at(i, q))
                nc.scalar.activation(flat(dec[:, :, :]), p_d[:, :], ACT.Exp).then_inc(s["dec_made"].sem, 1)
                a.wait_ge(s["tr_ps"].sem, s["tr_ps"].at(i, q + 1))
                a.wait_ge(s["y_ps"].sem, s["y_ps"].at(i, q - 1))
                nc.scalar.copy(xb_hi[:, q % 2, :, :].rearrange("p n t -> p (n t)"), p_tr[:, 0:2 * P]).then_inc(s["xb_hi_made"].sem, 1)
                a.wait_ge(s["cs_ps"].sem, s["cs_ps"].at(i, q + 1))
                a.wait_ge(s["s_decayed"].sem, s["s_decayed"].at(i, q))
                nc.scalar.activation(flat(ecs[:, :, :]), p_d[:, :], ACT.Exp).then_inc(s["ecs_made"].sem, 1)
                a.wait_ge(s["xs_made"].sem, s["xs_made"].at(i, q + 1))
                a.wait_ge(s["st_ps"].sem, s["st_ps"].at(i, q))
                nc.scalar.copy(flat(xs_hi[:, :, :]), flat(xs32[:, :, :])).then_inc(s["xs_hi_made"].sem, 1)
                a.wait_ge(s["y_ps"].sem, s["y_ps"].at(i, q))
                a.wait_ge(s["s_updated"].sem, s["s_updated"].at(i, q - 1))
                nc.scalar.copy(flat(s_hi[:, :, :]), flat(state[:, u // CPB, :, :])).then_inc(s["s_hi_made"].sem, 1)
                a.wait_ge(s["att_made"].sem, s["att_made"].at(i, q + 1))
                nc.scalar.copy(flat(att_hi[:, :, :]), flat(att32[:, :, :])).then_inc(s["att_hi_made"].sem, 1)
                a.wait_ge(s["cp_made"].sem, s["cp_made"].at(i, q + 1))
                nc.scalar.copy(flat(cp_hi[:, :, :]), flat(cp32[:, :, :])).then_inc(s["cp_hi_made"].sem, 1)

            def back(i, q):
                a.wait_ge(s["y_gated"].sem, s["y_gated"].at(i, q + 1))
                a.wait_ge(s["o_ps"].sem, s["o_ps"].at(i, q))
                nc.scalar.copy(flat(y_hi[:, :, :]), flat(y32[:, :, :])).then_inc(s["y_hi_made"].sem, 1)

            def body(i, more):
                for step in range(STEPS):
                    if step < TILES:
                        front(i, step)
                    if step == 0 and more:
                        turn(i + 1)
                    if more:
                        if step == 4:
                            dt_exp(i + 1)
                        evacuate(i + 1, EV_AT[step])
                    if 1 <= step <= TILES:
                        back(i, step - 1)
                if more:
                    silu(i + 1)

            a.wait_ge(par_in.sem, par_in.at(0, 6 * 16))
            nc.scalar.activation(neg_a[:, :], head_sb[:, 0, :], ACT.Exp).then_inc(neg_a_made.sem, 1)
            a.wait_ge(win_scaled.sem, win_scaled.at(0, KD))
            wv = cx[:, 0:KD * D_PROJ].rearrange("p (k n) -> p k n", k=KD)
            nc.scalar.copy(wi_hi[:, :, :], wv[:, :, 0:NW]).then_inc(w_hi_made.sem, 1)
            nc.scalar.copy(wdt[:, :, 0:HEADS], wv[:, :, NW:D_PROJ]).then_inc(w_hi_made.sem, 1)
            a.wait_ge(wout_in.sem, wout_in.at(0, 16))
            nc.scalar.copy(flat(wo_hi[:, :, :]), zs[:, 0:HEADS * D_MODEL]).then_inc(w_hi_made.sem, 1)
            turn(0)
            a.wait_ge(w_lo_made.sem, w_lo_made.at(0, 3))
            evacuate(0, [0])
            dt_exp(0)
            evacuate(0, range(1, NG))
            silu(0)
            with nc.scalar.Fori(0, BLOCKS - 1) as i:
                body(i, True)
            body(BLOCKS - 1, False)

        @block.gpsimd
        def _(g):
            for v in pool.values():
                v.seed(g)
            nc.gpsimd.memset(ident[:, :], 0.0).then_inc(mask_made.sem, 1)
            nc.gpsimd.memset(upper[:, :], 1.0).then_inc(mask_made.sem, 1)
            nc.gpsimd.memset(after_f, 1.0).then_inc(mask_made.sem, 1)
            nc.gpsimd.memset(ones_f, 1.0).then_inc(mask_made.sem, 1)
            nc.gpsimd.memset(mhalf[:, :], -0.5).then_inc(consts.sem, 1)
            g.wait_ge(mask_made.sem, mask_made.at(0, 4))
            nc.gpsimd.affine_select(out=ident[:, :], in_=ident[:, :], compare_op=ALU.not_equal, fill=1.0, base=0,
                                    pattern=[[-1, P]], channel_multiplier=1).then_inc(consts.sem, 1)
            nc.gpsimd.affine_select(out=upper[:, :], in_=upper[:, :], compare_op=ALU.is_ge, fill=0.0, base=0,
                                    pattern=[[1, P]], channel_multiplier=-1).then_inc(consts.sem, 1)
            nc.gpsimd.affine_select(out=after_f, in_=after_f, compare_op=ALU.is_gt, fill=0.0, base=0,
                                    pattern=[[-1, P]], channel_multiplier=1).then_inc(mask_made.sem, 1)
            g.wait_ge(mask_made.sem, mask_made.at(0, 5))
            nc.gpsimd.tensor_copy(after[:, :], after_f).then_inc(consts.sem, 1)
            nc.gpsimd.tensor_copy(ones[:, :], ones_f).then_inc(consts.sem, 1)

            def norm_scales(j):
                g.wait_ge(s["mean_var"].sem, s["mean_var"].at(j))
                g.wait_ge(s["normed"].sem, s["normed"].at(j - 1))
                waits_apart(g, passed_pool)
                mean, var = mv[:, :, 0], mv[:, :, 1]
                ve, rstd, t1, t2, t3, r1 = (lt[:, n, :] for n in range(6))
                keep = lnk[:, bass.ds(j * 2 * TILES, 2 * TILES)]
                step = [0]

                def chain(ins):
                    step[0] += 1
                    ins.then_inc(s["ln_step"].sem, 1)
                    g.wait_ge(s["ln_step"].sem, s["ln_step"].at(j, step[0]))
                    waits_apart(g, passed_pool)

                chain(nc.gpsimd.tensor_scalar(ve, var, EPS, 1.0, ALU.add, ALU.mult))
                chain(nc.gpsimd.tensor_tensor(rstd, ve, mhalf[:, :], ALU.pow))
                chain(nc.gpsimd.tensor_tensor(t1, var, rstd, ALU.mult))
                chain(nc.gpsimd.tensor_tensor(t2, t1, rstd, ALU.mult))
                chain(nc.gpsimd.tensor_scalar(t3, t2, EPS, 1.0, ALU.add, ALU.mult))
                chain(nc.gpsimd.tensor_tensor(r1, t3, mhalf[:, :], ALU.pow))
                chain(nc.gpsimd.tensor_tensor(t1, mean, rstd, ALU.mult))
                chain(nc.gpsimd.tensor_scalar(t2, t1, -1.0, 1.0, ALU.mult, ALU.mult))
                chain(nc.gpsimd.tensor_tensor(lz[:, 0, :], rstd, r1, ALU.mult))
                chain(nc.gpsimd.tensor_tensor(lz[:, 1, :], t2, r1, ALU.mult))
                chain(nc.gpsimd.tensor_copy(keep[:, 0:TILES], rstd))
                nc.gpsimd.tensor_copy(keep[:, TILES:2 * TILES], t2).then_inc(s["ln_scale"].sem, 1)

            def front(i, q):
                u = ORDER[q]
                hs = slice(u * HEADS, (u + 1) * HEADS)
                if q == 0:
                    g.wait_ge(s["dt_ready"].sem, s["dt_ready"].at(i))
                    g.wait_ge(s["silu_made"].sem, s["silu_made"].at(i))
                g.wait_ge(s["cs_ps"].sem, s["cs_ps"].at(i, q))
                nc.gpsimd.tensor_tensor(r_hi[:, :, :], over_heads(upper[:, :]), per_head(a_hi[:, hs].bitcast(F32)), ALU.mult)
                nc.gpsimd.tensor_tensor(r_lo[:, :, :], over_heads(upper[:, :]), per_head(a_lo[:, hs]), ALU.mult)\
                    .then_inc(s["r_made"].sem, 1)
                g.wait_ge(s["t1"].sem, s["t1"].at(i, q))
                nc.gpsimd.tensor_tensor(mdt[:, :, :], over_heads(upper[:, :]), per_head(dtv[:, hs]), ALU.mult)\
                    .then_inc(s["mdt_made"].sem, 1)
                g.wait_ge(s["sc_ps"].sem, s["sc_ps"].at(i, q))
                g.wait_ge(s["b_hi_made"].sem, s["b_hi_made"].at(i, q + 1))
                nc.gpsimd.tensor_tensor(b_lo[:, :], xb32[:, 1, :], b_hi[:, :].bitcast(F32), ALU.subtract)\
                    .then_inc(s["b_lo_made"].sem, 1)
                g.wait_ge(s["c_hi_made"].sem, s["c_hi_made"].at(i, q + 1))
                waits_apart(g, passed_pool)
                nc.gpsimd.tensor_tensor(c_lo[:, :, :], c_of(i, u), c_hi[:, :, :].bitcast(F32), ALU.subtract)\
                    .then_inc(s["c_lo_made"].sem, 1)
                g.wait_ge(s["ecs_made"].sem, s["ecs_made"].at(i, q + 1))
                g.wait_ge(s["cp_hi_made"].sem, s["cp_hi_made"].at(i, q))
                waits_apart(g, passed_pool)
                nc.gpsimd.tensor_tensor(cp32[:, :, :], c_of(i, u), ecs[:, :, :], ALU.mult).then_inc(s["cp_made"].sem, 1)
                g.wait_ge(s["st_ps"].sem, s["st_ps"].at(i, q))
                g.wait_ge(s["xs_hi_made"].sem, s["xs_hi_made"].at(i, q + 1))
                nc.gpsimd.tensor_tensor(flat(xs_lo[:, :, :]), flat(xs32[:, :, :]), flat(xs_hi[:, :, :].bitcast(F32)),
                                        ALU.subtract).then_inc(s["xs_lo_made"].sem, 1)
                g.wait_ge(s["y_ps"].sem, s["y_ps"].at(i, q))
                g.wait_ge(s["att_hi_made"].sem, s["att_hi_made"].at(i, q + 1))
                nc.gpsimd.tensor_tensor(flat(att_lo[:, :, :]), flat(att32[:, :, :]), flat(att_hi[:, :, :].bitcast(F32)),
                                        ALU.subtract).then_inc(s["att_lo_made"].sem, 1)
                g.wait_ge(s["cp_hi_made"].sem, s["cp_hi_made"].at(i, q + 1))
                nc.gpsimd.tensor_tensor(flat(cp_lo[:, :, :]), flat(cp32[:, :, :]), flat(cp_hi[:, :, :].bitcast(F32)),
                                        ALU.subtract).then_inc(s["cp_lo_made"].sem, 1)
                g.wait_ge(s["s_hi_made"].sem, s["s_hi_made"].at(i, q + 1))
                g.wait_ge(s["s_lo_made"].sem, s["s_lo_made"].at(i, q + 1))
                decay = ecs[:, :, P - 1:P].broadcast_to([P, HEADS, P])
                nc.gpsimd.tensor_tensor(state[:, u // CPB, :, :], state[:, u // CPB, :, :], decay, ALU.mult)\
                    .then_inc(s["s_decayed"].sem, 1)

            def body(i, more):
                for step in range(STEPS):
                    if step < TILES:
                        front(i, step)
                    if step == 0 and more:
                        norm_scales(i + 1)

            g.wait_ge(consts.sem, consts.at(0, 5))
            norm_scales(0)
            with nc.gpsimd.Fori(0, BLOCKS - 1) as i:
                body(i, True)
            body(BLOCKS - 1, False)

        @block.vector
        def _(v):
            for e in dve.values():
                e.seed(v)

            def norm(j):
                v.wait_ge(x_in.sem, x_in.at(j))
                v.wait_ge(s["ln_scale"].sem, s["ln_scale"].at(j - 1))
                for u in range(TILES):
                    nc.vector.bn_stats(bn[:, u, :], xin[:, u, :]).then_inc(s["bn_made"].sem, 1)
                for u in range(TILES):
                    v.wait_ge(s["bn_made"].sem, s["bn_made"].at(j, u + 1))
                    waits_apart(v, passed_vector)
                    nc.vector.bn_aggr(mv[:, u, :], bn[:, u, :]).then_inc(s["mean_var"].sem, 1)
                v.wait_ge(s["ln_scale"].sem, s["ln_scale"].at(j))
                for u in range(TILES):
                    nc.vector.tensor_scalar(xin[:, u, :], xin[:, u, :], lz[:, 0, u:u + 1], lz[:, 1, u:u + 1],
                                            ALU.mult, ALU.add).then_inc(s["normed"].sem, 1)

            def turn(j):
                for u in range(TILES):
                    v.wait_ge(s["zt_hi_made"].sem, s["zt_hi_made"].at(j, u + 1))
                    if u == 0:
                        v.wait_ge(s["in_ps"].sem, s["in_ps"].at(j - 1))
                    cols = slice(u * P, (u + 1) * P)
                    nc.vector.tensor_tensor(zt_lo[:, :, cols], p_tr[:, :].rearrange("p (k t) -> p k t", k=KD),
                                            zt_hi[:, :, cols].bitcast(F32), ALU.subtract).then_inc(s["zt_lo_made"].sem, 1)

            def convolve(j, groups):
                for g in groups:
                    n = IN_GROUPS[g][2]
                    acc = cacc[:, n * BT:(n + 1) * BT].rearrange("p (b t) -> p b t", b=BATCH)
                    v.wait_ge(s["in_out"].sem, s["in_out"].at(j, g + 1))
                    if g == 1:
                        v.wait_ge(s["silu_made"].sem, s["silu_made"].at(j - 1))
                    nc.vector.tensor_scalar(acc, raw[:, n, :, 0:CW], cw_sb[:, n, 0:1], cb_sb[:, n:n + 1],
                                            ALU.mult, ALU.add).then_inc(s["tap"].sem, 1)
                    for k in range(1, TAPS):
                        v.wait_ge(s["tap"].sem, s["tap"].at(j, (g - 1) * TAPS + k))
                        nc.vector.scalar_tensor_tensor(out=acc, in0=raw[:, n, :, k:k + CW], scalar=cw_sb[:, n, k:k + 1],
                                                       in1=acc, op0=ALU.mult, op1=ALU.add).then_inc(s["tap"].sem, 1)

            def keep_history(j):
                v.wait_ge(s["tap"].sem, s["tap"].at(j))
                nc.vector.tensor_copy(raw[:, :, :, 0:TAPS - 1].rearrange("p n b t -> p (n b) t"),
                                      raw[:, :, :, CW:].rearrange("p n b t -> p (n b) t")).then_inc(s["hist"].sem, 1)

            xd, ax, ed, t3, t4, t5, t6, t7 = (dtt[:, n, :] for n in range(8))
            dt_tail = s["dt_tail"]

            def chain(j, n, ins):
                ins.then_inc(s["dt_step"].sem, 1)
                v.wait_ge(s["dt_step"].sem, s["dt_step"].at(j, n))

            def dt_start(j):
                v.wait_ge(s["in_out"].sem, s["in_out"].at(j, 1))
                x3 = xd.rearrange("p (u h) -> p u h", u=TILES)
                bias = head_sb[:, 2:3, :].broadcast_to([P, TILES, HEADS])
                chain(j, 1, nc.vector.tensor_tensor(x3, dtraw[:, :, 0:HEADS], dtraw[:, :, HEADS:], ALU.add))
                chain(j, 2, nc.vector.tensor_tensor(x3, x3, bias, ALU.add))
                nc.vector.scalar_tensor_tensor(out=ax, in0=xd, scalar=-1.0, in1=xd, op0=ALU.mult, op1=ALU.max)\
                    .then_inc(s["dt_abs"].sem, 1)

            def dt_finish(j):
                v.wait_ge(s["dt_exp"].sem, s["dt_exp"].at(j))
                chain(j, 3, nc.vector.tensor_scalar(t3, ed, 2.0, None, ALU.add))
                chain(j, 4, nc.vector.reciprocal(t4, t3))
                chain(j, 5, nc.vector.tensor_tensor(t5, ed, t4, ALU.mult))
                chain(j, 6, nc.vector.tensor_tensor(t6, t5, t5, ALU.mult))
                terms = [1.0 / (2 * k + 1) for k in range(1, 8)]
                nc.vector.tensor_scalar(t7, t6, terms[-1], None, ALU.mult).then_inc(s["dt_step"].sem, 1)
                n = 7
                for c in reversed(terms[:-1]):
                    v.wait_ge(s["dt_step"].sem, s["dt_step"].at(j, n))
                    nc.vector.scalar_tensor_tensor(out=t7, in0=t7, scalar=c, in1=t6, op0=ALU.add, op1=ALU.mult)\
                        .then_inc(s["dt_step"].sem, 1)
                    n += 1
                v.wait_ge(s["dt_step"].sem, s["dt_step"].at(j, n))
                nc.vector.scalar_tensor_tensor(out=t7, in0=t7, scalar=1.0, in1=t5, op0=ALU.add, op1=ALU.mult)\
                    .then_inc(s["dt_step"].sem, 1)
                v.wait_ge(s["dt_step"].sem, s["dt_step"].at(j, n + 1))
                assert n + 1 == s["dt_step"].per

            def dt_write(j):
                v.wait_ge(s["mdt_made"].sem, s["mdt_made"].at(j - 1))
                nc.vector.tensor_scalar(t3, xd, 0.0, None, ALU.max).then_inc(dt_tail.sem, 1)
                v.wait_ge(dt_tail.sem, dt_tail.at(j, 1))
                nc.vector.scalar_tensor_tensor(out=dtv[:, :], in0=t7, scalar=2.0, in1=t3, op0=ALU.mult, op1=ALU.add)\
                    .then_inc(dt_tail.sem, 1)
                v.wait_ge(dt_tail.sem, dt_tail.at(j, 2))
                nc.vector.scalar_tensor_tensor(
                    out=t4.rearrange("p (u h) -> p u h", u=TILES), in0=dtv[:, :].rearrange("p (u h) -> p u h", u=TILES),
                    scalar=-1.0, in1=neg_a[:, :].rearrange("p (o h) -> p o h", o=1).broadcast_to([P, TILES, HEADS]),
                    op0=ALU.mult, op1=ALU.mult).then_inc(dt_tail.sem, 1)
                v.wait_ge(dt_tail.sem, dt_tail.at(j, 3))
                nc.vector.tensor_copy(a_hi[:, :], t4).then_inc(dt_tail.sem, 1)
                v.wait_ge(dt_tail.sem, dt_tail.at(j, 4))
                nc.vector.tensor_tensor(a_lo[:, :], t4, a_hi[:, :].bitcast(F32), ALU.subtract).then_inc(s["dt_ready"].sem, 1)

            def front(i, q):
                u = ORDER[q]
                if q == 0:
                    v.wait_ge(s["silu_made"].sem, s["silu_made"].at(i))
                v.wait_ge(s["tr_ps"].sem, s["tr_ps"].at(i, q))
                v.wait_ge(s["b_lo_made"].sem, s["b_lo_made"].at(i, q))
                nc.vector.tensor_copy(xb32[:, :, :], cxs(i, 0, 2 * BT).rearrange("p (n t) -> p n t", n=2)[:, :, u * P:(u + 1) * P])\
                    .then_inc(s["xb_copied"].sem, 1)
                v.wait_ge(s["xb_hi_made"].sem, s["xb_hi_made"].at(i, q + 1))
                v.wait_ge(s["y_ps"].sem, s["y_ps"].at(i, q - 1))
                nc.vector.tensor_tensor(xb_lo[:, q % 2, :, :].rearrange("p n t -> p (n t)"), p_tr[:, 0:2 * P],
                                        xb_hi[:, q % 2, :, :].rearrange("p n t -> p (n t)").bitcast(F32), ALU.subtract)\
                    .then_inc(s["xb_lo_made"].sem, 1)
                v.wait_ge(s["dec_made"].sem, s["dec_made"].at(i, q + 1))
                v.wait_ge(s["dt_ready"].sem, s["dt_ready"].at(i))
                nc.vector.tensor_tensor(wd[:, :], dec[:, :, P - 1], dtv[:, u * HEADS:(u + 1) * HEADS], ALU.mult)\
                    .then_inc(s["wd_made"].sem, 1)
                v.wait_ge(s["wd_made"].sem, s["wd_made"].at(i, q + 1))
                v.wait_ge(s["xs_lo_made"].sem, s["xs_lo_made"].at(i, q))
                nc.vector.tensor_tensor(xs32[:, :, :], over_heads(p_tr[:, 0:P]), per_head(wd[:, :]), ALU.mult)\
                    .then_inc(s["xs_made"].sem, 1)
                v.wait_ge(s["mdt_made"].sem, s["mdt_made"].at(i, q + 1))
                v.wait_ge(s["att_lo_made"].sem, s["att_lo_made"].at(i, q))
                nc.vector.tensor_tensor(flat(att32[:, :, :]), flat(dec[:, :, :]), flat(mdt[:, :, :]), ALU.mult)\
                    .then_inc(s["t1"].sem, 1)
                v.wait_ge(s["t1"].sem, s["t1"].at(i, q + 1))
                v.wait_ge(s["sc_ps"].sem, s["sc_ps"].at(i, q + 1))
                nc.vector.tensor_tensor(flat(att32[:, :, :]), p_s[:, :], flat(att32[:, :, :]), ALU.mult)\
                    .then_inc(s["t2"].sem, 1)
                v.wait_ge(s["t2"].sem, s["t2"].at(i, q + 1))
                for h in range(HEADS):
                    ins = nc.vector.scalar_tensor_tensor(out=att32[:, h, :], in0=ident[:, :], scalar=head_sb[:, 1, h:h + 1],
                                                         in1=att32[:, h, :], op0=ALU.mult, op1=ALU.add)
                ins.then_inc(s["att_made"].sem, 1)
                v.wait_ge(s["s_hi_made"].sem, s["s_hi_made"].at(i, q + 1))
                v.wait_ge(s["y_ps"].sem, s["y_ps"].at(i, q))
                nc.vector.tensor_tensor(flat(s_lo[:, :, :]), flat(state[:, u // CPB, :, :]), flat(s_hi[:, :, :].bitcast(F32)),
                                        ALU.subtract).then_inc(s["s_lo_made"].sem, 1)

            def back(i, q):
                u = ORDER[q]
                v.wait_ge(s["st_ps"].sem, s["st_ps"].at(i, q + 1))
                v.wait_ge(s["s_decayed"].sem, s["s_decayed"].at(i, q + 1))
                sv = flat(state[:, u // CPB, :, :])
                nc.vector.tensor_tensor(sv, p_st[:, :], sv, ALU.add).then_inc(s["s_updated"].sem, 1)
                v.wait_ge(s["y_ps"].sem, s["y_ps"].at(i, q + 1))
                v.wait_ge(s["in_out"].sem, s["in_out"].at(i))
                v.wait_ge(s["y_hi_made"].sem, s["y_hi_made"].at(i, q))
                nc.vector.tensor_tensor(y32[:, :, :], p_y[:, :].rearrange("p (h t) -> p h t", h=HEADS), z_of(i, u), ALU.mult)\
                    .then_inc(s["y_gated"].sem, 1)
                v.wait_ge(s["y_hi_made"].sem, s["y_hi_made"].at(i, q + 1))
                nc.vector.tensor_tensor(flat(y_lo[:, :, :]), flat(y32[:, :, :]), flat(y_hi[:, :, :].bitcast(F32)),
                                        ALU.subtract).then_inc(s["y_lo_made"].sem, 1)

            def output(i, q):
                u = ORDER[q]
                v.wait_ge(xr_in.sem, xr_in.at(i))
                keep = lnk[:, bass.ds(i * 2 * TILES, 2 * TILES)]
                nc.vector.tensor_scalar(xr[:, u, :], xr[:, u, :], keep[:, u:u + 1], keep[:, TILES + u:TILES + u + 1],
                                        ALU.mult, ALU.add).then_inc(s["xhat"].sem, 1)
                v.wait_ge(s["xhat"].sem, s["xhat"].at(i, q + 1))
                v.wait_ge(s["o_ps"].sem, s["o_ps"].at(i, q + 1))
                nc.vector.tensor_tensor(xr[:, u, :], p_o[:, :], xr[:, u, :], ALU.add).then_inc(s["h_made"].sem, 1)

            def body(i, more):
                for step in range(STEPS):
                    if step < TILES:
                        front(i, step)
                    if step == 0 and more:
                        norm(i + 1)
                        turn(i + 1)
                    if 1 <= step <= TILES:
                        back(i, step - 1)
                    if more:
                        if step == 3:
                            dt_start(i + 1)
                        if step == 4:
                            dt_finish(i + 1)
                            dt_write(i + 1)
                        convolve(i + 1, CONV_AT[step])
                    if step >= 2:
                        output(i, step - 2)
                if more:
                    keep_history(i + 1)

            nc.vector.memset(raw[:, :, :, 0:TAPS - 1], 0.0).then_inc(zeroed.sem, 1)
            nc.vector.memset(state[:, :, :, :], 0.0).then_inc(zeroed.sem, 1)
            norm(0)
            v.wait_ge(par_in.sem, par_in.at(0, 6 * 16))
            v.wait_ge(win_in.sem, win_in.at(0, 16 * KD))
            for k in range(KD):
                rows = cx[:, k * D_PROJ:(k + 1) * D_PROJ]
                nc.vector.tensor_scalar(rows, rows, ln1_sb[:, k:k + 1], None, ALU.mult).then_inc(win_scaled.sem, 1)
            wv = cx[:, 0:KD * D_PROJ].rearrange("p (k n) -> p k n", k=KD)
            v.wait_ge(w_hi_made.sem, w_hi_made.at(0, 3))
            v.wait_ge(win_scaled.sem, win_scaled.at(0, KD))
            nc.vector.tensor_tensor(wi_lo[:, :, :], wv[:, :, 0:NW], wi_hi[:, :, :].bitcast(F32), ALU.subtract)\
                .then_inc(w_lo_made.sem, 1)
            nc.vector.tensor_tensor(wdt[:, :, HEADS:], wv[:, :, NW:D_PROJ], wdt[:, :, 0:HEADS].bitcast(F32), ALU.subtract)\
                .then_inc(w_lo_made.sem, 1)
            nc.vector.tensor_tensor(flat(wo_lo[:, :, :]), zs[:, 0:HEADS * D_MODEL], flat(wo_hi[:, :, :].bitcast(F32)),
                                    ALU.subtract).then_inc(w_lo_made.sem, 1)
            turn(0)
            dt_start(0)
            v.wait_ge(neg_a_made.sem, neg_a_made.at(0, 1))
            dt_finish(0)
            dt_write(0)
            v.wait_ge(zeroed.sem, zeroed.at(0, 2))
            convolve(0, range(1, 1 + CONV))
            keep_history(0)
            with nc.vector.Fori(0, BLOCKS - 1) as i:
                body(i, True)
            body(BLOCKS - 1, False)


def mlp_phase(nc, x, ln2, gate, up, down, lora_a, lora_b, w_ffn, ffn_bias, lora_coef, h_scratch, out):
    with ExitStack() as ctx:
        def sb(name, shape, dt=F32):
            return ctx.enter_context(nc.sbuf_tensor(name, shape, dt))

        def psum(name):
            return ctx.enter_context(nc.psum_tensor(name, [P, 512], F32))

        def sig(name, per, seeded=True):
            return Signal(nc, ctx, name, per, seeded)

        D = D_MODEL
        PIECE = 2
        PIECES = FT // PIECE
        w_gu = sb("w_gu", [P, KD, 2, INTER])
        w_dn = sb("w_dn", [P, FT, D])
        gu_hi, gu_lo = sb("gu_hi", [P, 2, KD, 2, P], F32R), sb("gu_lo", [P, 2, KD, 2, P], F32R)
        dn_hi, dn_lo = sb("dn_hi", [P, 2, D], F32R), sb("dn_lo", [P, 2, D], F32R)
        ZT = KD * BT
        zt_hi, zt_lo = sb("zt2_hi", [P, 2 * ZT], F32R), sb("zt2_lo", [P, 2 * ZT], F32R)
        hz = sb("hz", [P, 2, D])
        g32, m32 = sb("g32", [P, BT]), sb("m32", [P, BT])
        m_hi, m_lo = sb("m_hi", [P, 2, BT], F32R), sb("m_lo", [P, 2, BT], F32R)
        hr = sb("hr", [P, TILES, D])
        x1 = sb("x1", [P, TILES, D])
        z3 = sb("z3", [P, D])
        z3t_hi, z3t_lo = sb("z3t_hi", [P, KD, P], F32R), sb("z3t_lo", [P, KD, P], F32R)
        fo = sb("fo", [P, D])
        we_hi, we_lo = sb("we_hi", [P, KD, D], F32R), sb("we_lo", [P, KD, D], F32R)
        bias = sb("bias", [P, D])
        ident = sb("ident2", [P, P])
        ln2_sb, coef = sb("ln2_sb", [P, KD]), sb("coef", [P, 1])
        mhalf = sb("mhalf2", [P, TILES])
        bn = sb("bn2", [P, 4, TILES, 6])
        mv = sb("mv2", [P, 4, TILES, 2])
        tmp = sb("tmp", [P, 4, 4, TILES])
        scl = sb("scl", [P, 4, 2, TILES])

        p_g, p_u, p_x, p_f = (psum(n) for n in ("p_g", "p_u", "p_x", "p_f"))
        p_m = [psum(f"p_m{u}") for u in range(TILES)]

        par_in, lora_in, wt_in = (sig(n, 1, False) for n in ("par2_in", "lora_in", "wt_in"))
        piece_in = [sig(f"piece_in{c}", 1, False) for c in range(PIECES)]
        hz_in = [sig(f"hz_in{n}", 16 * TILES // 2, False) for n in range(2)]
        hr_in, x1_in = sig("hr_in", 16, False), sig("x1_in", 32, False)
        out_done = sig("out_done", 16 * TILES)
        consts, ident_zero = sig("consts2", 1, False), sig("ident_zero", 1, False)
        w_scaled, lora_scaled, lora_ps, lora_added, we_hi_made, we_lo_made = (
            sig(n, 1, False) for n in ("w_scaled", "lora_scaled", "lora_ps", "lora_added", "we_hi_made", "we_lo_made"))
        pe = {n: sig(n, per) for n, per in dict(
            g_ps=FT, u_ps=FT, dn_ps=FT, z2_ps=TILES, z3_ps=TILES, f_ps=TILES).items()}
        act = {n: sig(n, per) for n, per in dict(
            silu_made=FT, m_hi_made=FT, gu_hi_made=FT, dn_hi_made=FT, z2_hi_made=TILES, z3_hi_made=TILES).items()}
        dve = {n: sig(n, per) for n, per in dict(
            m_made=FT, m_lo_made=FT, dn_lo_made=FT, z2_lo_made=TILES, z3_lo_made=TILES,
            bn_h=TILES, mv_h=TILES, z2_made=TILES,
            h2_made=TILES, bn_1=TILES, mv_1=TILES, n1_made=TILES, bn_2=TILES, mv_2=TILES, z3_made=TILES,
            f_made=TILES, bn_3=TILES, mv_3=TILES, n3_made=TILES).items()}
        pool = {n: sig(n, per) for n, per in dict(
            gu_lo_made=FT, st_h=3 * TILES, sc_h=TILES, st_1=3, sc_1=1, st_2=3, sc_2=1, st_3=3 * TILES, sc_3=TILES,
            x1_made=TILES, out_made=TILES).items()}
        s = {**pe, **act, **dve, **pool}

        passed_pool, passed_vector = (ctx.enter_context(nc.semaphore(n)) for n in ("passed_pool", "passed_vector"))

        block = ctx.enter_context(nc.Block())
        x_blocks = x.rearrange("(b i c p) d -> b i p c d", b=BATCH, i=BLOCKS, c=CPB)
        o_tiles = out.rearrange("(b i c p) d -> b i c p d", b=BATCH, i=BLOCKS, c=CPB)

        def zts(t, j, first, count):
            return t[:, bass.ds((j % 2) * ZT + first, count)]

        def zt_tile(t, j, u):
            return zts(t, j, 0, ZT).rearrange("p (k t) -> p k t", k=KD)[:, :, u * P:(u + 1) * P]

        Z3_AT = {3 + 2 * u: u for u in range(TILES)}
        F_AT = {4 + 2 * u: u for u in range(TILES)}
        OUT_AT = {5 + 2 * u: u for u in range(TILES)}
        STORE_AT = {6 + 2 * u: u for u in range(TILES)}
        LORA_AT = {2 + k: k for k in range(KD)}

        @block.sync
        def _(sp):
            def load_tile(j, u):
                if not (isinstance(j, int) and j == 0 and u < 2):
                    sp.wait_ge(s["z2_ps"].sem, s["z2_ps"].at(j, u - 1))
                sp.dma_start(hz[:, u % 2, :], h_scratch[bass.ds(j * TILES + u, 1)].rearrange("o p d -> (o p) d"))\
                    .then_inc(hz_in[u % 2].sem, 16)

            def load_hr(j):
                sp.dma_start(hr[:, :, :], h_scratch[bass.ds(j * TILES, TILES)].rearrange("u p d -> p u d"))\
                    .then_inc(hr_in.sem, 16)

            def load_x1(j):
                for b in range(BATCH):
                    sp.dma_start(x1[:, b * CPB:(b + 1) * CPB, :], x_blocks[b, bass.ds(j, 1)].rearrange("o p c d -> (o p) c d"))\
                        .then_inc(x1_in.sem, 16)

            def store(t, u):
                sp.wait_ge(s["out_made"].sem, s["out_made"].at(t, u + 1))
                sp.dma_start(o_tiles[u // CPB, bass.ds(t, 1), u % CPB].rearrange("o p d -> (o p) d"), fo[:, :])\
                    .then_inc(out_done.sem, 16)

            def load_piece(c):
                cols = slice(c * PIECE * P, (c + 1) * PIECE * P)
                for n, w in enumerate((gate, up)):
                    sp.dma_start(w_gu[:, :, n, cols], w[:, cols].rearrange("(k p) f -> p k f", p=P)).then_inc(piece_in[c].sem, 16)
                sp.dma_start(w_dn[:, c * PIECE:(c + 1) * PIECE, :],
                             down[cols, :].rearrange("(f p) d -> p f d", p=P)).then_inc(piece_in[c].sem, 16)

            out_done.seed(sp)
            sp.dma_start(ln2_sb[:, :], ln2).then_inc(par_in.sem, 16)
            load_tile(0, 0)
            load_tile(0, 1)
            load_piece(0)
            load_tile(0, 2)
            load_tile(0, 3)
            load_piece(1)
            for dst, src in ((z3, lora_a), (fo, lora_b), (coef, lora_coef), (bias, ffn_bias)):
                sp.dma_start(dst[:, :], src).then_inc(lora_in.sem, 16)
            sp.dma_start(x1[:, :, :], w_ffn.rearrange("(k p) o -> p k o", p=P)).then_inc(wt_in.sem, 16)
            for c in range(2, PIECES):
                load_piece(c)

            def body(j, tail, more):
                if tail:
                    sp.wait_ge(s["x1_made"].sem, s["x1_made"].at(j - 1))
                load_hr(j)
                if more:
                    load_tile(j + 1, 0)
                for u in range(TILES):
                    if more and u + 1 < TILES:
                        load_tile(j + 1, u + 1)
                    if tail:
                        store(j - 1, u)
                if not tail:
                    sp.wait_ge(we_lo_made.sem, we_lo_made.at(0, 1))
                load_x1(j)

            body(0, False, True)
            with nc.sync.Fori(1, BLOCKS - 1) as j:
                body(j, True, True)
            body(BLOCKS - 1, True, False)
            for u in range(TILES):
                store(BLOCKS - 1, u)
            sp.wait_ge(out_done.sem, out_done.at(BLOCKS - 1))

        @block.tensor
        def _(t):
            for v in pe.values():
                v.seed(t)

            def turn_z2(j, u):
                t.wait_ge(s["z2_made"].sem, s["z2_made"].at(j, u + 1))
                t.wait_ge(s["z2_lo_made"].sem, s["z2_lo_made"].at(j, u))
                for k in range(KD):
                    ins = nc.tensor.transpose(p_x[:, k * P:(k + 1) * P], hz[:, u % 2, k * P:(k + 1) * P], ident[:, :])
                ins.then_inc(s["z2_ps"].sem, 1)

            def turn_z3(j, u, more):
                t.wait_ge(s["z3_made"].sem, s["z3_made"].at(j, u + 1))
                t.wait_ge(s["z3_lo_made"].sem, s["z3_lo_made"].at(j, u))
                if more:
                    t.wait_ge(s["z2_lo_made"].sem, s["z2_lo_made"].at(j + 2, u))
                for k in range(KD):
                    ins = nc.tensor.transpose(p_x[:, k * P:(k + 1) * P], z3[:, k * P:(k + 1) * P], ident[:, :])
                ins.then_inc(s["z3_ps"].sem, 1)

            def linear(j, u):
                t.wait_ge(s["z3_lo_made"].sem, s["z3_lo_made"].at(j, u + 1))
                t.wait_ge(s["f_made"].sem, s["f_made"].at(j, u))
                n = 0
                for k in range(KD):
                    for l, r in split_passes(z3t_hi, z3t_lo, we_hi, we_lo):
                        ins = nc.tensor.matmul(p_f[:, :], l[:, k, :], r[:, k, :], start=(n == 0), stop=(n == 3 * KD - 1))
                        n += 1
                ins.then_inc(s["f_ps"].sem, 1)

            def gate_up(j, f, which):
                n = 0
                bank = (p_g, p_u)[which]
                for k in range(KD):
                    for l, r in split_passes(gu_hi, gu_lo, zt_hi, zt_lo):
                        ins = nc.tensor.matmul(bank[:, :], l[:, f % 2, k, which, :], zts(r, j, k * BT, BT),
                                               start=(n == 0), stop=(n == 3 * KD - 1))
                        n += 1
                return ins

            def down_part(j, f):
                t.wait_ge(s["m_hi_made"].sem, s["m_hi_made"].at(j, f + 1))
                t.wait_ge(s["m_lo_made"].sem, s["m_lo_made"].at(j, f + 1))
                t.wait_ge(s["dn_hi_made"].sem, s["dn_hi_made"].at(j, f + 1))
                t.wait_ge(s["dn_lo_made"].sem, s["dn_lo_made"].at(j, f + 1))
                if f == 0:
                    t.wait_ge(s["h2_made"].sem, s["h2_made"].at(j - 1))
                for u in range(TILES):
                    for n, (l, r) in enumerate(split_passes(m_hi, m_lo, dn_hi, dn_lo)):
                        ins = nc.tensor.matmul(p_m[u][:, :], l[:, f % 2, u * P:(u + 1) * P], r[:, f % 2, :],
                                               start=(f == 0 and n == 0), stop=(f == FT - 1 and n == 2))
                ins.then_inc(s["dn_ps"].sem, 1)

            def body(j, tail, more):
                t.wait_ge(s["z2_lo_made"].sem, s["z2_lo_made"].at(j))
                for f in range(FT):
                    t.wait_ge(s["gu_hi_made"].sem, s["gu_hi_made"].at(j, f + 1))
                    t.wait_ge(s["gu_lo_made"].sem, s["gu_lo_made"].at(j, f + 1))
                    t.wait_ge(s["silu_made"].sem, s["silu_made"].at(j, f))
                    gate_up(j, f, 0).then_inc(s["g_ps"].sem, 1)
                    t.wait_ge(s["m_made"].sem, s["m_made"].at(j, f))
                    gate_up(j, f, 1).then_inc(s["u_ps"].sem, 1)
                    if f:
                        down_part(j, f - 1)
                    if not tail and f in LORA_AT:
                        k = LORA_AT[f]
                        t.wait_ge(lora_scaled.sem, lora_scaled.at(0, 1))
                        if k:
                            t.wait_ge(lora_added.sem, lora_added.at(0, k))
                        nc.tensor.matmul(p_f[:, :], z3[:, k * P:(k + 1) * P], fo[:, :], start=True, stop=True)\
                            .then_inc(lora_ps.sem, 1)
                    if tail and f in Z3_AT:
                        turn_z3(j - 1, Z3_AT[f], more)
                    if tail and f in F_AT:
                        linear(j - 1, F_AT[f])
                    if more and f in F_AT:
                        if tail:
                            t.wait_ge(s["z3_lo_made"].sem, s["z3_lo_made"].at(j - 1, F_AT[f] + 1))
                        turn_z2(j + 1, F_AT[f])
                down_part(j, FT - 1)

            t.wait_ge(consts.sem, consts.at(0, 2))
            for u in range(TILES):
                turn_z2(0, u)
            body(0, False, True)
            with nc.tensor.Fori(1, BLOCKS - 1) as j:
                body(j, True, True)
            body(BLOCKS - 1, True, False)
            for u in range(TILES):
                turn_z3(BLOCKS - 1, u, False)
                linear(BLOCKS - 1, u)

        @block.scalar
        def _(a):
            for v in act.values():
                v.seed(a)

            def split_gu(j, n, f):
                cols = slice(f * P, (f + 1) * P)
                a.wait_ge(w_scaled.sem, w_scaled.at(0, (f // PIECE + 1) * KD))
                a.wait_ge(s["u_ps"].sem, s["u_ps"].at(j, n))
                for w in range(2):
                    ins = nc.scalar.copy(gu_hi[:, f % 2, :, w, :], w_gu[:, :, w, cols])
                ins.then_inc(s["gu_hi_made"].sem, 1)

            def split_dn(j, f):
                a.wait_ge(s["dn_ps"].sem, s["dn_ps"].at(j, f - 1))
                nc.scalar.copy(dn_hi[:, f % 2, :], w_dn[:, f, :]).then_inc(s["dn_hi_made"].sem, 1)

            def turn_z2(j, u):
                a.wait_ge(s["z2_ps"].sem, s["z2_ps"].at(j, u + 1))
                a.wait_ge(s["u_ps"].sem, s["u_ps"].at(j - 2))
                nc.scalar.copy(zt_tile(zt_hi, j, u), p_x[:, :].rearrange("p (k t) -> p k t", k=KD))\
                    .then_inc(s["z2_hi_made"].sem, 1)

            def turn_z3(j, u):
                a.wait_ge(s["z3_ps"].sem, s["z3_ps"].at(j, u + 1))
                a.wait_ge(s["f_ps"].sem, s["f_ps"].at(j, u))
                nc.scalar.copy(z3t_hi[:, :, :].rearrange("p k t -> p (k t)"), p_x[:, :]).then_inc(s["z3_hi_made"].sem, 1)

            def body(j, tail, more):
                for f in range(FT):
                    if f < FT - 1:
                        split_gu(j, f, f + 1)
                    elif more:
                        split_gu(j, f, 0)
                    split_dn(j, f)
                    if tail and f - 1 in Z3_AT:
                        turn_z3(j - 1, Z3_AT[f - 1])
                    if more and f - 1 in F_AT:
                        turn_z2(j + 1, F_AT[f - 1])
                    a.wait_ge(s["g_ps"].sem, s["g_ps"].at(j, f + 1))
                    a.wait_ge(s["m_made"].sem, s["m_made"].at(j, f))
                    nc.scalar.activation(g32[:, :], p_g[:, :], ACT.Silu).then_inc(s["silu_made"].sem, 1)
                    a.wait_ge(s["m_made"].sem, s["m_made"].at(j, f + 1))
                    a.wait_ge(s["dn_ps"].sem, s["dn_ps"].at(j, f - 1))
                    nc.scalar.copy(m_hi[:, f % 2, :], m32[:, :]).then_inc(s["m_hi_made"].sem, 1)
                    if not tail and f == FT - 3:
                        a.wait_ge(lora_added.sem, lora_added.at(0, KD))
                        nc.scalar.copy(we_hi[:, :, :], x1[:, :, :]).then_inc(we_hi_made.sem, 1)

            split_gu(0, 0, 0)
            for u in range(TILES):
                turn_z2(0, u)
            body(0, False, True)
            with nc.scalar.Fori(1, BLOCKS - 1) as j:
                body(j, True, True)
            body(BLOCKS - 1, True, False)
            for u in range(TILES):
                turn_z3(BLOCKS - 1, u)

        H, N1, N2, N3 = range(4)

        @block.gpsimd
        def _(g):
            for v in pool.values():
                v.seed(g)
            nc.gpsimd.memset(mhalf[:, :], -0.5).then_inc(consts.sem, 1)
            nc.gpsimd.memset(ident[:, :], 0.0).then_inc(ident_zero.sem, 1)
            g.wait_ge(ident_zero.sem, ident_zero.at(0, 1))
            nc.gpsimd.affine_select(out=ident[:, :], in_=ident[:, :], compare_op=ALU.not_equal, fill=1.0, base=0,
                                    pattern=[[-1, P]], channel_multiplier=1).then_inc(consts.sem, 1)
            g.wait_ge(consts.sem, consts.at(0, 2))

            def chain(step, made, j, n0, row, cols, rms):
                mean, var = mv[:, row, cols, 0], mv[:, row, cols, 1]
                t0, t1, t2, t3 = (tmp[:, row, n, cols] for n in range(4))

                def then(n, ins):
                    ins.then_inc(step.sem, 1)
                    g.wait_ge(step.sem, step.at(j, n0 + n))
                    waits_apart(g, passed_pool)

                if rms:
                    then(1, nc.gpsimd.tensor_tensor(t0, mean, mean, ALU.mult))
                    then(2, nc.gpsimd.tensor_tensor(t1, t0, var, ALU.add))
                    then(3, nc.gpsimd.tensor_scalar(t2, t1, EPS, 1.0, ALU.add, ALU.mult))
                    nc.gpsimd.tensor_tensor(scl[:, row, 0, cols], t2, mhalf[:, cols], ALU.pow).then_inc(made.sem, 1)
                else:
                    then(1, nc.gpsimd.tensor_scalar(t2, var, EPS, 1.0, ALU.add, ALU.mult))
                    then(2, nc.gpsimd.tensor_tensor(scl[:, row, 0, cols], t2, mhalf[:, cols], ALU.pow))
                    then(3, nc.gpsimd.tensor_tensor(t0, mean, scl[:, row, 0, cols], ALU.mult))
                    nc.gpsimd.tensor_scalar(scl[:, row, 1, cols], t0, -1.0, 1.0, ALU.mult, ALU.mult).then_inc(made.sem, 1)

            def split_lo(j, n, f):
                cols = slice(f * P, (f + 1) * P)
                g.wait_ge(s["gu_hi_made"].sem, s["gu_hi_made"].at(j, n))
                for w in range(2):
                    ins = nc.gpsimd.tensor_tensor(gu_lo[:, f % 2, :, w, :], w_gu[:, :, w, cols],
                                                  gu_hi[:, f % 2, :, w, :].bitcast(F32), ALU.subtract)
                ins.then_inc(s["gu_lo_made"].sem, 1)

            def norm_h(j, u):
                g.wait_ge(s["mv_h"].sem, s["mv_h"].at(j, u + 1))
                g.wait_ge(s["z2_made"].sem, s["z2_made"].at(j, u))
                waits_apart(g, passed_pool)
                chain(s["st_h"], s["sc_h"], j, 3 * u, H, slice(u, u + 1), True)

            def end(j, u):
                g.wait_ge(s["n3_made"].sem, s["n3_made"].at(j, u + 1))
                nc.gpsimd.tensor_tensor(fo[:, :], fo[:, :], x1[:, u, :], ALU.add).then_inc(s["out_made"].sem, 1)

            def norm_3(j, u):
                g.wait_ge(s["mv_3"].sem, s["mv_3"].at(j, u + 1))
                waits_apart(g, passed_pool)
                chain(s["st_3"], s["sc_3"], j, 3 * u, N3, slice(u, u + 1), False)

            def norm_1(j):
                g.wait_ge(s["mv_1"].sem, s["mv_1"].at(j))
                g.wait_ge(s["n1_made"].sem, s["n1_made"].at(j - 1))
                waits_apart(g, passed_pool)
                chain(s["st_1"], s["sc_1"], j, 0, N1, slice(0, TILES), False)

            def first_sum(j):
                g.wait_ge(x1_in.sem, x1_in.at(j))
                for u in range(TILES):
                    g.wait_ge(s["n1_made"].sem, s["n1_made"].at(j, u + 1))
                    nc.gpsimd.tensor_tensor(x1[:, u, :], x1[:, u, :], hr[:, u, :], ALU.add).then_inc(s["x1_made"].sem, 1)

            def norm_2(j):
                g.wait_ge(s["mv_2"].sem, s["mv_2"].at(j))
                g.wait_ge(s["z3_made"].sem, s["z3_made"].at(j - 1))
                waits_apart(g, passed_pool)
                chain(s["st_2"], s["sc_2"], j, 0, N2, slice(0, TILES), False)

            def body(j, tail, more):
                for f in range(FT):
                    if f < FT - 1:
                        split_lo(j, f + 2, f + 1)
                    elif more:
                        split_lo(j, FT + 1, 0)
                    if tail:
                        if f in STORE_AT:
                            end(j - 1, STORE_AT[f])
                        if f == 0:
                            norm_1(j - 1)
                        if f == 1:
                            first_sum(j - 1)
                        if f == 2:
                            norm_2(j - 1)
                        if f in OUT_AT:
                            norm_3(j - 1, OUT_AT[f])
                    if more and f in Z3_AT:
                        norm_h(j + 1, Z3_AT[f])

            norm_h(0, 0)
            norm_h(0, 1)
            split_lo(0, 1, 0)
            norm_h(0, 2)
            norm_h(0, 3)
            body(0, False, True)
            with nc.gpsimd.Fori(1, BLOCKS - 1) as j:
                body(j, True, True)
            body(BLOCKS - 1, True, False)
            last = BLOCKS - 1
            norm_1(last)
            first_sum(last)
            norm_2(last)
            for u in range(TILES):
                norm_3(last, u)
                end(last, u)

        @block.vector
        def _(v):
            for e in dve.values():
                e.seed(v)

            def stats(src, row, u, bn_sig, mv_sig, j):
                nc.vector.bn_stats(bn[:, row, u, :], src).then_inc(bn_sig.sem, 1)
                v.wait_ge(bn_sig.sem, bn_sig.at(j, u + 1))
                waits_apart(v, passed_vector)
                nc.vector.bn_aggr(mv[:, row, u, :], bn[:, row, u, :]).then_inc(mv_sig.sem, 1)

            def scaled(dst, src, row, u):
                return nc.vector.tensor_scalar(dst, src, scl[:, row, 0, u:u + 1], scl[:, row, 1, u:u + 1], ALU.mult, ALU.add)

            def scale_weights(c):
                v.wait_ge(piece_in[c].sem, piece_in[c].at(0, 48))
                v.wait_ge(par_in.sem, par_in.at(0, 16))
                cols = slice(c * PIECE * P, (c + 1) * PIECE * P)
                for k in range(KD):
                    nc.vector.tensor_scalar(w_gu[:, k, :, cols], w_gu[:, k, :, cols], ln2_sb[:, k:k + 1], None, ALU.mult)\
                        .then_inc(w_scaled.sem, 1)

            def split_dn(j, f):
                v.wait_ge(s["dn_hi_made"].sem, s["dn_hi_made"].at(j, f + 1))
                nc.vector.tensor_tensor(dn_lo[:, f % 2, :], w_dn[:, f, :], dn_hi[:, f % 2, :].bitcast(F32), ALU.subtract)\
                    .then_inc(s["dn_lo_made"].sem, 1)

            def norm_h(j, u):
                v.wait_ge(hz_in[u % 2].sem, hz_in[u % 2].at(j, 16 * (u // 2 + 1)))
                v.wait_ge(s["sc_h"].sem, s["sc_h"].at(j - 1, u + 1))
                stats(hz[:, u % 2, :], H, u, s["bn_h"], s["mv_h"], j)

            def make_z2(j, u):
                v.wait_ge(s["sc_h"].sem, s["sc_h"].at(j, u + 1))
                nc.vector.tensor_scalar(hz[:, u % 2, :], hz[:, u % 2, :], scl[:, H, 0, u:u + 1], None, ALU.mult)\
                    .then_inc(s["z2_made"].sem, 1)

            def turn_z2(j, u):
                v.wait_ge(s["z2_hi_made"].sem, s["z2_hi_made"].at(j, u + 1))
                nc.vector.tensor_tensor(zt_tile(zt_lo, j, u), p_x[:, :].rearrange("p (k t) -> p k t", k=KD),
                                        zt_tile(zt_hi, j, u).bitcast(F32), ALU.subtract).then_inc(s["z2_lo_made"].sem, 1)

            def sums(j):
                v.wait_ge(hr_in.sem, hr_in.at(j))
                v.wait_ge(s["dn_ps"].sem, s["dn_ps"].at(j))
                v.wait_ge(s["sc_1"].sem, s["sc_1"].at(j - 1))
                for u in range(TILES):
                    nc.vector.tensor_tensor(hr[:, u, :], p_m[u][:, :], hr[:, u, :], ALU.add).then_inc(s["h2_made"].sem, 1)

            def first_stats(j):
                for u in range(TILES):
                    v.wait_ge(s["h2_made"].sem, s["h2_made"].at(j, u + 1))
                    stats(hr[:, u, :], N1, u, s["bn_1"], s["mv_1"], j)

            def first_norm(j):
                v.wait_ge(s["sc_1"].sem, s["sc_1"].at(j))
                for u in range(TILES):
                    scaled(hr[:, u, :], hr[:, u, :], N1, u).then_inc(s["n1_made"].sem, 1)

            def second_stats(j):
                v.wait_ge(s["sc_2"].sem, s["sc_2"].at(j - 1))
                for u in range(TILES):
                    v.wait_ge(s["x1_made"].sem, s["x1_made"].at(j, u + 1))
                    stats(x1[:, u, :], N2, u, s["bn_2"], s["mv_2"], j)

            def make_z3(j, u):
                v.wait_ge(s["sc_2"].sem, s["sc_2"].at(j))
                v.wait_ge(s["z3_ps"].sem, s["z3_ps"].at(j, u))
                scaled(z3[:, :], x1[:, u, :], N2, u).then_inc(s["z3_made"].sem, 1)

            def turn_z3(j, u):
                v.wait_ge(s["z3_hi_made"].sem, s["z3_hi_made"].at(j, u + 1))
                nc.vector.tensor_tensor(z3t_lo[:, :, :].rearrange("p k t -> p (k t)"), p_x[:, :],
                                        z3t_hi[:, :, :].rearrange("p k t -> p (k t)").bitcast(F32), ALU.subtract)\
                    .then_inc(s["z3_lo_made"].sem, 1)

            def linear(j, u):
                v.wait_ge(s["f_ps"].sem, s["f_ps"].at(j, u + 1))
                v.wait_ge(out_done.sem, out_done.at(j, 16 * u))
                nc.vector.tensor_tensor(fo[:, :], p_f[:, :], bias[:, :], ALU.add).then_inc(s["f_made"].sem, 1)
                v.wait_ge(s["f_made"].sem, s["f_made"].at(j, u + 1))
                v.wait_ge(s["sc_3"].sem, s["sc_3"].at(j - 1, u + 1))
                stats(fo[:, :], N3, u, s["bn_3"], s["mv_3"], j)

            def last_norm(j, u):
                v.wait_ge(s["sc_3"].sem, s["sc_3"].at(j, u + 1))
                scaled(fo[:, :], fo[:, :], N3, u).then_inc(s["n3_made"].sem, 1)

            def body(j, tail, more):
                for f in range(FT):
                    split_dn(j, f)
                    if tail:
                        if f == 0:
                            sums(j - 1)
                        if f == 1:
                            first_norm(j - 1)
                        if f == 2:
                            second_stats(j - 1)
                        if f - 1 in Z3_AT:
                            turn_z3(j - 1, Z3_AT[f - 1])
                        if f - 1 in F_AT:
                            linear(j - 1, F_AT[f - 1])
                    if more and f - 1 in F_AT:
                        turn_z2(j + 1, F_AT[f - 1])
                    v.wait_ge(s["u_ps"].sem, s["u_ps"].at(j, f + 1))
                    v.wait_ge(s["silu_made"].sem, s["silu_made"].at(j, f + 1))
                    v.wait_ge(s["m_hi_made"].sem, s["m_hi_made"].at(j, f))
                    v.wait_ge(s["m_lo_made"].sem, s["m_lo_made"].at(j, f))
                    nc.vector.tensor_tensor(m32[:, :], p_u[:, :], g32[:, :], ALU.mult).then_inc(s["m_made"].sem, 1)
                    v.wait_ge(s["m_hi_made"].sem, s["m_hi_made"].at(j, f + 1))
                    nc.vector.tensor_tensor(m_lo[:, f % 2, :], m32[:, :], m_hi[:, f % 2, :].bitcast(F32), ALU.subtract)\
                        .then_inc(s["m_lo_made"].sem, 1)
                    if not tail:
                        if f % PIECE == 0 and f // PIECE + 1 < PIECES:
                            scale_weights(f // PIECE + 1)
                        if f in LORA_AT:
                            k = LORA_AT[f]
                            v.wait_ge(lora_ps.sem, lora_ps.at(0, k + 1))
                            v.wait_ge(wt_in.sem, wt_in.at(0, 16))
                            nc.vector.tensor_tensor(x1[:, k, :], p_f[:, :], x1[:, k, :], ALU.add).then_inc(lora_added.sem, 1)
                        if f == FT - 2:
                            v.wait_ge(we_hi_made.sem, we_hi_made.at(0, 1))
                            nc.vector.tensor_tensor(we_lo[:, :, :], x1[:, :, :], we_hi[:, :, :].bitcast(F32), ALU.subtract)\
                                .then_inc(we_lo_made.sem, 1)
                    if tail:
                        if f == 0:
                            first_stats(j - 1)
                        if f == 2:
                            make_z3(j - 1, 0)
                        if f in F_AT and F_AT[f] + 1 < TILES:
                            make_z3(j - 1, F_AT[f] + 1)
                        if f in OUT_AT:
                            last_norm(j - 1, OUT_AT[f])
                    if more:
                        if f + 1 in Z3_AT:
                            norm_h(j + 1, Z3_AT[f + 1])
                        if f in Z3_AT:
                            make_z2(j + 1, Z3_AT[f])

            norm_h(0, 0)
            norm_h(0, 1)
            scale_weights(0)
            make_z2(0, 0)
            make_z2(0, 1)
            turn_z2(0, 0)
            turn_z2(0, 1)
            for u in range(2, TILES):
                norm_h(0, u)
                make_z2(0, u)
                turn_z2(0, u)
            v.wait_ge(lora_in.sem, lora_in.at(0, 64))
            nc.vector.tensor_scalar(fo[:, :], fo[:, :], coef[:, :], LORA_SCALE, ALU.mult, ALU.mult).then_inc(lora_scaled.sem, 1)
            body(0, False, True)
            with nc.vector.Fori(1, BLOCKS - 1) as j:
                body(j, True, True)
            body(BLOCKS - 1, True, False)
            last = BLOCKS - 1
            sums(last)
            first_stats(last)
            first_norm(last)
            second_stats(last)
            for u in range(TILES):
                make_z3(last, u)
                turn_z3(last, u)
                linear(last, u)
                last_norm(last, u)


def kernel(**inputs):
    import numpy as np
    import concourse.bacc as _bacc
    from concourse.bass_utils import run_bass_kernel_spmd as _run

    a = {k.replace("L0_attn_", "").replace("L0_ffn_", "ffn_"): np.asarray(v) for k, v in inputs.items()}
    columns = lambda w, n: w.reshape(n, P).T
    every = lambda w: np.broadcast_to(w, (P, w.size))
    arrays = {
        "x": a["hidden_states"].reshape(BATCH * SEQ, D_MODEL),
        "w_in": a["w_in"].T,
        "w_out": a["w_out"].T,
        "conv_w": a["conv_w"].reshape(CONV, P, TAPS).transpose(1, 0, 2),
        "conv_b": columns(a["conv_b"], CONV),
        "a_log": every(a["A_log"]), "d_skip": every(a["D"]), "dt_bias": every(a["dt_bias"]),
        "ln1": columns(a["ln1_w"], KD), "ln2": columns(a["ln2_w"], KD),
        "gate": a["gate_w"].T, "up": a["up_w"].T, "down": a["down_w"].T,
        "lora_a": a["ffn_lora_A"].reshape(RANKS, D_MODEL),
        "lora_b": a["ffn_lora_B"].transpose(0, 2, 1).reshape(RANKS, D_MODEL),
        "w_ffn": a["ffn_W"].T,
        "ffn_bias": every(a["ffn_bias"]),
        "lora_coef": np.repeat(a["ffn_lora_weights"], RANKS // a["ffn_lora_weights"].size).reshape(RANKS, 1),
    }
    nc = _bacc.Bacc("TRN2", target_bir_lowering=False, num_devices=1)
    arrays = {n: np.ascontiguousarray(v) for n, v in arrays.items()}
    aps = {n: nc.dram_tensor(n, v.shape, F32, kind="ExternalInput").ap() for n, v in arrays.items()}
    h_scratch = nc.dram_tensor("h_scratch", (BLOCKS * TILES, P, D_MODEL), F32, kind="Internal").ap()
    out = nc.dram_tensor("out", (BATCH, SEQ, D_MODEL), F32, kind="ExternalOutput").ap()
    sandwich_program(nc, h_scratch=h_scratch, out=out.rearrange("b s d -> (b s) d"), **aps)
    r = _run(nc, [arrays], core_ids=[0])
    return r.results[0]["out"]
```

```python
from contextlib import ExitStack

import concourse.bass as bass
from concourse import mybir

F32 = mybir.dt.float32
F32R = mybir.dt.float32r
ALU = mybir.AluOpType
ACT = mybir.ActivationFunctionType

P = 128
EPS = 1e-5
BATCH, SEQ, D_MODEL = 2, 1024, 512
HEADS, STATE, TAPS = 4, 128, 4
D_INNER = 512
D_PROJ = 2 * D_INNER + 2 * P + HEADS
INTER = 1792
RANKS = 128
LORA_SCALE = 2.0

KD = D_MODEL // P
TILES = 4
BT = TILES * P
BLOCKS = BATCH * SEQ // BT
CPB = TILES // BATCH
CW = CPB * P
FT = INTER // P
ORDER = [b * CPB + c for c in range(CPB) for b in range(BATCH)]

CONV = 2 + HEADS
IN_GROUPS = [("dt", 2 * D_INNER + 2 * P, 0)] + \
    [("conv", D_INNER + P, 1), ("conv", D_INNER, 0)] + \
    [("conv", D_INNER + 2 * P + P * h, 2 + h) for h in range(HEADS)] + \
    [("z", P * h, h) for h in range(HEADS)]
NG = len(IN_GROUPS)
IN_AT = [[9, 10], [0, 1, 2], [3, 4, 5], [6, 7, 8]]
CONV_AT = [[], [1], [2, 3, 4], [5, 6]]
SEED = 2


class Signal:

    def __init__(self, nc, ctx, name, per, seeded=True):
        self.sem = ctx.enter_context(nc.semaphore(name))
        self.per = per
        self.base = SEED if seeded else 0

    def at(self, block, n=None):
        return (block + self.base) * self.per + (self.per if n is None else n)

    def seed(self, engine):
        engine.sem_inc(self.sem, self.base * self.per)


def waits_apart(engine, passed):
    engine.sem_inc(passed, 1)


def sandwich_program(nc, x, w_in, w_out, conv_w, conv_b, a_log, d_skip, dt_bias, ln1, ln2, gate, up, down,
                     lora_a, lora_b, w_ffn, ffn_bias, lora_coef, h_scratch, out):
    state_space_phase(nc, x, w_in, w_out, conv_w, conv_b, a_log, d_skip, dt_bias, ln1, h_scratch)
    mlp_phase(nc, x, ln2, gate, up, down, lora_a, lora_b, w_ffn, ffn_bias, lora_coef, h_scratch, out)


def split_passes(hi_l, lo_l, hi_r, lo_r):
    return [(hi_l, hi_r), (hi_l, lo_r), (lo_l, hi_r)]


def state_space_phase(nc, x, w_in, w_out, conv_w, conv_b, a_log, d_skip, dt_bias, ln1, h_scratch):
    with ExitStack() as ctx:
        def sb(name, shape, dt=F32):
            return ctx.enter_context(nc.sbuf_tensor(name, shape, dt))

        def psum(name):
            return ctx.enter_context(nc.psum_tensor(name, [P, 512], F32))

        def sig(name, per, seeded=True):
            return Signal(nc, ctx, name, per, seeded)

        NW = D_PROJ - HEADS
        wi_hi, wi_lo = sb("wi_hi", [P, KD, NW], F32R), sb("wi_lo", [P, KD, NW], F32R)
        wdt = sb("wdt", [P, KD, 2 * HEADS], F32R)
        wo_hi, wo_lo = sb("wo_hi", [P, HEADS, D_MODEL], F32R), sb("wo_lo", [P, HEADS, D_MODEL], F32R)
        xin = sb("xin", [P, TILES, D_MODEL])
        zt_hi, zt_lo = sb("zt_hi", [P, KD, BT], F32R), sb("zt_lo", [P, KD, BT], F32R)
        raw = sb("raw", [P, CONV, BATCH, TAPS - 1 + CW])
        CX = CONV * BT
        cx = sb("cx", [P, 2 * CX])
        ZS = HEADS * BT
        zs = sb("zs", [P, 2 * ZS])
        xr = sb("xr", [P, TILES, D_MODEL])
        xb32 = sb("xb32", [P, 2, P])
        b_hi, b_lo = sb("b_hi", [P, P], F32R), sb("b_lo", [P, P], F32R)
        xb_hi, xb_lo = sb("xb_hi", [P, 2, 2, P], F32R), sb("xb_lo", [P, 2, 2, P], F32R)
        c_hi, c_lo = sb("c_hi", [P, HEADS, P], F32R), sb("c_lo", [P, HEADS, P], F32R)
        r_hi, r_lo = sb("r_hi", [P, HEADS, P], F32R), sb("r_lo", [P, HEADS, P], F32R)
        dec = sb("dec", [P, HEADS, P])
        ecs = sb("ecs", [P, HEADS, P])
        mdt = sb("mdt", [P, HEADS, P])
        att32 = sb("att32", [P, HEADS, P])
        att_hi, att_lo = sb("att_hi", [P, 2, HEADS, P], F32R), sb("att_lo", [P, 2, HEADS, P], F32R)
        cp32 = sb("cp32", [P, HEADS, P])
        cp_hi, cp_lo = sb("cp_hi", [P, 2, HEADS, P], F32R), sb("cp_lo", [P, 2, HEADS, P], F32R)
        xs32 = sb("xs32", [P, HEADS, P])
        xs_hi, xs_lo = sb("xs_hi", [P, HEADS, P], F32R), sb("xs_lo", [P, HEADS, P], F32R)
        state = sb("state", [P, BATCH, HEADS, P])
        s_hi, s_lo = sb("s_hi", [P, 2, HEADS, P], F32R), sb("s_lo", [P, 2, HEADS, P], F32R)
        y32 = sb("y32", [P, HEADS, P])
        y_hi, y_lo = sb("y_hi", [P, HEADS, P], F32R), sb("y_lo", [P, HEADS, P], F32R)
        ident, upper = sb("ident", [P, P]), sb("upper", [P, P])
        after_f, ones_f = xb32[:, 0, :], xb32[:, 1, :]
        after, ones = sb("after", [P, P], F32R), sb("ones", [P, P], F32R)
        ln1_sb, cw_sb, cb_sb = sb("ln1_sb", [P, KD]), sb("cw_sb", [P, CONV, TAPS]), sb("cb_sb", [P, CONV])
        head_sb = sb("head_sb", [P, 3, HEADS])
        neg_a = sb("neg_a", [P, HEADS])
        mhalf = sb("mhalf", [P, TILES])
        bn = sb("bn", [P, TILES, 6])
        mv = sb("mv", [P, TILES, 2])
        lt = sb("lt", [P, 6, TILES])
        lz = sb("lz", [P, 2, TILES])
        lnk = sb("lnk", [P, BLOCKS * 2 * TILES])
        DH = TILES * HEADS
        dtraw = sb("dtraw", [P, TILES, 2 * HEADS])
        dtt = sb("dtt", [P, 8, DH])
        dtv, a_hi, a_lo = sb("dtv", [P, DH]), sb("a_hi", [P, DH], F32R), sb("a_lo", [P, DH])
        wd = sb("wd", [P, HEADS])

        p_in = [psum("p_in0"), psum("p_in1")]
        p_tr, p_d, p_s, p_y, p_st, p_o = (psum(n) for n in ("p_tr", "p_d", "p_s", "p_y", "p_st", "p_o"))

        ln1_in, par_in, wout_in = (sig(n, 1, False) for n in ("ln1_in", "par_in", "wout_in"))
        win_in = [sig(f"win_in{k}", 1, False) for k in range(KD)]
        x_in = sig("x_in", 32, False)
        xr_in = [sig(f"xr_in{u}", 16, False) for u in range(TILES)]
        h_out = sig("h_out", 16 * TILES, False)
        consts = sig("consts", 1, False)
        mask_made = sig("mask_made", 1, False)
        zeroed, win_scaled, wi_hi_made, wi_lo_made, wi_lo_pool, wo_hi_made, wo_lo_made, neg_a_made = (
            sig(n, 1, False) for n in ("zeroed", "win_scaled", "wi_hi_made", "wi_lo_made", "wi_lo_pool", "wo_hi_made",
                                       "wo_lo_made", "neg_a_made"))
        dve = {n: sig(n, per) for n, per in dict(
            bn_made=TILES, mean_var=TILES, normed=TILES, zt_lo_made=TILES, tap=4 * CONV, hist=1,
            dt_abs=1, dt_step=14, dt_tail=4, dt_ready=1, xb_copied=4, xb_lo_made=4, wd_made=4, xs_made=4,
            t1=4, t2=4, att_made=4, s_lo_made=4, s_updated=4, y_gated=4, y_lo_made=4, xhat=4, h_made=4).items()}
        act = {n: sig(n, per) for n, per in dict(
            zt_hi_made=TILES, in_out=NG, silu_made=CONV, dt_exp=1, dec_made=4, ecs_made=4, c_hi_made=4, b_hi_made=4,
            xb_hi_made=4, att_hi_made=4, cp_hi_made=4, xs_hi_made=4, s_hi_made=4, y_hi_made=4).items()}
        pool = {n: sig(n, per) for n, per in dict(
            ln_step=11, ln_scale=1, r_made=4, mdt_made=4, c_lo_made=4, b_lo_made=4, att_lo_made=4, cp_made=4,
            cp_lo_made=4, xs_lo_made=4, s_decayed=4).items()}
        pe = {n: sig(n, per) for n, per in dict(
            zt_ps=TILES, in_ps=NG, d_ps=4, cs_ps=4, tr_ps=4, sc_ps=4, y_ps=4, st_ps=4, o_ps=4).items()}
        s = {**dve, **act, **pool, **pe}

        passed_pool, passed_vector = (ctx.enter_context(nc.semaphore(n)) for n in ("passed_pool", "passed_vector"))

        block = ctx.enter_context(nc.Block())

        def cxs(i, first, count):
            return cx[:, bass.ds((i % 2) * CX + first, count)]

        def c_of(i, u):
            return cxs(i, 2 * BT, HEADS * BT).rearrange("p (h t) -> p h t", h=HEADS)[:, :, u * P:(u + 1) * P]

        def z_of(i, u):
            v = zs[:, bass.ds((i % 2) * ZS, ZS)]
            return v.rearrange("p (h t) -> p h t", h=HEADS)[:, :, u * P:(u + 1) * P]

        def per_head(v):
            return v.rearrange("p (h o) -> p h o", o=1).broadcast_to([P, HEADS, P])

        def over_heads(v):
            return v.rearrange("p (o q) -> p o q", o=1).broadcast_to([P, HEADS, P])

        def flat(v):
            return v.rearrange("p h q -> p (h q)")

        x_blocks = x.rearrange("(b i c p) d -> b i p c d", b=BATCH, i=BLOCKS, c=CPB)

        @block.sync
        def _(sp):
            def load_x(i):
                for b in range(BATCH):
                    src = x_blocks[b, bass.ds(i, 1)].rearrange("o p c d -> (o p) c d")
                    sp.dma_start(xin[:, b * CPB:(b + 1) * CPB, :], src).then_inc(x_in.sem, 16)

            def load_xr(i, u):
                src = x_blocks[u // CPB, bass.ds(i, 1)].rearrange("o p c d -> (o p) c d")[:, u % CPB, :]
                sp.dma_start(xr[:, u, :], src).then_inc(xr_in[u].sem, 16)

            def store_h(i, q):
                u = ORDER[q]
                sp.wait_ge(s["h_made"].sem, s["h_made"].at(i, q + 1))
                sp.dma_start(h_scratch[bass.ds(i * TILES + u, 1)].rearrange("o p d -> (o p) d"), xr[:, u, :])\
                    .then_inc(h_out.sem, 16)

            def store_and_load(i, q):
                store_h(i, q)
                sp.wait_ge(h_out.sem, h_out.at(i, 16 * (q + 1)))
                load_xr(i + 1, ORDER[q])

            load_x(0)
            sp.dma_start(ln1_sb[:], ln1).then_inc(ln1_in.sem, 16)
            for k in range(KD):
                sp.dma_start(cx[:, k * D_PROJ:(k + 1) * D_PROJ], w_in[k * P:(k + 1) * P, :]).then_inc(win_in[k].sem, 16)
            sp.dma_start(cw_sb[:], conv_w).then_inc(par_in.sem, 16)
            sp.dma_start(cb_sb[:], conv_b).then_inc(par_in.sem, 16)
            for n, src in enumerate((a_log, d_skip, dt_bias)):
                sp.dma_start(head_sb[:, n, :], src).then_inc(par_in.sem, 16)
            sp.dma_start(zs[:, ZS:ZS + HEADS * D_MODEL].rearrange("p (h n) -> p h n", h=HEADS),
                         w_out.rearrange("(h p) n -> p h n", p=P)).then_inc(wout_in.sem, 16)
            for u in range(TILES):
                load_xr(0, u)

            def body(i, first, more):
                if more:
                    sp.wait_ge(s["zt_ps"].sem, s["zt_ps"].at(i))
                    load_x(i + 1)
                if not first:
                    for q in range(1, TILES):
                        store_and_load(i - 1, q)
                if more:
                    store_and_load(i, 0)
                else:
                    store_h(i, 0)

            body(0, True, True)
            with nc.sync.Fori(1, BLOCKS - 1) as i:
                body(i, False, True)
            body(BLOCKS - 1, False, False)
            for q in range(1, TILES):
                store_h(BLOCKS - 1, q)
            sp.wait_ge(h_out.sem, h_out.at(BLOCKS - 1))

        @block.tensor
        def _(t):
            for v in pe.values():
                v.seed(t)

            def turn(j):
                for u in range(TILES):
                    t.wait_ge(s["normed"].sem, s["normed"].at(j, u + 1))
                    if u == 0:
                        t.wait_ge(s["in_out"].sem, s["in_out"].at(j - 1))
                    if u >= 2:
                        t.wait_ge(s["zt_lo_made"].sem, s["zt_lo_made"].at(j, u - 1))
                    for k in range(KD):
                        ins = nc.tensor.transpose(p_in[u % 2][:, k * P:(k + 1) * P], xin[:, u, k * P:(k + 1) * P], ident[:, :])
                    ins.then_inc(s["zt_ps"].sem, 1)

            def project(j, groups):
                for g in groups:
                    kind, col, _ = IN_GROUPS[g]
                    if g == 0:
                        t.wait_ge(s["zt_lo_made"].sem, s["zt_lo_made"].at(j))
                    t.wait_ge(s["in_out"].sem, s["in_out"].at(j, max(g - 1, 0)))
                    bank = p_in[g % 2]
                    if kind == "dt":
                        for u in range(TILES):
                            n = 0
                            for w in (zt_hi, zt_lo):
                                for k in range(KD):
                                    ins = nc.tensor.matmul(bank[:, u * 2 * HEADS:(u + 1) * 2 * HEADS],
                                                           w[:, k, u * P:(u + 1) * P], wdt[:, k, :],
                                                           start=(n == 0), stop=(n == 2 * KD - 1))
                                    n += 1
                    else:
                        n = 0
                        for k in range(KD):
                            for l, r in split_passes(wi_hi, wi_lo, zt_hi, zt_lo):
                                ins = nc.tensor.matmul(bank[:, :], l[:, k, col:col + P], r[:, k, :],
                                                       start=(n == 0), stop=(n == 3 * KD - 1))
                                n += 1
                    ins.then_inc(s["in_ps"].sem, 1)

            def front(i, q):
                t.wait_ge(s["r_made"].sem, s["r_made"].at(i, q + 1))
                t.wait_ge(s["ecs_made"].sem, s["ecs_made"].at(i, q))
                nc.tensor.matmul(p_d[:, :], after[:, :], flat(r_hi[:, :, :]), start=True, stop=False)
                nc.tensor.matmul(p_d[:, :], after[:, :], flat(r_lo[:, :, :]), start=False, stop=True).then_inc(s["d_ps"].sem, 1)
                t.wait_ge(s["xb_copied"].sem, s["xb_copied"].at(i, q + 1))
                t.wait_ge(s["xs_made"].sem, s["xs_made"].at(i, q))
                for n in range(2):
                    ins = nc.tensor.transpose(p_tr[:, n * P:(n + 1) * P], xb32[:, n, :], ident[:, :])
                ins.then_inc(s["tr_ps"].sem, 1)
                t.wait_ge(s["c_hi_made"].sem, s["c_hi_made"].at(i, q + 1))
                t.wait_ge(s["c_lo_made"].sem, s["c_lo_made"].at(i, q + 1))
                t.wait_ge(s["b_hi_made"].sem, s["b_hi_made"].at(i, q + 1))
                t.wait_ge(s["b_lo_made"].sem, s["b_lo_made"].at(i, q + 1))
                t.wait_ge(s["t2"].sem, s["t2"].at(i, q))
                for n, (l, r) in enumerate(split_passes(b_hi, b_lo, c_hi, c_lo)):
                    ins = nc.tensor.matmul(p_s[:, :], l[:, :], flat(r[:, :, :]), start=(n == 0), stop=(n == 2))
                ins.then_inc(s["sc_ps"].sem, 1)
                t.wait_ge(s["dec_made"].sem, s["dec_made"].at(i, q + 1))
                nc.tensor.matmul(p_d[:, :], ones[:, :], flat(r_hi[:, :, :]), start=True, stop=False)
                nc.tensor.matmul(p_d[:, :], ones[:, :], flat(r_lo[:, :, :]), start=False, stop=True).then_inc(s["cs_ps"].sem, 1)

            def back(i, q):
                t.wait_ge(s["xs_hi_made"].sem, s["xs_hi_made"].at(i, q + 1))
                t.wait_ge(s["xs_lo_made"].sem, s["xs_lo_made"].at(i, q + 1))
                t.wait_ge(s["s_updated"].sem, s["s_updated"].at(i, q))
                for n, (l, r) in enumerate(split_passes(xb_hi, xb_lo, xs_hi, xs_lo)):
                    ins = nc.tensor.matmul(p_st[:, :], l[:, q % 2, 1, :], flat(r[:, :, :]), start=(n == 0), stop=(n == 2))
                ins.then_inc(s["st_ps"].sem, 1)
                t.wait_ge(s["att_hi_made"].sem, s["att_hi_made"].at(i, q + 1))
                t.wait_ge(s["att_lo_made"].sem, s["att_lo_made"].at(i, q + 1))
                t.wait_ge(s["y_gated"].sem, s["y_gated"].at(i, q))
                for n, (l, r) in enumerate(split_passes(xb_hi, xb_lo, att_hi, att_lo)):
                    nc.tensor.matmul(p_y[:, :], l[:, q % 2, 0, :], flat(r[:, q % 2, :, :]), start=(n == 0), stop=False,
                                     skip_group_check=True)
                t.wait_ge(s["cp_hi_made"].sem, s["cp_hi_made"].at(i, q + 1))
                t.wait_ge(s["cp_lo_made"].sem, s["cp_lo_made"].at(i, q + 1))
                t.wait_ge(s["s_hi_made"].sem, s["s_hi_made"].at(i, q + 1))
                t.wait_ge(s["s_lo_made"].sem, s["s_lo_made"].at(i, q + 1))
                for h in range(HEADS):
                    for n, (l, r) in enumerate(split_passes(s_hi, s_lo, cp_hi, cp_lo)):
                        ins = nc.tensor.matmul(p_y[:, h * P:(h + 1) * P], l[:, q % 2, h, :], r[:, q % 2, h, :], start=False,
                                               stop=(h == HEADS - 1 and n == 2), skip_group_check=True)
                ins.then_inc(s["y_ps"].sem, 1)

            def output(i, q):
                t.wait_ge(wo_lo_made.sem, wo_lo_made.at(0, 1))
                t.wait_ge(s["y_hi_made"].sem, s["y_hi_made"].at(i, q + 1))
                t.wait_ge(s["y_lo_made"].sem, s["y_lo_made"].at(i, q + 1))
                t.wait_ge(s["h_made"].sem, s["h_made"].at(i, q))
                n = 0
                for h in range(HEADS):
                    for l, r in split_passes(y_hi, y_lo, wo_hi, wo_lo):
                        ins = nc.tensor.matmul(p_o[:, :], l[:, h, :], r[:, h, :], start=(n == 0), stop=(n == 3 * HEADS - 1))
                        n += 1
                ins.then_inc(s["o_ps"].sem, 1)

            def step(i, q, extra=None, before=2):
                front(i, q)
                if before:
                    back(i, q - 1)
                if extra:
                    extra()
                if before:
                    output(i, q - 1)

            def turn_and_project(j, groups):
                turn(j)
                project(j, groups)

            def body(i, first, more):
                if not first:
                    step(i - 1, 3, lambda: project(i, IN_AT[3]))
                step(i, 0, lambda: project(i, IN_AT[0]), 0 if first else 2)
                step(i, 1, (lambda: turn_and_project(i + 1, IN_AT[1])) if more else None)
                step(i, 2, (lambda: project(i + 1, IN_AT[2])) if more else None)

            t.wait_ge(consts.sem, consts.at(0, 5))
            turn(0)
            t.wait_ge(wi_lo_made.sem, wi_lo_made.at(0, KD))
            t.wait_ge(wi_lo_pool.sem, wi_lo_pool.at(0, 2))
            project(0, IN_AT[1] + IN_AT[2] + IN_AT[3])
            body(0, True, True)
            with nc.tensor.Fori(1, BLOCKS - 1) as i:
                body(i, False, True)
            body(BLOCKS - 1, False, False)
            step(BLOCKS - 1, 3)
            back(BLOCKS - 1, 3)
            output(BLOCKS - 1, 3)

        @block.scalar
        def _(a):
            for v in act.values():
                v.seed(a)

            def turn(j):
                for u in range(TILES):
                    a.wait_ge(s["zt_ps"].sem, s["zt_ps"].at(j, u + 1))
                    if u == 0:
                        a.wait_ge(s["in_ps"].sem, s["in_ps"].at(j - 1))
                    nc.scalar.copy(zt_hi[:, :, u * P:(u + 1) * P],
                                   p_in[u % 2][:, :].rearrange("p (k t) -> p k t", k=KD)).then_inc(s["zt_hi_made"].sem, 1)

            def evacuate(j, groups):
                for g in groups:
                    kind, _, n = IN_GROUPS[g]
                    a.wait_ge(s["in_ps"].sem, s["in_ps"].at(j, g + 1))
                    if kind == "dt":
                        a.wait_ge(s["dt_abs"].sem, s["dt_abs"].at(j - 1))
                        ins = nc.scalar.copy(dtraw[:, :, :].rearrange("p u e -> p (u e)"), p_in[g % 2][:, 0:TILES * 2 * HEADS])
                    elif kind == "conv":
                        a.wait_ge(s["hist"].sem, s["hist"].at(j - 1))
                        ins = nc.scalar.copy(raw[:, n, :, TAPS - 1:], p_in[g % 2][:, :].rearrange("p (b t) -> p b t", b=BATCH))
                    else:
                        ins = nc.scalar.activation(zs[:, bass.ds((j % 2) * ZS + n * BT, BT)], p_in[g % 2][:, :], ACT.Silu)
                    ins.then_inc(s["in_out"].sem, 1)

            def dt_exp(j):
                a.wait_ge(s["dt_abs"].sem, s["dt_abs"].at(j))
                nc.scalar.activation(dtt[:, 2, :], dtt[:, 1, :], ACT.Exp, scale=-1.0).then_inc(s["dt_exp"].sem, 1)

            def silu(j, first, count):
                a.wait_ge(s["tap"].sem, s["tap"].at(j, TAPS * (first + count)))
                part = cxs(j, first * BT, count * BT)
                nc.scalar.activation(part, part, ACT.Silu).then_inc(s["silu_made"].sem, count)

            def prepare(i, q):
                a.wait_ge(s["sc_ps"].sem, s["sc_ps"].at(i, q))
                a.wait_ge(s["xb_copied"].sem, s["xb_copied"].at(i, q + 1))
                nc.scalar.copy(b_hi[:, :], xb32[:, 1, :]).then_inc(s["b_hi_made"].sem, 1)
                nc.scalar.copy(c_hi[:, :, :], c_of(i, ORDER[q])).then_inc(s["c_hi_made"].sem, 1)

            def front(i, q):
                b = ORDER[q] // CPB
                a.wait_ge(s["y_ps"].sem, s["y_ps"].at(i, q - 1))
                a.wait_ge(s["s_updated"].sem, s["s_updated"].at(i, q - 1))
                nc.scalar.copy(flat(s_hi[:, q % 2, :, :]), flat(state[:, b, :, :])).then_inc(s["s_hi_made"].sem, 1)
                a.wait_ge(s["d_ps"].sem, s["d_ps"].at(i, q + 1))
                a.wait_ge(s["t1"].sem, s["t1"].at(i, q))
                nc.scalar.activation(flat(dec[:, :, :]), p_d[:, :], ACT.Exp).then_inc(s["dec_made"].sem, 1)
                a.wait_ge(s["tr_ps"].sem, s["tr_ps"].at(i, q + 1))
                nc.scalar.copy(xb_hi[:, q % 2, :, :].rearrange("p n t -> p (n t)"), p_tr[:, 0:2 * P]).then_inc(s["xb_hi_made"].sem, 1)
                a.wait_ge(s["cs_ps"].sem, s["cs_ps"].at(i, q + 1))
                a.wait_ge(s["s_decayed"].sem, s["s_decayed"].at(i, q))
                nc.scalar.activation(flat(ecs[:, :, :]), p_d[:, :], ACT.Exp).then_inc(s["ecs_made"].sem, 1)

            def halves(i, q):
                a.wait_ge(s["xs_made"].sem, s["xs_made"].at(i, q + 1))
                a.wait_ge(s["st_ps"].sem, s["st_ps"].at(i, q))
                nc.scalar.copy(flat(xs_hi[:, :, :]), flat(xs32[:, :, :])).then_inc(s["xs_hi_made"].sem, 1)
                a.wait_ge(s["cp_made"].sem, s["cp_made"].at(i, q + 1))
                nc.scalar.copy(flat(cp_hi[:, q % 2, :, :]), flat(cp32[:, :, :])).then_inc(s["cp_hi_made"].sem, 1)
                a.wait_ge(s["att_made"].sem, s["att_made"].at(i, q + 1))
                nc.scalar.copy(flat(att_hi[:, q % 2, :, :]), flat(att32[:, :, :])).then_inc(s["att_hi_made"].sem, 1)

            def back(i, q):
                a.wait_ge(s["y_gated"].sem, s["y_gated"].at(i, q + 1))
                a.wait_ge(s["o_ps"].sem, s["o_ps"].at(i, q))
                nc.scalar.copy(flat(y_hi[:, :, :]), flat(y32[:, :, :])).then_inc(s["y_hi_made"].sem, 1)

            def body(i, first, more):
                if not first:
                    front(i - 1, 3)
                    halves(i - 1, 3)
                    back(i - 1, 2)
                    evacuate(i, IN_AT[3])
                    silu(i, 0, 4)
                    silu(i, 4, 2)
                    prepare(i, 0)
                front(i, 0)
                halves(i, 0)
                evacuate(i, IN_AT[0][:1])
                if not first:
                    back(i, -1)
                prepare(i, 1)
                evacuate(i, IN_AT[0][1:])
                front(i, 1)
                halves(i, 1)
                if more:
                    turn(i + 1)
                back(i, 0)
                prepare(i, 2)
                if more:
                    evacuate(i + 1, IN_AT[1])
                front(i, 2)
                if more:
                    dt_exp(i + 1)
                halves(i, 2)
                if more:
                    evacuate(i + 1, IN_AT[2][:1])
                back(i, 1)
                prepare(i, 3)
                if more:
                    evacuate(i + 1, IN_AT[2][1:])

            wv = cx[:, 0:KD * D_PROJ].rearrange("p (k n) -> p k n", k=KD)

            def split_w(k):
                a.wait_ge(win_scaled.sem, win_scaled.at(0, k + 1))
                nc.scalar.copy(wi_hi[:, k, :], wv[:, k, 0:NW])
                nc.scalar.copy(wdt[:, k, 0:HEADS], wv[:, k, NW:D_PROJ]).then_inc(wi_hi_made.sem, 1)

            for k in range(KD):
                split_w(k)
            turn(0)
            a.wait_ge(par_in.sem, par_in.at(0, 5 * 16))
            nc.scalar.activation(neg_a[:, :], head_sb[:, 0, :], ACT.Exp).then_inc(neg_a_made.sem, 1)
            evacuate(0, IN_AT[1][:1])
            dt_exp(0)
            evacuate(0, IN_AT[1][1:])
            evacuate(0, IN_AT[2])
            a.wait_ge(wout_in.sem, wout_in.at(0, 16))
            nc.scalar.copy(flat(wo_hi[:, :, :]), zs[:, ZS:ZS + HEADS * D_MODEL]).then_inc(wo_hi_made.sem, 1)
            evacuate(0, IN_AT[3])
            silu(0, 0, 4)
            silu(0, 4, 2)
            prepare(0, 0)
            body(0, True, True)
            with nc.scalar.Fori(1, BLOCKS - 1) as i:
                body(i, False, True)
            body(BLOCKS - 1, False, False)
            last = BLOCKS - 1
            front(last, 3)
            halves(last, 3)
            back(last, 2)
            back(last, 3)

        @block.gpsimd
        def _(g):
            for v in pool.values():
                v.seed(g)
            nc.gpsimd.memset(ident[:, :], 0.0).then_inc(mask_made.sem, 1)
            nc.gpsimd.memset(upper[:, :], 1.0).then_inc(mask_made.sem, 1)
            nc.gpsimd.memset(after_f, 1.0).then_inc(mask_made.sem, 1)
            nc.gpsimd.memset(ones_f, 1.0).then_inc(mask_made.sem, 1)
            nc.gpsimd.memset(mhalf[:, :], -0.5).then_inc(consts.sem, 1)
            g.wait_ge(mask_made.sem, mask_made.at(0, 4))
            nc.gpsimd.affine_select(out=ident[:, :], in_=ident[:, :], compare_op=ALU.not_equal, fill=1.0, base=0,
                                    pattern=[[-1, P]], channel_multiplier=1).then_inc(consts.sem, 1)
            nc.gpsimd.affine_select(out=upper[:, :], in_=upper[:, :], compare_op=ALU.is_ge, fill=0.0, base=0,
                                    pattern=[[1, P]], channel_multiplier=-1).then_inc(consts.sem, 1)
            nc.gpsimd.affine_select(out=after_f, in_=after_f, compare_op=ALU.is_gt, fill=0.0, base=0,
                                    pattern=[[-1, P]], channel_multiplier=1).then_inc(mask_made.sem, 1)
            g.wait_ge(mask_made.sem, mask_made.at(0, 5))
            nc.gpsimd.tensor_copy(after[:, :], after_f).then_inc(consts.sem, 1)
            nc.gpsimd.tensor_copy(ones[:, :], ones_f).then_inc(consts.sem, 1)

            def norm_scales(j):
                g.wait_ge(s["mean_var"].sem, s["mean_var"].at(j))
                g.wait_ge(s["normed"].sem, s["normed"].at(j - 1))
                waits_apart(g, passed_pool)
                mean, var = mv[:, :, 0], mv[:, :, 1]
                ve, rstd, t1, t2, t3, r1 = (lt[:, n, :] for n in range(6))
                keep = lnk[:, bass.ds(j * 2 * TILES, 2 * TILES)]
                step = [0]

                def chain(ins):
                    step[0] += 1
                    ins.then_inc(s["ln_step"].sem, 1)
                    g.wait_ge(s["ln_step"].sem, s["ln_step"].at(j, step[0]))
                    waits_apart(g, passed_pool)

                chain(nc.gpsimd.tensor_scalar(ve, var, EPS, 1.0, ALU.add, ALU.mult))
                chain(nc.gpsimd.tensor_tensor(rstd, ve, mhalf[:, :], ALU.pow))
                chain(nc.gpsimd.tensor_tensor(t1, var, rstd, ALU.mult))
                chain(nc.gpsimd.tensor_tensor(t2, t1, rstd, ALU.mult))
                chain(nc.gpsimd.tensor_scalar(t3, t2, EPS, 1.0, ALU.add, ALU.mult))
                chain(nc.gpsimd.tensor_tensor(r1, t3, mhalf[:, :], ALU.pow))
                chain(nc.gpsimd.tensor_tensor(t1, mean, rstd, ALU.mult))
                chain(nc.gpsimd.tensor_scalar(t2, t1, -1.0, 1.0, ALU.mult, ALU.mult))
                chain(nc.gpsimd.tensor_tensor(lz[:, 0, :], rstd, r1, ALU.mult))
                chain(nc.gpsimd.tensor_tensor(lz[:, 1, :], t2, r1, ALU.mult))
                chain(nc.gpsimd.tensor_copy(keep[:, 0:TILES], rstd))
                nc.gpsimd.tensor_copy(keep[:, TILES:2 * TILES], t2).then_inc(s["ln_scale"].sem, 1)

            def prepare(i, q):
                u = ORDER[q]
                hs = slice(u * HEADS, (u + 1) * HEADS)
                if q == 0:
                    g.wait_ge(s["dt_ready"].sem, s["dt_ready"].at(i))
                g.wait_ge(s["cs_ps"].sem, s["cs_ps"].at(i, q))
                nc.gpsimd.tensor_tensor(r_hi[:, :, :], over_heads(upper[:, :]), per_head(a_hi[:, hs].bitcast(F32)), ALU.mult)
                nc.gpsimd.tensor_tensor(r_lo[:, :, :], over_heads(upper[:, :]), per_head(a_lo[:, hs]), ALU.mult)\
                    .then_inc(s["r_made"].sem, 1)
                g.wait_ge(s["t1"].sem, s["t1"].at(i, q))
                nc.gpsimd.tensor_tensor(mdt[:, :, :], over_heads(upper[:, :]), per_head(dtv[:, hs]), ALU.mult)\
                    .then_inc(s["mdt_made"].sem, 1)
                g.wait_ge(s["b_hi_made"].sem, s["b_hi_made"].at(i, q + 1))
                nc.gpsimd.tensor_tensor(b_lo[:, :], xb32[:, 1, :], b_hi[:, :].bitcast(F32), ALU.subtract)\
                    .then_inc(s["b_lo_made"].sem, 1)
                g.wait_ge(s["c_hi_made"].sem, s["c_hi_made"].at(i, q + 1))
                waits_apart(g, passed_pool)
                nc.gpsimd.tensor_tensor(c_lo[:, :, :], c_of(i, u), c_hi[:, :, :].bitcast(F32), ALU.subtract)\
                    .then_inc(s["c_lo_made"].sem, 1)

            def front(i, q):
                u = ORDER[q]
                g.wait_ge(s["ecs_made"].sem, s["ecs_made"].at(i, q + 1))
                g.wait_ge(s["cp_hi_made"].sem, s["cp_hi_made"].at(i, q))
                waits_apart(g, passed_pool)
                nc.gpsimd.tensor_tensor(cp32[:, :, :], c_of(i, u), ecs[:, :, :], ALU.mult).then_inc(s["cp_made"].sem, 1)
                g.wait_ge(s["xs_hi_made"].sem, s["xs_hi_made"].at(i, q + 1))
                nc.gpsimd.tensor_tensor(flat(xs_lo[:, :, :]), flat(xs32[:, :, :]), flat(xs_hi[:, :, :].bitcast(F32)),
                                        ALU.subtract).then_inc(s["xs_lo_made"].sem, 1)
                g.wait_ge(s["cp_hi_made"].sem, s["cp_hi_made"].at(i, q + 1))
                nc.gpsimd.tensor_tensor(flat(cp_lo[:, q % 2, :, :]), flat(cp32[:, :, :]),
                                        flat(cp_hi[:, q % 2, :, :].bitcast(F32)), ALU.subtract).then_inc(s["cp_lo_made"].sem, 1)
                g.wait_ge(s["att_hi_made"].sem, s["att_hi_made"].at(i, q + 1))
                nc.gpsimd.tensor_tensor(flat(att_lo[:, q % 2, :, :]), flat(att32[:, :, :]),
                                        flat(att_hi[:, q % 2, :, :].bitcast(F32)), ALU.subtract).then_inc(s["att_lo_made"].sem, 1)
                g.wait_ge(s["s_lo_made"].sem, s["s_lo_made"].at(i, q + 1))
                decay = ecs[:, :, P - 1:P].broadcast_to([P, HEADS, P])
                nc.gpsimd.tensor_tensor(state[:, u // CPB, :, :], state[:, u // CPB, :, :], decay, ALU.mult)\
                    .then_inc(s["s_decayed"].sem, 1)

            def body(i, first, more):
                if not first:
                    front(i - 1, 3)
                    prepare(i, 0)
                    if more:
                        norm_scales(i + 1)
                front(i, 0)
                prepare(i, 1)
                if first:
                    norm_scales(i + 1)
                front(i, 1)
                prepare(i, 2)
                front(i, 2)
                prepare(i, 3)

            g.wait_ge(consts.sem, consts.at(0, 5))
            norm_scales(0)
            wv = cx[:, 0:KD * D_PROJ].rearrange("p (k n) -> p k n", k=KD)
            for k in range(1, KD, 2):
                g.wait_ge(wi_hi_made.sem, wi_hi_made.at(0, k + 1))
                nc.gpsimd.tensor_tensor(wi_lo[:, k, :], wv[:, k, 0:NW], wi_hi[:, k, :].bitcast(F32), ALU.subtract)\
                    .then_inc(wi_lo_pool.sem, 1)
            g.wait_ge(wo_hi_made.sem, wo_hi_made.at(0, 1))
            nc.gpsimd.tensor_tensor(flat(wo_lo[:, :, :]), zs[:, ZS:ZS + HEADS * D_MODEL], flat(wo_hi[:, :, :].bitcast(F32)),
                                    ALU.subtract).then_inc(wo_lo_made.sem, 1)
            prepare(0, 0)
            body(0, True, True)
            with nc.gpsimd.Fori(1, BLOCKS - 1) as i:
                body(i, False, True)
            body(BLOCKS - 1, False, False)
            front(BLOCKS - 1, 3)

        @block.vector
        def _(v):
            for e in dve.values():
                e.seed(v)

            def stats(j):
                v.wait_ge(x_in.sem, x_in.at(j))
                v.wait_ge(s["ln_scale"].sem, s["ln_scale"].at(j - 1))
                for u in range(TILES):
                    nc.vector.bn_stats(bn[:, u, :], xin[:, u, :]).then_inc(s["bn_made"].sem, 1)
                for u in range(TILES):
                    v.wait_ge(s["bn_made"].sem, s["bn_made"].at(j, u + 1))
                    waits_apart(v, passed_vector)
                    nc.vector.bn_aggr(mv[:, u, :], bn[:, u, :]).then_inc(s["mean_var"].sem, 1)

            def normalise(j):
                v.wait_ge(s["ln_scale"].sem, s["ln_scale"].at(j))
                for u in range(TILES):
                    nc.vector.tensor_scalar(xin[:, u, :], xin[:, u, :], lz[:, 0, u:u + 1], lz[:, 1, u:u + 1],
                                            ALU.mult, ALU.add).then_inc(s["normed"].sem, 1)

            def turn(j):
                for u in range(TILES):
                    v.wait_ge(s["zt_hi_made"].sem, s["zt_hi_made"].at(j, u + 1))
                    cols = slice(u * P, (u + 1) * P)
                    nc.vector.tensor_tensor(zt_lo[:, :, cols], p_in[u % 2][:, :].rearrange("p (k t) -> p k t", k=KD),
                                            zt_hi[:, :, cols].bitcast(F32), ALU.subtract).then_inc(s["zt_lo_made"].sem, 1)

            def convolve(j, groups):
                for g in groups:
                    n = IN_GROUPS[g][2]
                    acc = cxs(j, n * BT, BT).rearrange("p (b t) -> p b t", b=BATCH)
                    v.wait_ge(s["in_out"].sem, s["in_out"].at(j, g + 1))
                    if g == 1:
                        v.wait_ge(s["cp_made"].sem, s["cp_made"].at(j - 2))
                    waits_apart(v, passed_vector)
                    nc.vector.tensor_scalar(acc, raw[:, n, :, 0:CW], cw_sb[:, n, 0:1], cb_sb[:, n:n + 1],
                                            ALU.mult, ALU.add).then_inc(s["tap"].sem, 1)
                    for k in range(1, TAPS):
                        v.wait_ge(s["tap"].sem, s["tap"].at(j, (g - 1) * TAPS + k))
                        waits_apart(v, passed_vector)
                        nc.vector.scalar_tensor_tensor(out=acc, in0=raw[:, n, :, k:k + CW], scalar=cw_sb[:, n, k:k + 1],
                                                       in1=acc, op0=ALU.mult, op1=ALU.add).then_inc(s["tap"].sem, 1)

            def keep_history(j):
                v.wait_ge(s["tap"].sem, s["tap"].at(j))
                nc.vector.tensor_copy(raw[:, :, :, 0:TAPS - 1].rearrange("p n b t -> p (n b) t"),
                                      raw[:, :, :, CW:].rearrange("p n b t -> p (n b) t")).then_inc(s["hist"].sem, 1)

            xd, ax, ed, t3, t4, t5, t6, t7 = (dtt[:, n, :] for n in range(8))
            dt_tail = s["dt_tail"]

            def chain(j, n, ins):
                ins.then_inc(s["dt_step"].sem, 1)
                v.wait_ge(s["dt_step"].sem, s["dt_step"].at(j, n))

            def dt_start(j):
                v.wait_ge(s["in_out"].sem, s["in_out"].at(j, 1))
                x3 = xd.rearrange("p (u h) -> p u h", u=TILES)
                bias = head_sb[:, 2:3, :].broadcast_to([P, TILES, HEADS])
                chain(j, 1, nc.vector.tensor_tensor(x3, dtraw[:, :, 0:HEADS], dtraw[:, :, HEADS:], ALU.add))
                chain(j, 2, nc.vector.tensor_tensor(x3, x3, bias, ALU.add))
                nc.vector.scalar_tensor_tensor(out=ax, in0=xd, scalar=-1.0, in1=xd, op0=ALU.mult, op1=ALU.max)\
                    .then_inc(s["dt_abs"].sem, 1)

            def dt_finish(j):
                v.wait_ge(s["dt_exp"].sem, s["dt_exp"].at(j))
                chain(j, 3, nc.vector.tensor_scalar(t3, ed, 2.0, None, ALU.add))
                chain(j, 4, nc.vector.reciprocal(t4, t3))
                chain(j, 5, nc.vector.tensor_tensor(t5, ed, t4, ALU.mult))
                chain(j, 6, nc.vector.tensor_tensor(t6, t5, t5, ALU.mult))
                terms = [1.0 / (2 * k + 1) for k in range(1, 8)]
                nc.vector.tensor_scalar(t7, t6, terms[-1], None, ALU.mult).then_inc(s["dt_step"].sem, 1)
                n = 7
                for c in reversed(terms[:-1]):
                    v.wait_ge(s["dt_step"].sem, s["dt_step"].at(j, n))
                    nc.vector.scalar_tensor_tensor(out=t7, in0=t7, scalar=c, in1=t6, op0=ALU.add, op1=ALU.mult)\
                        .then_inc(s["dt_step"].sem, 1)
                    n += 1
                v.wait_ge(s["dt_step"].sem, s["dt_step"].at(j, n))
                nc.vector.scalar_tensor_tensor(out=t7, in0=t7, scalar=1.0, in1=t5, op0=ALU.add, op1=ALU.mult)\
                    .then_inc(s["dt_step"].sem, 1)
                v.wait_ge(s["dt_step"].sem, s["dt_step"].at(j, n + 1))
                assert n + 1 == s["dt_step"].per

            def dt_write(j):
                v.wait_ge(s["mdt_made"].sem, s["mdt_made"].at(j - 1))
                v.wait_ge(s["wd_made"].sem, s["wd_made"].at(j - 1))
                nc.vector.tensor_scalar(t3, xd, 0.0, None, ALU.max).then_inc(dt_tail.sem, 1)
                v.wait_ge(dt_tail.sem, dt_tail.at(j, 1))
                nc.vector.scalar_tensor_tensor(out=dtv[:, :], in0=t7, scalar=2.0, in1=t3, op0=ALU.mult, op1=ALU.add)\
                    .then_inc(dt_tail.sem, 1)
                v.wait_ge(dt_tail.sem, dt_tail.at(j, 2))
                nc.vector.scalar_tensor_tensor(
                    out=t4.rearrange("p (u h) -> p u h", u=TILES), in0=dtv[:, :].rearrange("p (u h) -> p u h", u=TILES),
                    scalar=-1.0, in1=neg_a[:, :].rearrange("p (o h) -> p o h", o=1).broadcast_to([P, TILES, HEADS]),
                    op0=ALU.mult, op1=ALU.mult).then_inc(dt_tail.sem, 1)
                v.wait_ge(dt_tail.sem, dt_tail.at(j, 3))
                nc.vector.tensor_copy(a_hi[:, :], t4).then_inc(dt_tail.sem, 1)
                v.wait_ge(dt_tail.sem, dt_tail.at(j, 4))
                nc.vector.tensor_tensor(a_lo[:, :], t4, a_hi[:, :].bitcast(F32), ALU.subtract).then_inc(s["dt_ready"].sem, 1)

            def prepare(i, q):
                u = ORDER[q]
                if q == 0:
                    v.wait_ge(s["silu_made"].sem, s["silu_made"].at(i))
                v.wait_ge(s["tr_ps"].sem, s["tr_ps"].at(i, q))
                v.wait_ge(s["b_lo_made"].sem, s["b_lo_made"].at(i, q))
                waits_apart(v, passed_vector)
                nc.vector.tensor_copy(xb32[:, :, :], cxs(i, 0, 2 * BT).rearrange("p (n t) -> p n t", n=2)[:, :, u * P:(u + 1) * P])\
                    .then_inc(s["xb_copied"].sem, 1)

            def take_state(i, q):
                v.wait_ge(s["s_hi_made"].sem, s["s_hi_made"].at(i, q + 1))
                nc.vector.tensor_tensor(flat(s_lo[:, q % 2, :, :]), flat(state[:, ORDER[q] // CPB, :, :]),
                                        flat(s_hi[:, q % 2, :, :].bitcast(F32)), ALU.subtract).then_inc(s["s_lo_made"].sem, 1)

            def front(i, q):
                u = ORDER[q]
                v.wait_ge(s["xb_hi_made"].sem, s["xb_hi_made"].at(i, q + 1))
                nc.vector.tensor_tensor(xb_lo[:, q % 2, :, :].rearrange("p n t -> p (n t)"), p_tr[:, 0:2 * P],
                                        xb_hi[:, q % 2, :, :].rearrange("p n t -> p (n t)").bitcast(F32), ALU.subtract)\
                    .then_inc(s["xb_lo_made"].sem, 1)
                v.wait_ge(s["dec_made"].sem, s["dec_made"].at(i, q + 1))
                v.wait_ge(s["dt_ready"].sem, s["dt_ready"].at(i))
                v.wait_ge(s["xs_made"].sem, s["xs_made"].at(i, q))
                nc.vector.tensor_tensor(wd[:, :], dec[:, :, P - 1], dtv[:, u * HEADS:(u + 1) * HEADS], ALU.mult)\
                    .then_inc(s["wd_made"].sem, 1)
                v.wait_ge(s["wd_made"].sem, s["wd_made"].at(i, q + 1))
                v.wait_ge(s["xs_lo_made"].sem, s["xs_lo_made"].at(i, q))
                nc.vector.tensor_tensor(xs32[:, :, :], over_heads(p_tr[:, 0:P]), per_head(wd[:, :]), ALU.mult)\
                    .then_inc(s["xs_made"].sem, 1)
                v.wait_ge(s["mdt_made"].sem, s["mdt_made"].at(i, q + 1))
                v.wait_ge(s["att_lo_made"].sem, s["att_lo_made"].at(i, q))
                nc.vector.tensor_tensor(flat(att32[:, :, :]), flat(dec[:, :, :]), flat(mdt[:, :, :]), ALU.mult)\
                    .then_inc(s["t1"].sem, 1)
                v.wait_ge(s["t1"].sem, s["t1"].at(i, q + 1))
                v.wait_ge(s["sc_ps"].sem, s["sc_ps"].at(i, q + 1))
                nc.vector.tensor_tensor(flat(att32[:, :, :]), p_s[:, :], flat(att32[:, :, :]), ALU.mult)\
                    .then_inc(s["t2"].sem, 1)
                v.wait_ge(s["t2"].sem, s["t2"].at(i, q + 1))
                for h in range(HEADS):
                    ins = nc.vector.scalar_tensor_tensor(out=att32[:, h, :], in0=ident[:, :], scalar=head_sb[:, 1, h:h + 1],
                                                         in1=att32[:, h, :], op0=ALU.mult, op1=ALU.add)
                ins.then_inc(s["att_made"].sem, 1)

            def back(i, q):
                b = ORDER[q] // CPB
                v.wait_ge(s["st_ps"].sem, s["st_ps"].at(i, q + 1))
                v.wait_ge(s["s_decayed"].sem, s["s_decayed"].at(i, q + 1))
                sv = flat(state[:, b, :, :])
                nc.vector.tensor_tensor(sv, p_st[:, :], sv, ALU.add).then_inc(s["s_updated"].sem, 1)
                v.wait_ge(s["y_ps"].sem, s["y_ps"].at(i, q + 1))
                v.wait_ge(s["y_hi_made"].sem, s["y_hi_made"].at(i, q))
                v.wait_ge(s["y_lo_made"].sem, s["y_lo_made"].at(i, q))
                waits_apart(v, passed_vector)
                j, u = (i, ORDER[q]) if q >= 0 else (i - 1, ORDER[q + TILES])
                nc.vector.tensor_tensor(y32[:, :, :], p_y[:, :].rearrange("p (h t) -> p h t", h=HEADS), z_of(j, u), ALU.mult)\
                    .then_inc(s["y_gated"].sem, 1)

            def low_y(i, q):
                v.wait_ge(s["y_hi_made"].sem, s["y_hi_made"].at(i, q + 1))
                nc.vector.tensor_tensor(flat(y_lo[:, :, :]), flat(y32[:, :, :]), flat(y_hi[:, :, :].bitcast(F32)),
                                        ALU.subtract).then_inc(s["y_lo_made"].sem, 1)

            def output(i, q):
                j, n = (i, q) if q >= 0 else (i - 1, q + TILES)
                u = ORDER[n]
                v.wait_ge(xr_in[u].sem, xr_in[u].at(j))
                waits_apart(v, passed_vector)
                keep = lnk[:, bass.ds(j * 2 * TILES, 2 * TILES)]
                nc.vector.tensor_scalar(xr[:, u, :], xr[:, u, :], keep[:, u:u + 1], keep[:, TILES + u:TILES + u + 1],
                                        ALU.mult, ALU.add).then_inc(s["xhat"].sem, 1)
                v.wait_ge(s["xhat"].sem, s["xhat"].at(i, q + 1))
                v.wait_ge(s["o_ps"].sem, s["o_ps"].at(i, q + 1))
                nc.vector.tensor_tensor(xr[:, u, :], p_o[:, :], xr[:, u, :], ALU.add).then_inc(s["h_made"].sem, 1)

            def rest(i, q, before=2):
                if before:
                    back(i, q - 1)
                if before > 1:
                    output(i, q - 2)
                if before:
                    low_y(i, q - 1)

            def body(i, first, more):
                if not first:
                    take_state(i - 1, 3)
                    front(i - 1, 3)
                    rest(i - 1, 3)
                    dt_write(i)
                    convolve(i, CONV_AT[3])
                    keep_history(i)
                    if more:
                        stats(i + 1)
                    prepare(i, 0)
                take_state(i, 0)
                front(i, 0)
                rest(i, 0, 0 if first else 2)
                prepare(i, 1)
                if more:
                    if first:
                        stats(i + 1)
                    normalise(i + 1)
                take_state(i, 1)
                front(i, 1)
                if more:
                    turn(i + 1)
                rest(i, 1, 1 if first else 2)
                prepare(i, 2)
                if more:
                    dt_start(i + 1)
                    convolve(i + 1, CONV_AT[1])
                take_state(i, 2)
                front(i, 2)
                rest(i, 2)
                prepare(i, 3)
                if more:
                    dt_finish(i + 1)
                    convolve(i + 1, CONV_AT[2])

            nc.vector.memset(raw[:, :, :, 0:TAPS - 1], 0.0).then_inc(zeroed.sem, 1)
            nc.vector.memset(state[:, :, :, :], 0.0).then_inc(zeroed.sem, 1)
            stats(0)
            v.wait_ge(ln1_in.sem, ln1_in.at(0, 16))
            wv = cx[:, 0:KD * D_PROJ].rearrange("p (k n) -> p k n", k=KD)

            def scale_w(k):
                v.wait_ge(win_in[k].sem, win_in[k].at(0, 16))
                nc.vector.tensor_scalar(wv[:, k, :], wv[:, k, :], ln1_sb[:, k:k + 1], None, ALU.mult).then_inc(win_scaled.sem, 1)

            def low_w(k):
                v.wait_ge(wi_hi_made.sem, wi_hi_made.at(0, k + 1))
                if k % 2 == 0:
                    nc.vector.tensor_tensor(wi_lo[:, k, :], wv[:, k, 0:NW], wi_hi[:, k, :].bitcast(F32), ALU.subtract)
                nc.vector.tensor_tensor(wdt[:, k, HEADS:], wv[:, k, NW:D_PROJ], wdt[:, k, 0:HEADS].bitcast(F32), ALU.subtract)\
                    .then_inc(wi_lo_made.sem, 1)

            scale_w(0)
            scale_w(1)
            low_w(0)
            scale_w(2)
            scale_w(3)
            normalise(0)
            low_w(1)
            low_w(2)
            low_w(3)
            turn(0)
            v.wait_ge(par_in.sem, par_in.at(0, 5 * 16))
            dt_start(0)
            v.wait_ge(neg_a_made.sem, neg_a_made.at(0, 1))
            v.wait_ge(zeroed.sem, zeroed.at(0, 2))
            v.wait_ge(wi_lo_made.sem, wi_lo_made.at(0, KD))
            v.wait_ge(wi_lo_pool.sem, wi_lo_pool.at(0, 2))
            dt_finish(0)
            dt_write(0)
            convolve(0, range(1, 1 + CONV))
            keep_history(0)
            prepare(0, 0)
            body(0, True, True)
            with nc.vector.Fori(1, BLOCKS - 1) as i:
                body(i, False, True)
            body(BLOCKS - 1, False, False)
            last = BLOCKS - 1
            take_state(last, 3)
            front(last, 3)
            rest(last, 3)
            back(last, 3)
            output(last, 2)
            low_y(last, 3)
            output(last, 3)


def mlp_phase(nc, x, ln2, gate, up, down, lora_a, lora_b, w_ffn, ffn_bias, lora_coef, h_scratch, out):
    with ExitStack() as ctx:
        def sb(name, shape, dt=F32):
            return ctx.enter_context(nc.sbuf_tensor(name, shape, dt))

        def psum(name):
            return ctx.enter_context(nc.psum_tensor(name, [P, 512], F32))

        def sig(name, per, seeded=True):
            return Signal(nc, ctx, name, per, seeded)

        D = D_MODEL
        PIECE = 2
        PIECES = FT // PIECE
        w_gu = sb("w_gu", [P, KD, 2, INTER])
        w_dn = sb("w_dn", [P, FT, D])
        gu_hi, gu_lo = sb("gu_hi", [P, 2, KD, 2, P], F32R), sb("gu_lo", [P, 2, KD, 2, P], F32R)
        dn_hi, dn_lo = sb("dn_hi", [P, 2, D], F32R), sb("dn_lo", [P, 2, D], F32R)
        ZT = KD * BT
        zt_hi, zt_lo = sb("zt2_hi", [P, 2 * ZT], F32R), sb("zt2_lo", [P, 2 * ZT], F32R)
        hz = sb("hz", [P, 2, D])
        g32, m32 = sb("g32", [P, BT]), sb("m32", [P, BT])
        m_hi, m_lo = sb("m_hi", [P, 2, BT], F32R), sb("m_lo", [P, 2, BT], F32R)
        hr = sb("hr", [P, TILES, D])
        x1 = sb("x1", [P, TILES, D])
        z3 = sb("z3", [P, D])
        z3t_hi, z3t_lo = sb("z3t_hi", [P, KD, P], F32R), sb("z3t_lo", [P, KD, P], F32R)
        fo = sb("fo", [P, D])
        we_hi, we_lo = sb("we_hi", [P, KD, D], F32R), sb("we_lo", [P, KD, D], F32R)
        bias = sb("bias", [P, D])
        ident = sb("ident2", [P, P])
        ln2_sb, coef = sb("ln2_sb", [P, KD]), sb("coef", [P, 1])
        mhalf = sb("mhalf2", [P, TILES])
        bn = sb("bn2", [P, 4, TILES, 6])
        mv = sb("mv2", [P, 4, TILES, 2])
        tmp = sb("tmp", [P, 4, 4, TILES])
        scl = sb("scl", [P, 4, 2, TILES])

        p_g, p_u, p_x, p_f = (psum(n) for n in ("p_g", "p_u", "p_x", "p_f"))
        p_m = [psum(f"p_m{u}") for u in range(TILES)]

        par_in, lora_in, wt_in = (sig(n, 1, False) for n in ("par2_in", "lora_in", "wt_in"))
        piece_in = [sig(f"piece_in{c}", 1, False) for c in range(PIECES)]
        hz_in = [sig(f"hz_in{n}", 16 * TILES // 2, False) for n in range(2)]
        hr_in, x1_in = sig("hr_in", 16, False), sig("x1_in", 32, False)
        out_done = sig("out_done", 16 * TILES)
        consts, ident_zero = sig("consts2", 1, False), sig("ident_zero", 1, False)
        w_scaled, lora_scaled, lora_ps, lora_added, we_hi_made, we_lo_made = (
            sig(n, 1, False) for n in ("w_scaled", "lora_scaled", "lora_ps", "lora_added", "we_hi_made", "we_lo_made"))
        pe = {n: sig(n, per) for n, per in dict(
            g_ps=FT, u_ps=FT, dn_ps=FT, z2_ps=TILES, z3_ps=TILES, f_ps=TILES).items()}
        act = {n: sig(n, per) for n, per in dict(
            silu_made=FT, m_hi_made=FT, gu_hi_made=FT, dn_hi_made=FT, z2_hi_made=TILES, z3_hi_made=TILES).items()}
        dve = {n: sig(n, per) for n, per in dict(
            m_made=FT, m_lo_made=FT, dn_lo_made=FT, z2_lo_made=TILES, z3_lo_made=TILES,
            bn_h=TILES, mv_h=TILES, z2_made=TILES,
            h2_made=TILES, bn_1=TILES, mv_1=TILES, n1_made=TILES, bn_2=TILES, mv_2=TILES, z3_made=TILES,
            f_made=TILES, bn_3=TILES, mv_3=TILES, n3_made=TILES).items()}
        pool = {n: sig(n, per) for n, per in dict(
            gu_lo_made=FT, st_h=3 * TILES, sc_h=TILES, st_1=3, sc_1=1, st_2=3, sc_2=1, st_3=3 * TILES, sc_3=TILES,
            x1_made=TILES, out_made=TILES).items()}
        s = {**pe, **act, **dve, **pool}

        passed_pool, passed_vector = (ctx.enter_context(nc.semaphore(n)) for n in ("passed_pool", "passed_vector"))

        block = ctx.enter_context(nc.Block())
        x_blocks = x.rearrange("(b i c p) d -> b i p c d", b=BATCH, i=BLOCKS, c=CPB)
        o_tiles = out.rearrange("(b i c p) d -> b i c p d", b=BATCH, i=BLOCKS, c=CPB)

        def zts(t, j, first, count):
            return t[:, bass.ds((j % 2) * ZT + first, count)]

        def zt_tile(t, j, u):
            return zts(t, j, 0, ZT).rearrange("p (k t) -> p k t", k=KD)[:, :, u * P:(u + 1) * P]

        Z3_AT = {3 + 2 * u: u for u in range(TILES)}
        F_AT = {4 + 2 * u: u for u in range(TILES)}
        OUT_AT = {5 + 2 * u: u for u in range(TILES)}
        STORE_AT = {6 + 2 * u: u for u in range(TILES)}
        LORA_AT = {2 + k: k for k in range(KD)}

        @block.sync
        def _(sp):
            def load_tile(j, u):
                if not (isinstance(j, int) and j == 0 and u < 2):
                    sp.wait_ge(s["z2_ps"].sem, s["z2_ps"].at(j, u - 1))
                sp.dma_start(hz[:, u % 2, :], h_scratch[bass.ds(j * TILES + u, 1)].rearrange("o p d -> (o p) d"))\
                    .then_inc(hz_in[u % 2].sem, 16)

            def load_hr(j):
                sp.dma_start(hr[:, :, :], h_scratch[bass.ds(j * TILES, TILES)].rearrange("u p d -> p u d"))\
                    .then_inc(hr_in.sem, 16)

            def load_x1(j):
                for b in range(BATCH):
                    sp.dma_start(x1[:, b * CPB:(b + 1) * CPB, :], x_blocks[b, bass.ds(j, 1)].rearrange("o p c d -> (o p) c d"))\
                        .then_inc(x1_in.sem, 16)

            def store(t, u):
                sp.wait_ge(s["out_made"].sem, s["out_made"].at(t, u + 1))
                sp.dma_start(o_tiles[u // CPB, bass.ds(t, 1), u % CPB].rearrange("o p d -> (o p) d"), fo[:, :])\
                    .then_inc(out_done.sem, 16)

            def load_piece(c):
                cols = slice(c * PIECE * P, (c + 1) * PIECE * P)
                for n, w in enumerate((gate, up)):
                    sp.dma_start(w_gu[:, :, n, cols], w[:, cols].rearrange("(k p) f -> p k f", p=P)).then_inc(piece_in[c].sem, 16)
                sp.dma_start(w_dn[:, c * PIECE:(c + 1) * PIECE, :],
                             down[cols, :].rearrange("(f p) d -> p f d", p=P)).then_inc(piece_in[c].sem, 16)

            out_done.seed(sp)
            sp.dma_start(ln2_sb[:, :], ln2).then_inc(par_in.sem, 16)
            load_tile(0, 0)
            load_tile(0, 1)
            load_piece(0)
            load_tile(0, 2)
            load_tile(0, 3)
            load_piece(1)
            for dst, src in ((z3, lora_a), (fo, lora_b), (coef, lora_coef), (bias, ffn_bias)):
                sp.dma_start(dst[:, :], src).then_inc(lora_in.sem, 16)
            sp.dma_start(x1[:, :, :], w_ffn.rearrange("(k p) o -> p k o", p=P)).then_inc(wt_in.sem, 16)
            for c in range(2, PIECES):
                load_piece(c)

            def body(j, tail, more):
                if tail:
                    sp.wait_ge(s["x1_made"].sem, s["x1_made"].at(j - 1))
                load_hr(j)
                if more:
                    load_tile(j + 1, 0)
                for u in range(TILES):
                    if more and u + 1 < TILES:
                        load_tile(j + 1, u + 1)
                    if tail:
                        store(j - 1, u)
                if not tail:
                    sp.wait_ge(we_lo_made.sem, we_lo_made.at(0, 1))
                load_x1(j)

            body(0, False, True)
            with nc.sync.Fori(1, BLOCKS - 1) as j:
                body(j, True, True)
            body(BLOCKS - 1, True, False)
            for u in range(TILES):
                store(BLOCKS - 1, u)
            sp.wait_ge(out_done.sem, out_done.at(BLOCKS - 1))

        @block.tensor
        def _(t):
            for v in pe.values():
                v.seed(t)

            def turn_z2(j, u):
                t.wait_ge(s["z2_made"].sem, s["z2_made"].at(j, u + 1))
                t.wait_ge(s["z2_lo_made"].sem, s["z2_lo_made"].at(j, u))
                for k in range(KD):
                    ins = nc.tensor.transpose(p_x[:, k * P:(k + 1) * P], hz[:, u % 2, k * P:(k + 1) * P], ident[:, :])
                ins.then_inc(s["z2_ps"].sem, 1)

            def turn_z3(j, u, more):
                t.wait_ge(s["z3_made"].sem, s["z3_made"].at(j, u + 1))
                t.wait_ge(s["z3_lo_made"].sem, s["z3_lo_made"].at(j, u))
                if more:
                    t.wait_ge(s["z2_lo_made"].sem, s["z2_lo_made"].at(j + 2, u))
                for k in range(KD):
                    ins = nc.tensor.transpose(p_x[:, k * P:(k + 1) * P], z3[:, k * P:(k + 1) * P], ident[:, :])
                ins.then_inc(s["z3_ps"].sem, 1)

            def linear(j, u):
                t.wait_ge(s["z3_lo_made"].sem, s["z3_lo_made"].at(j, u + 1))
                t.wait_ge(s["f_made"].sem, s["f_made"].at(j, u))
                n = 0
                for k in range(KD):
                    for l, r in split_passes(z3t_hi, z3t_lo, we_hi, we_lo):
                        ins = nc.tensor.matmul(p_f[:, :], l[:, k, :], r[:, k, :], start=(n == 0), stop=(n == 3 * KD - 1))
                        n += 1
                ins.then_inc(s["f_ps"].sem, 1)

            def gate_up(j, f, which):
                n = 0
                bank = (p_g, p_u)[which]
                for k in range(KD):
                    for l, r in split_passes(gu_hi, gu_lo, zt_hi, zt_lo):
                        ins = nc.tensor.matmul(bank[:, :], l[:, f % 2, k, which, :], zts(r, j, k * BT, BT),
                                               start=(n == 0), stop=(n == 3 * KD - 1))
                        n += 1
                return ins

            def down_part(j, f):
                t.wait_ge(s["m_hi_made"].sem, s["m_hi_made"].at(j, f + 1))
                t.wait_ge(s["m_lo_made"].sem, s["m_lo_made"].at(j, f + 1))
                t.wait_ge(s["dn_hi_made"].sem, s["dn_hi_made"].at(j, f + 1))
                t.wait_ge(s["dn_lo_made"].sem, s["dn_lo_made"].at(j, f + 1))
                if f == 0:
                    t.wait_ge(s["h2_made"].sem, s["h2_made"].at(j - 1))
                for u in range(TILES):
                    for n, (l, r) in enumerate(split_passes(m_hi, m_lo, dn_hi, dn_lo)):
                        ins = nc.tensor.matmul(p_m[u][:, :], l[:, f % 2, u * P:(u + 1) * P], r[:, f % 2, :],
                                               start=(f == 0 and n == 0), stop=(f == FT - 1 and n == 2))
                ins.then_inc(s["dn_ps"].sem, 1)

            def body(j, tail, more):
                t.wait_ge(s["z2_lo_made"].sem, s["z2_lo_made"].at(j))
                for f in range(FT):
                    t.wait_ge(s["gu_hi_made"].sem, s["gu_hi_made"].at(j, f + 1))
                    t.wait_ge(s["gu_lo_made"].sem, s["gu_lo_made"].at(j, f + 1))
                    t.wait_ge(s["silu_made"].sem, s["silu_made"].at(j, f))
                    gate_up(j, f, 0).then_inc(s["g_ps"].sem, 1)
                    t.wait_ge(s["m_made"].sem, s["m_made"].at(j, f))
                    gate_up(j, f, 1).then_inc(s["u_ps"].sem, 1)
                    if f:
                        down_part(j, f - 1)
                    if not tail and f in LORA_AT:
                        k = LORA_AT[f]
                        t.wait_ge(lora_scaled.sem, lora_scaled.at(0, 1))
                        if k:
                            t.wait_ge(lora_added.sem, lora_added.at(0, k))
                        nc.tensor.matmul(p_f[:, :], z3[:, k * P:(k + 1) * P], fo[:, :], start=True, stop=True)\
                            .then_inc(lora_ps.sem, 1)
                    if tail and f in Z3_AT:
                        turn_z3(j - 1, Z3_AT[f], more)
                    if tail and f in F_AT:
                        linear(j - 1, F_AT[f])
                    if more and f in F_AT:
                        if tail:
                            t.wait_ge(s["z3_lo_made"].sem, s["z3_lo_made"].at(j - 1, F_AT[f] + 1))
                        turn_z2(j + 1, F_AT[f])
                down_part(j, FT - 1)

            t.wait_ge(consts.sem, consts.at(0, 2))
            for u in range(TILES):
                turn_z2(0, u)
            body(0, False, True)
            with nc.tensor.Fori(1, BLOCKS - 1) as j:
                body(j, True, True)
            body(BLOCKS - 1, True, False)
            for u in range(TILES):
                turn_z3(BLOCKS - 1, u, False)
                linear(BLOCKS - 1, u)

        @block.scalar
        def _(a):
            for v in act.values():
                v.seed(a)

            def split_gu(j, n, f):
                cols = slice(f * P, (f + 1) * P)
                a.wait_ge(w_scaled.sem, w_scaled.at(0, (f // PIECE + 1) * KD))
                a.wait_ge(s["u_ps"].sem, s["u_ps"].at(j, n))
                for w in range(2):
                    ins = nc.scalar.copy(gu_hi[:, f % 2, :, w, :], w_gu[:, :, w, cols])
                ins.then_inc(s["gu_hi_made"].sem, 1)

            def split_dn(j, f):
                a.wait_ge(s["dn_ps"].sem, s["dn_ps"].at(j, f - 1))
                nc.scalar.copy(dn_hi[:, f % 2, :], w_dn[:, f, :]).then_inc(s["dn_hi_made"].sem, 1)

            def turn_z2(j, u):
                a.wait_ge(s["z2_ps"].sem, s["z2_ps"].at(j, u + 1))
                a.wait_ge(s["u_ps"].sem, s["u_ps"].at(j - 2))
                nc.scalar.copy(zt_tile(zt_hi, j, u), p_x[:, :].rearrange("p (k t) -> p k t", k=KD))\
                    .then_inc(s["z2_hi_made"].sem, 1)

            def turn_z3(j, u):
                a.wait_ge(s["z3_ps"].sem, s["z3_ps"].at(j, u + 1))
                a.wait_ge(s["f_ps"].sem, s["f_ps"].at(j, u))
                nc.scalar.copy(z3t_hi[:, :, :].rearrange("p k t -> p (k t)"), p_x[:, :]).then_inc(s["z3_hi_made"].sem, 1)

            def body(j, tail, more):
                for f in range(FT):
                    if f < FT - 1:
                        split_gu(j, f, f + 1)
                    elif more:
                        split_gu(j, f, 0)
                    split_dn(j, f)
                    if tail and f - 1 in Z3_AT:
                        turn_z3(j - 1, Z3_AT[f - 1])
                    if more and f - 1 in F_AT:
                        turn_z2(j + 1, F_AT[f - 1])
                    a.wait_ge(s["g_ps"].sem, s["g_ps"].at(j, f + 1))
                    a.wait_ge(s["m_made"].sem, s["m_made"].at(j, f))
                    nc.scalar.activation(g32[:, :], p_g[:, :], ACT.Silu).then_inc(s["silu_made"].sem, 1)
                    a.wait_ge(s["m_made"].sem, s["m_made"].at(j, f + 1))
                    a.wait_ge(s["dn_ps"].sem, s["dn_ps"].at(j, f - 1))
                    nc.scalar.copy(m_hi[:, f % 2, :], m32[:, :]).then_inc(s["m_hi_made"].sem, 1)
                    if not tail and f == FT - 3:
                        a.wait_ge(lora_added.sem, lora_added.at(0, KD))
                        nc.scalar.copy(we_hi[:, :, :], x1[:, :, :]).then_inc(we_hi_made.sem, 1)

            split_gu(0, 0, 0)
            for u in range(TILES):
                turn_z2(0, u)
            body(0, False, True)
            with nc.scalar.Fori(1, BLOCKS - 1) as j:
                body(j, True, True)
            body(BLOCKS - 1, True, False)
            for u in range(TILES):
                turn_z3(BLOCKS - 1, u)

        H, N1, N2, N3 = range(4)

        @block.gpsimd
        def _(g):
            for v in pool.values():
                v.seed(g)
            nc.gpsimd.memset(mhalf[:, :], -0.5).then_inc(consts.sem, 1)
            nc.gpsimd.memset(ident[:, :], 0.0).then_inc(ident_zero.sem, 1)
            g.wait_ge(ident_zero.sem, ident_zero.at(0, 1))
            nc.gpsimd.affine_select(out=ident[:, :], in_=ident[:, :], compare_op=ALU.not_equal, fill=1.0, base=0,
                                    pattern=[[-1, P]], channel_multiplier=1).then_inc(consts.sem, 1)
            g.wait_ge(consts.sem, consts.at(0, 2))

            def chain(step, made, j, n0, row, cols, rms):
                mean, var = mv[:, row, cols, 0], mv[:, row, cols, 1]
                t0, t1, t2, t3 = (tmp[:, row, n, cols] for n in range(4))

                def then(n, ins):
                    ins.then_inc(step.sem, 1)
                    g.wait_ge(step.sem, step.at(j, n0 + n))
                    waits_apart(g, passed_pool)

                if rms:
                    then(1, nc.gpsimd.tensor_tensor(t0, mean, mean, ALU.mult))
                    then(2, nc.gpsimd.tensor_tensor(t1, t0, var, ALU.add))
                    then(3, nc.gpsimd.tensor_scalar(t2, t1, EPS, 1.0, ALU.add, ALU.mult))
                    nc.gpsimd.tensor_tensor(scl[:, row, 0, cols], t2, mhalf[:, cols], ALU.pow).then_inc(made.sem, 1)
                else:
                    then(1, nc.gpsimd.tensor_scalar(t2, var, EPS, 1.0, ALU.add, ALU.mult))
                    then(2, nc.gpsimd.tensor_tensor(scl[:, row, 0, cols], t2, mhalf[:, cols], ALU.pow))
                    then(3, nc.gpsimd.tensor_tensor(t0, mean, scl[:, row, 0, cols], ALU.mult))
                    nc.gpsimd.tensor_scalar(scl[:, row, 1, cols], t0, -1.0, 1.0, ALU.mult, ALU.mult).then_inc(made.sem, 1)

            def split_lo(j, n, f):
                cols = slice(f * P, (f + 1) * P)
                g.wait_ge(s["gu_hi_made"].sem, s["gu_hi_made"].at(j, n))
                for w in range(2):
                    ins = nc.gpsimd.tensor_tensor(gu_lo[:, f % 2, :, w, :], w_gu[:, :, w, cols],
                                                  gu_hi[:, f % 2, :, w, :].bitcast(F32), ALU.subtract)
                ins.then_inc(s["gu_lo_made"].sem, 1)

            def norm_h(j, u):
                g.wait_ge(s["mv_h"].sem, s["mv_h"].at(j, u + 1))
                g.wait_ge(s["z2_made"].sem, s["z2_made"].at(j, u))
                waits_apart(g, passed_pool)
                chain(s["st_h"], s["sc_h"], j, 3 * u, H, slice(u, u + 1), True)

            def end(j, u):
                g.wait_ge(s["n3_made"].sem, s["n3_made"].at(j, u + 1))
                nc.gpsimd.tensor_tensor(fo[:, :], fo[:, :], x1[:, u, :], ALU.add).then_inc(s["out_made"].sem, 1)

            def norm_3(j, u):
                g.wait_ge(s["mv_3"].sem, s["mv_3"].at(j, u + 1))
                waits_apart(g, passed_pool)
                chain(s["st_3"], s["sc_3"], j, 3 * u, N3, slice(u, u + 1), False)

            def norm_1(j):
                g.wait_ge(s["mv_1"].sem, s["mv_1"].at(j))
                g.wait_ge(s["n1_made"].sem, s["n1_made"].at(j - 1))
                waits_apart(g, passed_pool)
                chain(s["st_1"], s["sc_1"], j, 0, N1, slice(0, TILES), False)

            def first_sum(j):
                g.wait_ge(x1_in.sem, x1_in.at(j))
                for u in range(TILES):
                    g.wait_ge(s["n1_made"].sem, s["n1_made"].at(j, u + 1))
                    nc.gpsimd.tensor_tensor(x1[:, u, :], x1[:, u, :], hr[:, u, :], ALU.add).then_inc(s["x1_made"].sem, 1)

            def norm_2(j):
                g.wait_ge(s["mv_2"].sem, s["mv_2"].at(j))
                g.wait_ge(s["z3_made"].sem, s["z3_made"].at(j - 1))
                waits_apart(g, passed_pool)
                chain(s["st_2"], s["sc_2"], j, 0, N2, slice(0, TILES), False)

            def body(j, tail, more):
                for f in range(FT):
                    if f < FT - 1:
                        split_lo(j, f + 2, f + 1)
                    elif more:
                        split_lo(j, FT + 1, 0)
                    if tail:
                        if f in STORE_AT:
                            end(j - 1, STORE_AT[f])
                        if f == 0:
                            norm_1(j - 1)
                        if f == 1:
                            first_sum(j - 1)
                        if f == 2:
                            norm_2(j - 1)
                        if f in OUT_AT:
                            norm_3(j - 1, OUT_AT[f])
                    if more and f in Z3_AT:
                        norm_h(j + 1, Z3_AT[f])

            norm_h(0, 0)
            norm_h(0, 1)
            split_lo(0, 1, 0)
            norm_h(0, 2)
            norm_h(0, 3)
            body(0, False, True)
            with nc.gpsimd.Fori(1, BLOCKS - 1) as j:
                body(j, True, True)
            body(BLOCKS - 1, True, False)
            last = BLOCKS - 1
            norm_1(last)
            first_sum(last)
            norm_2(last)
            for u in range(TILES):
                norm_3(last, u)
                end(last, u)

        @block.vector
        def _(v):
            for e in dve.values():
                e.seed(v)

            def stats(src, row, u, bn_sig, mv_sig, j):
                nc.vector.bn_stats(bn[:, row, u, :], src).then_inc(bn_sig.sem, 1)
                v.wait_ge(bn_sig.sem, bn_sig.at(j, u + 1))
                waits_apart(v, passed_vector)
                nc.vector.bn_aggr(mv[:, row, u, :], bn[:, row, u, :]).then_inc(mv_sig.sem, 1)

            def scaled(dst, src, row, u):
                return nc.vector.tensor_scalar(dst, src, scl[:, row, 0, u:u + 1], scl[:, row, 1, u:u + 1], ALU.mult, ALU.add)

            def scale_weights(c):
                v.wait_ge(piece_in[c].sem, piece_in[c].at(0, 48))
                v.wait_ge(par_in.sem, par_in.at(0, 16))
                cols = slice(c * PIECE * P, (c + 1) * PIECE * P)
                for k in range(KD):
                    nc.vector.tensor_scalar(w_gu[:, k, :, cols], w_gu[:, k, :, cols], ln2_sb[:, k:k + 1], None, ALU.mult)\
                        .then_inc(w_scaled.sem, 1)

            def split_dn(j, f):
                v.wait_ge(s["dn_hi_made"].sem, s["dn_hi_made"].at(j, f + 1))
                nc.vector.tensor_tensor(dn_lo[:, f % 2, :], w_dn[:, f, :], dn_hi[:, f % 2, :].bitcast(F32), ALU.subtract)\
                    .then_inc(s["dn_lo_made"].sem, 1)

            def norm_h(j, u):
                v.wait_ge(hz_in[u % 2].sem, hz_in[u % 2].at(j, 16 * (u // 2 + 1)))
                v.wait_ge(s["sc_h"].sem, s["sc_h"].at(j - 1, u + 1))
                stats(hz[:, u % 2, :], H, u, s["bn_h"], s["mv_h"], j)

            def make_z2(j, u):
                v.wait_ge(s["sc_h"].sem, s["sc_h"].at(j, u + 1))
                nc.vector.tensor_scalar(hz[:, u % 2, :], hz[:, u % 2, :], scl[:, H, 0, u:u + 1], None, ALU.mult)\
                    .then_inc(s["z2_made"].sem, 1)

            def turn_z2(j, u):
                v.wait_ge(s["z2_hi_made"].sem, s["z2_hi_made"].at(j, u + 1))
                nc.vector.tensor_tensor(zt_tile(zt_lo, j, u), p_x[:, :].rearrange("p (k t) -> p k t", k=KD),
                                        zt_tile(zt_hi, j, u).bitcast(F32), ALU.subtract).then_inc(s["z2_lo_made"].sem, 1)

            def sums(j):
                v.wait_ge(hr_in.sem, hr_in.at(j))
                v.wait_ge(s["dn_ps"].sem, s["dn_ps"].at(j))
                v.wait_ge(s["sc_1"].sem, s["sc_1"].at(j - 1))
                for u in range(TILES):
                    nc.vector.tensor_tensor(hr[:, u, :], p_m[u][:, :], hr[:, u, :], ALU.add).then_inc(s["h2_made"].sem, 1)

            def first_stats(j):
                for u in range(TILES):
                    v.wait_ge(s["h2_made"].sem, s["h2_made"].at(j, u + 1))
                    stats(hr[:, u, :], N1, u, s["bn_1"], s["mv_1"], j)

            def first_norm(j):
                v.wait_ge(s["sc_1"].sem, s["sc_1"].at(j))
                for u in range(TILES):
                    scaled(hr[:, u, :], hr[:, u, :], N1, u).then_inc(s["n1_made"].sem, 1)

            def second_stats(j):
                v.wait_ge(s["sc_2"].sem, s["sc_2"].at(j - 1))
                for u in range(TILES):
                    v.wait_ge(s["x1_made"].sem, s["x1_made"].at(j, u + 1))
                    stats(x1[:, u, :], N2, u, s["bn_2"], s["mv_2"], j)

            def make_z3(j, u):
                v.wait_ge(s["sc_2"].sem, s["sc_2"].at(j))
                v.wait_ge(s["z3_ps"].sem, s["z3_ps"].at(j, u))
                scaled(z3[:, :], x1[:, u, :], N2, u).then_inc(s["z3_made"].sem, 1)

            def turn_z3(j, u):
                v.wait_ge(s["z3_hi_made"].sem, s["z3_hi_made"].at(j, u + 1))
                nc.vector.tensor_tensor(z3t_lo[:, :, :].rearrange("p k t -> p (k t)"), p_x[:, :],
                                        z3t_hi[:, :, :].rearrange("p k t -> p (k t)").bitcast(F32), ALU.subtract)\
                    .then_inc(s["z3_lo_made"].sem, 1)

            def linear(j, u):
                v.wait_ge(s["f_ps"].sem, s["f_ps"].at(j, u + 1))
                v.wait_ge(out_done.sem, out_done.at(j, 16 * u))
                nc.vector.tensor_tensor(fo[:, :], p_f[:, :], bias[:, :], ALU.add).then_inc(s["f_made"].sem, 1)
                v.wait_ge(s["f_made"].sem, s["f_made"].at(j, u + 1))
                v.wait_ge(s["sc_3"].sem, s["sc_3"].at(j - 1, u + 1))
                stats(fo[:, :], N3, u, s["bn_3"], s["mv_3"], j)

            def last_norm(j, u):
                v.wait_ge(s["sc_3"].sem, s["sc_3"].at(j, u + 1))
                scaled(fo[:, :], fo[:, :], N3, u).then_inc(s["n3_made"].sem, 1)

            def body(j, tail, more):
                for f in range(FT):
                    split_dn(j, f)
                    if tail:
                        if f == 0:
                            sums(j - 1)
                        if f == 1:
                            first_norm(j - 1)
                        if f == 2:
                            second_stats(j - 1)
                        if f - 1 in Z3_AT:
                            turn_z3(j - 1, Z3_AT[f - 1])
                        if f - 1 in F_AT:
                            linear(j - 1, F_AT[f - 1])
                    if more and f - 1 in F_AT:
                        turn_z2(j + 1, F_AT[f - 1])
                    v.wait_ge(s["u_ps"].sem, s["u_ps"].at(j, f + 1))
                    v.wait_ge(s["silu_made"].sem, s["silu_made"].at(j, f + 1))
                    v.wait_ge(s["m_hi_made"].sem, s["m_hi_made"].at(j, f))
                    v.wait_ge(s["m_lo_made"].sem, s["m_lo_made"].at(j, f))
                    nc.vector.tensor_tensor(m32[:, :], p_u[:, :], g32[:, :], ALU.mult).then_inc(s["m_made"].sem, 1)
                    v.wait_ge(s["m_hi_made"].sem, s["m_hi_made"].at(j, f + 1))
                    nc.vector.tensor_tensor(m_lo[:, f % 2, :], m32[:, :], m_hi[:, f % 2, :].bitcast(F32), ALU.subtract)\
                        .then_inc(s["m_lo_made"].sem, 1)
                    if not tail:
                        if f % PIECE == 0 and f // PIECE + 1 < PIECES:
                            scale_weights(f // PIECE + 1)
                        if f in LORA_AT:
                            k = LORA_AT[f]
                            v.wait_ge(lora_ps.sem, lora_ps.at(0, k + 1))
                            v.wait_ge(wt_in.sem, wt_in.at(0, 16))
                            nc.vector.tensor_tensor(x1[:, k, :], p_f[:, :], x1[:, k, :], ALU.add).then_inc(lora_added.sem, 1)
                        if f == FT - 2:
                            v.wait_ge(we_hi_made.sem, we_hi_made.at(0, 1))
                            nc.vector.tensor_tensor(we_lo[:, :, :], x1[:, :, :], we_hi[:, :, :].bitcast(F32), ALU.subtract)\
                                .then_inc(we_lo_made.sem, 1)
                    if tail:
                        if f == 0:
                            first_stats(j - 1)
                        if f == 2:
                            make_z3(j - 1, 0)
                        if f in F_AT and F_AT[f] + 1 < TILES:
                            make_z3(j - 1, F_AT[f] + 1)
                        if f in OUT_AT:
                            last_norm(j - 1, OUT_AT[f])
                    if more:
                        if f + 1 in Z3_AT:
                            norm_h(j + 1, Z3_AT[f + 1])
                        if f in Z3_AT:
                            make_z2(j + 1, Z3_AT[f])

            norm_h(0, 0)
            norm_h(0, 1)
            scale_weights(0)
            make_z2(0, 0)
            make_z2(0, 1)
            turn_z2(0, 0)
            turn_z2(0, 1)
            for u in range(2, TILES):
                norm_h(0, u)
                make_z2(0, u)
                turn_z2(0, u)
            v.wait_ge(lora_in.sem, lora_in.at(0, 64))
            nc.vector.tensor_scalar(fo[:, :], fo[:, :], coef[:, :], LORA_SCALE, ALU.mult, ALU.mult).then_inc(lora_scaled.sem, 1)
            body(0, False, True)
            with nc.vector.Fori(1, BLOCKS - 1) as j:
                body(j, True, True)
            body(BLOCKS - 1, True, False)
            last = BLOCKS - 1
            sums(last)
            first_stats(last)
            first_norm(last)
            second_stats(last)
            for u in range(TILES):
                make_z3(last, u)
                turn_z3(last, u)
                linear(last, u)
                last_norm(last, u)


def kernel(**inputs):
    import numpy as np
    import concourse.bacc as _bacc
    from concourse.bass_utils import run_bass_kernel_spmd as _run

    a = {k.replace("L0_attn_", "").replace("L0_ffn_", "ffn_"): np.asarray(v) for k, v in inputs.items()}
    columns = lambda w, n: w.reshape(n, P).T
    every = lambda w: np.broadcast_to(w, (P, w.size))
    arrays = {
        "x": a["hidden_states"].reshape(BATCH * SEQ, D_MODEL),
        "w_in": a["w_in"].T,
        "w_out": a["w_out"].T,
        "conv_w": a["conv_w"].reshape(CONV, P, TAPS).transpose(1, 0, 2),
        "conv_b": columns(a["conv_b"], CONV),
        "a_log": every(a["A_log"]), "d_skip": every(a["D"]), "dt_bias": every(a["dt_bias"]),
        "ln1": columns(a["ln1_w"], KD), "ln2": columns(a["ln2_w"], KD),
        "gate": a["gate_w"].T, "up": a["up_w"].T, "down": a["down_w"].T,
        "lora_a": a["ffn_lora_A"].reshape(RANKS, D_MODEL),
        "lora_b": a["ffn_lora_B"].transpose(0, 2, 1).reshape(RANKS, D_MODEL),
        "w_ffn": a["ffn_W"].T,
        "ffn_bias": every(a["ffn_bias"]),
        "lora_coef": np.repeat(a["ffn_lora_weights"], RANKS // a["ffn_lora_weights"].size).reshape(RANKS, 1),
    }
    nc = _bacc.Bacc("TRN2", target_bir_lowering=False, num_devices=1)
    arrays = {n: np.ascontiguousarray(v) for n, v in arrays.items()}
    aps = {n: nc.dram_tensor(n, v.shape, F32, kind="ExternalInput").ap() for n, v in arrays.items()}
    h_scratch = nc.dram_tensor("h_scratch", (BLOCKS * TILES, P, D_MODEL), F32, kind="Internal").ap()
    out = nc.dram_tensor("out", (BATCH, SEQ, D_MODEL), F32, kind="ExternalOutput").ap()
    sandwich_program(nc, h_scratch=h_scratch, out=out.rearrange("b s d -> (b s) d"), **aps)
    r = _run(nc, [arrays], core_ids=[0])
    return r.results[0]["out"]
```

```python
from contextlib import ExitStack

import concourse.bass as bass
from concourse import mybir

F32 = mybir.dt.float32
F32R = mybir.dt.float32r
ALU = mybir.AluOpType
ACT = mybir.ActivationFunctionType

P = 128
EPS = 1e-5
BATCH, SEQ, D_MODEL = 2, 1024, 512
HEADS, STATE, TAPS = 4, 128, 4
D_INNER = 512
D_PROJ = 2 * D_INNER + 2 * P + HEADS
INTER = 1792
RANKS = 128
LORA_SCALE = 2.0

KD = D_MODEL // P
TILES = 4
BT = TILES * P
BLOCKS = BATCH * SEQ // BT
CPB = TILES // BATCH
CW = CPB * P
FT = INTER // P
ORDER = [b * CPB + c for c in range(CPB) for b in range(BATCH)]

CONV = 2 + HEADS
IN_GROUPS = [("dt", 2 * D_INNER + 2 * P, 0)] + \
    [("conv", D_INNER + P, 1), ("conv", D_INNER, 0)] + \
    [("conv", D_INNER + 2 * P + P * h, 2 + h) for h in range(HEADS)] + \
    [("z", P * h, h) for h in range(HEADS)]
NG = len(IN_GROUPS)
IN_AT = [[9, 10], [0, 1, 2], [3, 4, 5], [6, 7, 8]]
CONV_AT = [[], [1], [2, 3, 4], [5, 6]]
SEED = 2


def is_last(j):
    return isinstance(j, int) and j == BLOCKS


class Signal:

    def __init__(self, nc, ctx, name, per, seeded=True):
        self.sem = ctx.enter_context(nc.semaphore(name))
        self.per = per
        self.base = SEED if seeded else 0

    def at(self, block, n=None):
        return (block + self.base) * self.per + (self.per if n is None else n)

    def seed(self, engine, done=0):
        engine.sem_inc(self.sem, (self.base + done) * self.per)


def waits_apart(engine, passed):
    engine.sem_inc(passed, 1)


def sandwich_program(nc, x, w_in, w_out, conv_w, conv_b, a_log, d_skip, dt_bias, ln1, ln2, gate, up, down,
                     lora_a, lora_b, w_ffn, ffn_bias, lora_coef, h_scratch, out):
    with ExitStack() as ctx:
        turned = [ctx.enter_context(nc.sbuf_tensor(n, [P, 2 * KD * BT], F32R)) for n in ("turned_hi", "turned_lo")]
        split = [ctx.enter_context(nc.sbuf_tensor(n, [P, KD * (D_PROJ - HEADS)], F32R)) for n in ("split_a", "split_b")]
        gu = [split[0][:, n * 4 * KD * P:(n + 1) * 4 * KD * P].rearrange("p (f k w c) -> p f k w c", f=2, k=KD, w=2)
              for n in range(2)]
        state_space_phase(nc, x, w_in, w_out, conv_w, conv_b, a_log, d_skip, dt_bias, ln1, ln2, gate, up, h_scratch,
                          turned, split, gu)
        mlp_phase(nc, x, ln2, gate, up, down, lora_a, lora_b, w_ffn, ffn_bias, lora_coef, h_scratch, out, turned, split,
                  gu)


def split_passes(hi_l, lo_l, hi_r, lo_r):
    return [(hi_l, hi_r), (hi_l, lo_r), (lo_l, hi_r)]


def state_space_phase(nc, x, w_in, w_out, conv_w, conv_b, a_log, d_skip, dt_bias, ln1, ln2, gate, up,
                      h_scratch, turned, split, gu):
    with ExitStack() as ctx:
        def sb(name, shape, dt=F32):
            return ctx.enter_context(nc.sbuf_tensor(name, shape, dt))

        def psum(name):
            return ctx.enter_context(nc.psum_tensor(name, [P, 512], F32))

        def sig(name, per, seeded=True):
            return Signal(nc, ctx, name, per, seeded)

        NW = D_PROJ - HEADS
        wi_hi, wi_lo = (v[:, :].rearrange("p (k n) -> p k n", k=KD) for v in split)
        wdt = sb("wdt", [P, KD, 2 * HEADS], F32R)
        wo_flat = [v[:, KD * BT:KD * BT + HEADS * D_MODEL] for v in turned]
        wo_hi, wo_lo = (v.rearrange("p (h n) -> p h n", h=HEADS) for v in wo_flat)
        xin = sb("xin", [P, TILES, D_MODEL])
        zt_hi, zt_lo = (v[:, 0:KD * BT].rearrange("p (k t) -> p k t", k=KD) for v in turned)
        raw = sb("raw", [P, CONV, BATCH, TAPS - 1 + CW])
        CX = CONV * BT
        cx = sb("cx", [P, 2 * CX])
        ZS = HEADS * BT
        zs = sb("zs", [P, 2 * ZS])
        xr = sb("xr", [P, TILES, D_MODEL])
        xb32 = sb("xb32", [P, 2, P])
        b_hi, b_lo = sb("b_hi", [P, P], F32R), sb("b_lo", [P, P], F32R)
        xb_hi, xb_lo = sb("xb_hi", [P, 2, 2, P], F32R), sb("xb_lo", [P, 2, 2, P], F32R)
        c_hi, c_lo = sb("c_hi", [P, HEADS, P], F32R), sb("c_lo", [P, HEADS, P], F32R)
        r_hi, r_lo = sb("r_hi", [P, HEADS, P], F32R), sb("r_lo", [P, HEADS, P], F32R)
        dec = sb("dec", [P, HEADS, P])
        ecs = sb("ecs", [P, HEADS, P])
        mdt = sb("mdt", [P, HEADS, P])
        att32 = sb("att32", [P, HEADS, P])
        att_hi, att_lo = sb("att_hi", [P, 2, HEADS, P], F32R), sb("att_lo", [P, 2, HEADS, P], F32R)
        cp32 = sb("cp32", [P, HEADS, P])
        cp_hi, cp_lo = sb("cp_hi", [P, 2, HEADS, P], F32R), sb("cp_lo", [P, 2, HEADS, P], F32R)
        xs32 = sb("xs32", [P, HEADS, P])
        xs_hi, xs_lo = sb("xs_hi", [P, HEADS, P], F32R), sb("xs_lo", [P, HEADS, P], F32R)
        state = sb("state", [P, BATCH, HEADS, P])
        s_hi, s_lo = sb("s_hi", [P, 2, HEADS, P], F32R), sb("s_lo", [P, 2, HEADS, P], F32R)
        y32 = sb("y32", [P, HEADS, P])
        y_hi, y_lo = sb("y_hi", [P, HEADS, P], F32R), sb("y_lo", [P, HEADS, P], F32R)
        ident, upper = sb("ident", [P, P]), sb("upper", [P, P])
        after_f, ones_f = xb32[:, 0, :], xb32[:, 1, :]
        after, ones = sb("after", [P, P], F32R), sb("ones", [P, P], F32R)
        first_w = xin[:, :, :].rearrange("p k (w c) -> p k w c", w=2)
        ln2_first = sb("ln2_first", [P, KD])
        ln1_sb, cw_sb, cb_sb = sb("ln1_sb", [P, KD]), sb("cw_sb", [P, CONV, TAPS]), sb("cb_sb", [P, CONV])
        head_sb = sb("head_sb", [P, 3, HEADS])
        neg_a = sb("neg_a", [P, HEADS])
        mhalf = sb("mhalf", [P, TILES])
        bn = sb("bn", [P, TILES, 6])
        mv = sb("mv", [P, TILES, 2])
        lt = sb("lt", [P, 8, TILES])
        lz = sb("lz", [P, 2, TILES])
        lnk = sb("lnk", [P, BLOCKS * 2 * TILES])
        DH = TILES * HEADS
        dtt = sb("dtt", [P, 8, DH])
        dtv, a_hi, a_lo = sb("dtv", [P, DH]), sb("a_hi", [P, DH], F32R), sb("a_lo", [P, DH])
        wd = sb("wd", [P, HEADS])

        p_in = [psum("p_in0"), psum("p_in1")]
        p_tr, p_d, p_s, p_y, p_st, p_o = (psum(n) for n in ("p_tr", "p_d", "p_s", "p_y", "p_st", "p_o"))

        ln1_in, par_in, wout_in = (sig(n, 1, False) for n in ("ln1_in", "par_in", "wout_in"))
        win_in = [sig(f"win_in{k}", 1, False) for k in range(KD)]
        x_in = sig("x_in", 32, False)
        xr_in = [sig(f"xr_in{u}", 16, False) for u in range(TILES)]
        h_out = sig("h_out", 16 * TILES, False)
        first_w_in, first_w_scaled, first_w_hi = (sig(n, 1, False) for n in ("first_w_in", "first_w_scaled", "first_w_hi"))
        consts = sig("consts", 1, False)
        mask_made = sig("mask_made", 1, False)
        zeroed, win_scaled, wi_hi_made, wi_lo_made, wi_lo_pool, wo_hi_made, wo_lo_made, neg_a_made = (
            sig(n, 1, False) for n in ("zeroed", "win_scaled", "wi_hi_made", "wi_lo_made", "wi_lo_pool", "wo_hi_made",
                                       "wo_lo_made", "neg_a_made"))
        dve = {n: sig(n, per) for n, per in dict(
            bn_made=TILES, mean_var=TILES, normed=TILES, zt_lo_made=TILES, tap=4 * CONV, hist=1,
            dt_abs=1, dt_step=14, dt_tail=4, dt_ready=1, xb_copied=4, xb_lo_made=4, wd_made=4, xs_made=4,
            t1=4, t2=4, att_made=4, s_lo_made=4, s_updated=4, y_gated=4, y_lo_made=4, xhat=4, h_made=4).items()}
        act = {n: sig(n, per) for n, per in dict(
            zt_hi_made=TILES, in_out=NG, silu_made=CONV, dt_exp=1, dec_made=4, ecs_made=4, c_hi_made=4, b_hi_made=4,
            xb_hi_made=4, att_hi_made=4, cp_hi_made=4, xs_hi_made=4, s_hi_made=4, y_hi_made=4).items()}
        pool = {n: sig(n, per) for n, per in dict(
            ln_step=11, ln_scale=1, r_made=4, mdt_made=4, c_lo_made=4, b_lo_made=4, att_lo_made=4, cp_made=4,
            cp_lo_made=4, xs_lo_made=4, s_decayed=4).items()}
        pe = {n: sig(n, per) for n, per in dict(
            zt_ps=TILES, in_ps=NG, dt_turned=1, d_ps=4, cs_ps=4, tr_ps=4, sc_ps=4, y_ps=4, st_ps=4, o_ps=4).items()}
        s = {**dve, **act, **pool, **pe}

        passed_pool, passed_vector = (ctx.enter_context(nc.semaphore(n)) for n in ("passed_pool", "passed_vector"))

        block = ctx.enter_context(nc.Block())
        turn_banks = [p_in[1], p_tr, p_s, p_in[0]]
        dt_ps = p_in[0][:, 0:TILES * 2 * HEADS].rearrange("p (u e) -> p u e", u=TILES)

        def cxs(i, first, count):
            return cx[:, bass.ds((i % 2) * CX + first, count)]

        def c_of(i, u):
            return cxs(i, 2 * BT, HEADS * BT).rearrange("p (h t) -> p h t", h=HEADS)[:, :, u * P:(u + 1) * P]

        def z_of(i, u):
            v = zs[:, bass.ds((i % 2) * ZS, ZS)]
            return v.rearrange("p (h t) -> p h t", h=HEADS)[:, :, u * P:(u + 1) * P]

        def per_head(v):
            return v.rearrange("p (h o) -> p h o", o=1).broadcast_to([P, HEADS, P])

        def over_heads(v):
            return v.rearrange("p (o q) -> p o q", o=1).broadcast_to([P, HEADS, P])

        def flat(v):
            return v.rearrange("p h q -> p (h q)")

        x_blocks = x.rearrange("(b i c p) d -> b i p c d", b=BATCH, i=BLOCKS, c=CPB)

        @block.sync
        def _(sp):
            def load_x(i):
                for b in range(BATCH):
                    src = x_blocks[b, bass.ds(i, 1)].rearrange("o p c d -> (o p) c d")
                    sp.dma_start(xin[:, b * CPB:(b + 1) * CPB, :], src).then_inc(x_in.sem, 16)

            def load_xr(i, u):
                src = x_blocks[u // CPB, bass.ds(i, 1)].rearrange("o p c d -> (o p) c d")[:, u % CPB, :]
                sp.dma_start(xr[:, u, :], src).then_inc(xr_in[u].sem, 16)

            def store_h(i, q):
                u = ORDER[q]
                sp.wait_ge(s["h_made"].sem, s["h_made"].at(i, q + 1))
                sp.dma_start(h_scratch[bass.ds(i * TILES + u, 1)].rearrange("o p d -> (o p) d"), xr[:, u, :])\
                    .then_inc(h_out.sem, 16)

            def store_and_load(i, q):
                store_h(i, q)
                sp.wait_ge(h_out.sem, h_out.at(i, 16 * (q + 1)))
                load_xr(i + 1, ORDER[q])

            load_x(0)
            sp.dma_start(ln1_sb[:], ln1).then_inc(ln1_in.sem, 16)
            for k in range(KD):
                sp.dma_start(cx[:, k * D_PROJ:(k + 1) * D_PROJ], w_in[k * P:(k + 1) * P, :]).then_inc(win_in[k].sem, 16)
            sp.dma_start(cw_sb[:], conv_w).then_inc(par_in.sem, 16)
            sp.dma_start(cb_sb[:], conv_b).then_inc(par_in.sem, 16)
            for n, src in enumerate((a_log, d_skip, dt_bias)):
                sp.dma_start(head_sb[:, n, :], src).then_inc(par_in.sem, 16)
            sp.dma_start(zs[:, ZS:ZS + HEADS * D_MODEL].rearrange("p (h n) -> p h n", h=HEADS),
                         w_out.rearrange("(h p) n -> p h n", p=P)).then_inc(wout_in.sem, 16)
            for u in range(TILES):
                load_xr(0, u)

            def body(i, first, more):
                sp.wait_ge(s["zt_ps"].sem, s["zt_ps"].at(i))
                if more:
                    load_x(i + 1)
                else:
                    sp.dma_start(xin[:, :, :], h_scratch[0:TILES].rearrange("u p d -> p u d")).then_inc(x_in.sem, 16)
                if not first:
                    for q in range(1, TILES):
                        store_and_load(i - 1, q)
                if more:
                    store_and_load(i, 0)
                else:
                    sp.wait_ge(s["zt_ps"].sem, s["zt_ps"].at(BLOCKS))
                    for n, w in enumerate((gate, up)):
                        sp.dma_start(first_w[:, :, n, :], w[:, 0:2 * P].rearrange("(k p) f -> p k f", p=P))\
                            .then_inc(first_w_in.sem, 16)
                    sp.dma_start(ln2_first[:, :], ln2).then_inc(first_w_in.sem, 16)
                    store_h(i, 0)

            body(0, True, True)
            with nc.sync.Fori(1, BLOCKS - 1) as i:
                body(i, False, True)
            body(BLOCKS - 1, False, False)
            for q in range(1, TILES):
                store_h(BLOCKS - 1, q)
            sp.wait_ge(h_out.sem, h_out.at(BLOCKS - 1))

        @block.tensor
        def _(t):
            for v in pe.values():
                v.seed(t)

            def turn(j):
                for u in range(TILES):
                    t.wait_ge(s["normed"].sem, s["normed"].at(j, u + 1))
                    if u == 0:
                        t.wait_ge(s["in_out"].sem, s["in_out"].at(j - 1, NG - 1))
                    if u == 1:
                        t.wait_ge(s["xs_made"].sem, s["xs_made"].at(j - 1, 1))
                    if u == 2:
                        t.wait_ge(s["t2"].sem, s["t2"].at(j - 1, 1))
                    if u == 3:
                        t.wait_ge(s["in_out"].sem, s["in_out"].at(j - 1))
                    for k in range(KD):
                        ins = nc.tensor.transpose(turn_banks[u][:, k * P:(k + 1) * P], xin[:, u, k * P:(k + 1) * P],
                                                  ident[:, :])
                    ins.then_inc(s["zt_ps"].sem, 1)

            def project(j, groups):
                for g in groups:
                    kind, col, _ = IN_GROUPS[g]
                    if g == 0:
                        t.wait_ge(s["zt_lo_made"].sem, s["zt_lo_made"].at(j))
                    t.wait_ge(s["in_out"].sem, s["in_out"].at(j, max(g - 1, 0)))
                    if g == 2:
                        t.wait_ge(s["dt_abs"].sem, s["dt_abs"].at(j))
                    bank = p_in[g % 2]
                    if kind == "dt":
                        n = 0
                        for z in (zt_hi, zt_lo):
                            for k in range(KD):
                                ins = nc.tensor.matmul(bank[0:2 * HEADS, :], wdt[:, k, :], z[:, k, :],
                                                       start=(n == 0), stop=(n == 2 * KD - 1))
                                n += 1
                    else:
                        n = 0
                        for k in range(KD):
                            for l, r in split_passes(wi_hi, wi_lo, zt_hi, zt_lo):
                                ins = nc.tensor.matmul(bank[:, :], l[:, k, col:col + P], r[:, k, :],
                                                       start=(n == 0), stop=(n == 3 * KD - 1))
                                n += 1
                    ins.then_inc(s["in_ps"].sem, 1)

            def turn_dt(j):
                t.wait_ge(s["in_out"].sem, s["in_out"].at(j, 1))
                for u in range(TILES):
                    ins = nc.tensor.matmul(dt_ps[:, u, :], y32[0:2 * HEADS, u, :], ident[0:2 * HEADS, 0:2 * HEADS],
                                           start=True, stop=True)
                ins.then_inc(s["dt_turned"].sem, 1)

            def front(i, q, back_of=None):
                def scores():
                    t.wait_ge(s["c_hi_made"].sem, s["c_hi_made"].at(i, q + 1))
                    t.wait_ge(s["c_lo_made"].sem, s["c_lo_made"].at(i, q + 1))
                    t.wait_ge(s["b_hi_made"].sem, s["b_hi_made"].at(i, q + 1))
                    t.wait_ge(s["b_lo_made"].sem, s["b_lo_made"].at(i, q + 1))
                    t.wait_ge(s["t2"].sem, s["t2"].at(i, q))
                    for n, (l, r) in enumerate(split_passes(b_hi, b_lo, c_hi, c_lo)):
                        ins = nc.tensor.matmul(p_s[:, :], l[:, :], flat(r[:, :, :]), start=(n == 0), stop=(n == 2))
                    ins.then_inc(s["sc_ps"].sem, 1)

                t.wait_ge(s["r_made"].sem, s["r_made"].at(i, q + 1))
                t.wait_ge(s["ecs_made"].sem, s["ecs_made"].at(i, q))
                nc.tensor.matmul(p_d[:, :], after[:, :], flat(r_hi[:, :, :]), start=True, stop=False)
                nc.tensor.matmul(p_d[:, :], after[:, :], flat(r_lo[:, :, :]), start=False, stop=True)\
                    .then_inc(s["d_ps"].sem, 1)
                t.wait_ge(s["xb_copied"].sem, s["xb_copied"].at(i, q + 1))
                t.wait_ge(s["xs_made"].sem, s["xs_made"].at(i, q))
                for n in range(2):
                    ins = nc.tensor.transpose(p_tr[:, n * P:(n + 1) * P], xb32[:, n, :], ident[:, :])
                ins.then_inc(s["tr_ps"].sem, 1)
                if back_of is None:
                    scores()
                t.wait_ge(s["dec_made"].sem, s["dec_made"].at(i, q + 1))
                nc.tensor.matmul(p_d[:, :], ones[:, :], flat(r_hi[:, :, :]), start=True, stop=False)
                nc.tensor.matmul(p_d[:, :], ones[:, :], flat(r_lo[:, :, :]), start=False, stop=True)\
                    .then_inc(s["cs_ps"].sem, 1)
                if back_of is not None:
                    back(i, back_of)
                    scores()

            def back(i, q):
                t.wait_ge(s["xs_hi_made"].sem, s["xs_hi_made"].at(i, q + 1))
                t.wait_ge(s["xs_lo_made"].sem, s["xs_lo_made"].at(i, q + 1))
                t.wait_ge(s["s_updated"].sem, s["s_updated"].at(i, q))
                for n, (l, r) in enumerate(split_passes(xb_hi, xb_lo, xs_hi, xs_lo)):
                    ins = nc.tensor.matmul(p_st[:, :], l[:, q % 2, 1, :], flat(r[:, :, :]), start=(n == 0), stop=(n == 2))
                ins.then_inc(s["st_ps"].sem, 1)
                t.wait_ge(s["att_hi_made"].sem, s["att_hi_made"].at(i, q + 1))
                t.wait_ge(s["att_lo_made"].sem, s["att_lo_made"].at(i, q + 1))
                t.wait_ge(s["y_gated"].sem, s["y_gated"].at(i, q))
                for n, (l, r) in enumerate(split_passes(xb_hi, xb_lo, att_hi, att_lo)):
                    nc.tensor.matmul(p_y[:, :], l[:, q % 2, 0, :], flat(r[:, q % 2, :, :]), start=(n == 0), stop=False,
                                     skip_group_check=True)
                t.wait_ge(s["cp_hi_made"].sem, s["cp_hi_made"].at(i, q + 1))
                t.wait_ge(s["cp_lo_made"].sem, s["cp_lo_made"].at(i, q + 1))
                t.wait_ge(s["s_hi_made"].sem, s["s_hi_made"].at(i, q + 1))
                t.wait_ge(s["s_lo_made"].sem, s["s_lo_made"].at(i, q + 1))
                for h in range(HEADS):
                    for n, (l, r) in enumerate(split_passes(s_hi, s_lo, cp_hi, cp_lo)):
                        ins = nc.tensor.matmul(p_y[:, h * P:(h + 1) * P], l[:, q % 2, h, :], r[:, q % 2, h, :], start=False,
                                               stop=(h == HEADS - 1 and n == 2), skip_group_check=True)
                ins.then_inc(s["y_ps"].sem, 1)

            def output(i, q):
                t.wait_ge(wo_lo_made.sem, wo_lo_made.at(0, 1))
                t.wait_ge(s["y_hi_made"].sem, s["y_hi_made"].at(i, q + 1))
                t.wait_ge(s["y_lo_made"].sem, s["y_lo_made"].at(i, q + 1))
                t.wait_ge(s["h_made"].sem, s["h_made"].at(i, q))
                n = 0
                for h in range(HEADS):
                    for l, r in split_passes(y_hi, y_lo, wo_hi, wo_lo):
                        ins = nc.tensor.matmul(p_o[:, :], l[:, h, :], r[:, h, :], start=(n == 0), stop=(n == 3 * HEADS - 1))
                        n += 1
                ins.then_inc(s["o_ps"].sem, 1)

            def body(i, first, more):
                if not first:
                    front(i - 1, 3)
                    back(i - 1, 2)
                    project(i, IN_AT[3])
                    output(i - 1, 2)
                project(i, IN_AT[0][:1])
                if not first:
                    back(i, -1)
                front(i, 0)
                project(i, IN_AT[0][1:])
                turn(i + 1)
                if not first:
                    output(i, -1)
                if more:
                    project(i + 1, IN_AT[1][:1])
                else:
                    t.wait_ge(s["zt_lo_made"].sem, s["zt_lo_made"].at(i + 1))
                front(i, 1)
                if more:
                    turn_dt(i + 1)
                back(i, 0)
                if more:
                    project(i + 1, IN_AT[1][1:])
                    output(i, 0)
                front(i, 2, None if more else 1)
                if more:
                    back(i, 1)
                    project(i + 1, IN_AT[2])
                    output(i, 1)
                else:
                    output(i, 0)

            t.wait_ge(consts.sem, consts.at(0, 5))
            turn(0)
            t.wait_ge(wi_lo_made.sem, wi_lo_made.at(0, KD))
            t.wait_ge(wi_lo_pool.sem, wi_lo_pool.at(0, 2))
            project(0, IN_AT[1][:2])
            turn_dt(0)
            project(0, IN_AT[1][2:] + IN_AT[2] + IN_AT[3])
            body(0, True, True)
            with nc.tensor.Fori(1, BLOCKS - 1) as i:
                body(i, False, True)
            body(BLOCKS - 1, False, False)
            front(BLOCKS - 1, 3, 2)
            output(BLOCKS - 1, 1)
            back(BLOCKS - 1, 3)
            output(BLOCKS - 1, 2)
            output(BLOCKS - 1, 3)

        @block.scalar
        def _(a):
            for v in act.values():
                v.seed(a)

            def turn(j):
                for u in range(TILES):
                    a.wait_ge(s["zt_ps"].sem, s["zt_ps"].at(j, u + 1))
                    if u == 0:
                        a.wait_ge(s["in_ps"].sem, s["in_ps"].at(j - 1))
                    nc.scalar.copy(zt_hi[:, :, u * P:(u + 1) * P],
                                   turn_banks[u][:, :].rearrange("p (k t) -> p k t", k=KD))\
                                       .then_inc(s["zt_hi_made"].sem, 1)

            def evacuate(j, groups):
                for g in groups:
                    kind, _, n = IN_GROUPS[g]
                    a.wait_ge(s["in_ps"].sem, s["in_ps"].at(j, g + 1))
                    if kind == "dt":
                        a.wait_ge(s["y_lo_made"].sem, s["y_lo_made"].at(j - 1, 0))
                        ins = nc.scalar.copy(y32[0:2 * HEADS, :, :].rearrange("p u t -> p (u t)"), p_in[g % 2][0:2 * HEADS, :])
                    elif kind == "conv":
                        a.wait_ge(s["hist"].sem, s["hist"].at(j - 1))
                        ins = nc.scalar.copy(raw[:, n, :, TAPS - 1:], p_in[g % 2][:, :].rearrange("p (b t) -> p b t", b=BATCH))
                    else:
                        ins = nc.scalar.activation(zs[:, bass.ds((j % 2) * ZS + n * BT, BT)], p_in[g % 2][:, :], ACT.Silu)
                    ins.then_inc(s["in_out"].sem, 1)

            def dt_exp(j):
                a.wait_ge(s["dt_abs"].sem, s["dt_abs"].at(j))
                nc.scalar.activation(dtt[:, 2, :], dtt[:, 1, :], ACT.Exp, scale=-1.0).then_inc(s["dt_exp"].sem, 1)

            def silu(j, first, count):
                a.wait_ge(s["tap"].sem, s["tap"].at(j, TAPS * (first + count)))
                part = cxs(j, first * BT, count * BT)
                nc.scalar.activation(part, part, ACT.Silu).then_inc(s["silu_made"].sem, count)

            def prepare_b(i, q):
                a.wait_ge(s["sc_ps"].sem, s["sc_ps"].at(i, q))
                a.wait_ge(s["xb_copied"].sem, s["xb_copied"].at(i, q + 1))
                nc.scalar.copy(b_hi[:, :], xb32[:, 1, :]).then_inc(s["b_hi_made"].sem, 1)

            def prepare_c(i, q):
                if q == 0:
                    a.wait_ge(s["silu_made"].sem, s["silu_made"].at(i))
                nc.scalar.copy(c_hi[:, :, :], c_of(i, ORDER[q])).then_inc(s["c_hi_made"].sem, 1)

            def prepare(i, q):
                prepare_b(i, q)
                prepare_c(i, q)

            def front(i, q):
                b = ORDER[q] // CPB
                a.wait_ge(s["y_ps"].sem, s["y_ps"].at(i, q - 1))
                a.wait_ge(s["s_updated"].sem, s["s_updated"].at(i, q - 1))
                nc.scalar.copy(flat(s_hi[:, q % 2, :, :]), flat(state[:, b, :, :])).then_inc(s["s_hi_made"].sem, 1)
                a.wait_ge(s["d_ps"].sem, s["d_ps"].at(i, q + 1))
                a.wait_ge(s["t1"].sem, s["t1"].at(i, q))
                nc.scalar.activation(flat(dec[:, :, :]), p_d[:, :], ACT.Exp).then_inc(s["dec_made"].sem, 1)
                a.wait_ge(s["tr_ps"].sem, s["tr_ps"].at(i, q + 1))
                nc.scalar.copy(xb_hi[:, q % 2, :, :].rearrange("p n t -> p (n t)"), p_tr[:, 0:2 * P])\
                    .then_inc(s["xb_hi_made"].sem, 1)
                a.wait_ge(s["cs_ps"].sem, s["cs_ps"].at(i, q + 1))
                a.wait_ge(s["s_decayed"].sem, s["s_decayed"].at(i, q))
                nc.scalar.activation(flat(ecs[:, :, :]), p_d[:, :], ACT.Exp).then_inc(s["ecs_made"].sem, 1)

            def halves(i, q):
                a.wait_ge(s["xs_made"].sem, s["xs_made"].at(i, q + 1))
                a.wait_ge(s["st_ps"].sem, s["st_ps"].at(i, q))
                nc.scalar.copy(flat(xs_hi[:, :, :]), flat(xs32[:, :, :])).then_inc(s["xs_hi_made"].sem, 1)
                a.wait_ge(s["cp_made"].sem, s["cp_made"].at(i, q + 1))
                nc.scalar.copy(flat(cp_hi[:, q % 2, :, :]), flat(cp32[:, :, :])).then_inc(s["cp_hi_made"].sem, 1)
                a.wait_ge(s["att_made"].sem, s["att_made"].at(i, q + 1))
                nc.scalar.copy(flat(att_hi[:, q % 2, :, :]), flat(att32[:, :, :])).then_inc(s["att_hi_made"].sem, 1)

            def back(i, q):
                a.wait_ge(s["y_gated"].sem, s["y_gated"].at(i, q + 1))
                a.wait_ge(s["o_ps"].sem, s["o_ps"].at(i, q))
                nc.scalar.copy(flat(y_hi[:, :, :]), flat(y32[:, :, :])).then_inc(s["y_hi_made"].sem, 1)

            def activate(j):
                silu(j, 0, 4)
                prepare_b(j, 0)
                silu(j, 4, 1)
                silu(j, 5, 1)
                prepare_c(j, 0)

            def body(i, first, more):
                if not first:
                    front(i - 1, 3)
                    halves(i - 1, 3)
                    evacuate(i, IN_AT[3][:1])
                    back(i - 1, 2)
                    evacuate(i, IN_AT[3][1:])
                    activate(i)
                evacuate(i, IN_AT[0][:1])
                front(i, 0)
                if not first:
                    back(i, -1)
                halves(i, 0)
                evacuate(i, IN_AT[0][1:])
                turn(i + 1)
                prepare(i, 1)
                if more:
                    evacuate(i + 1, IN_AT[1][:1])
                front(i, 1)
                halves(i, 1)
                if more:
                    dt_exp(i + 1)
                    back(i, 0)
                prepare(i, 2)
                if more:
                    evacuate(i + 1, IN_AT[1][1:])
                else:
                    back(i, 0)
                front(i, 2)
                halves(i, 2)
                if more:
                    evacuate(i + 1, IN_AT[2][:1])
                    back(i, 1)
                prepare(i, 3)
                if more:
                    evacuate(i + 1, IN_AT[2][1:])
                else:
                    back(i, 1)

            wv = cx[:, 0:KD * D_PROJ].rearrange("p (k n) -> p k n", k=KD)

            def split_w(k):
                a.wait_ge(win_scaled.sem, win_scaled.at(0, k + 1))
                nc.scalar.copy(wi_hi[:, k, :], wv[:, k, 0:NW])
                nc.scalar.copy(wdt[:, k, 0:HEADS], wv[:, k, NW:D_PROJ]).then_inc(wi_hi_made.sem, 1)

            for k in range(KD):
                split_w(k)
            turn(0)
            a.wait_ge(par_in.sem, par_in.at(0, 5 * 16))
            nc.scalar.activation(neg_a[:, :], head_sb[:, 0, :], ACT.Exp).then_inc(neg_a_made.sem, 1)
            evacuate(0, IN_AT[1][:1])
            dt_exp(0)
            evacuate(0, IN_AT[1][1:])
            evacuate(0, IN_AT[2])
            a.wait_ge(wout_in.sem, wout_in.at(0, 16))
            nc.scalar.copy(wo_flat[0], zs[:, ZS:ZS + HEADS * D_MODEL])\
                .then_inc(wo_hi_made.sem, 1)
            evacuate(0, IN_AT[3])
            activate(0)
            body(0, True, True)
            with nc.scalar.Fori(1, BLOCKS - 1) as i:
                body(i, False, True)
            body(BLOCKS - 1, False, False)
            last = BLOCKS - 1
            front(last, 3)
            halves(last, 3)
            back(last, 2)
            a.wait_ge(first_w_scaled.sem, first_w_scaled.at(0, KD))
            for f in range(2):
                for w in range(2):
                    nc.scalar.copy(gu[0][:, f, :, w, :], first_w[:, :, w, f * P:(f + 1) * P])\
                        .then_inc(first_w_hi.sem, 1)
            back(last, 3)

        @block.gpsimd
        def _(g):
            for v in pool.values():
                v.seed(g)
            nc.gpsimd.memset(ident[:, :], 0.0).then_inc(mask_made.sem, 1)
            nc.gpsimd.memset(upper[:, :], 1.0).then_inc(mask_made.sem, 1)
            nc.gpsimd.memset(after_f, 1.0).then_inc(mask_made.sem, 1)
            nc.gpsimd.memset(ones_f, 1.0).then_inc(mask_made.sem, 1)
            nc.gpsimd.memset(mhalf[:, :], -0.5).then_inc(consts.sem, 1)
            g.wait_ge(mask_made.sem, mask_made.at(0, 4))
            nc.gpsimd.affine_select(out=ident[:, :], in_=ident[:, :], compare_op=ALU.not_equal, fill=1.0, base=0,
                                    pattern=[[-1, P]], channel_multiplier=1).then_inc(consts.sem, 1)
            nc.gpsimd.affine_select(out=upper[:, :], in_=upper[:, :], compare_op=ALU.is_ge, fill=0.0, base=0,
                                    pattern=[[1, P]], channel_multiplier=-1).then_inc(consts.sem, 1)
            nc.gpsimd.affine_select(out=after_f, in_=after_f, compare_op=ALU.is_gt, fill=0.0, base=0,
                                    pattern=[[-1, P]], channel_multiplier=1).then_inc(mask_made.sem, 1)
            g.wait_ge(mask_made.sem, mask_made.at(0, 5))
            nc.gpsimd.tensor_copy(after[:, :], after_f).then_inc(consts.sem, 1)
            nc.gpsimd.tensor_copy(ones[:, :], ones_f).then_inc(consts.sem, 1)

            def do_rms(j, mean, var):
                square, power, shifted = lt[:, 0, :], lt[:, 1, :], lt[:, 2, :]
                nc.gpsimd.tensor_tensor(square, mean, mean, ALU.mult).then_inc(s["ln_step"].sem, 1)
                g.wait_ge(s["ln_step"].sem, s["ln_step"].at(j, 1))
                nc.gpsimd.tensor_tensor(power, square, var, ALU.add).then_inc(s["ln_step"].sem, 1)
                g.wait_ge(s["ln_step"].sem, s["ln_step"].at(j, 2))
                nc.gpsimd.tensor_scalar(shifted, power, EPS, 1.0, ALU.add, ALU.mult).then_inc(s["ln_step"].sem, 1)
                g.wait_ge(s["ln_step"].sem, s["ln_step"].at(j, 3))
                nc.gpsimd.tensor_tensor(lz[:, 0, :], shifted, mhalf[:, :], ALU.pow).then_inc(s["ln_scale"].sem, 1)

            def norm_scales(j):
                g.wait_ge(s["mean_var"].sem, s["mean_var"].at(j))
                g.wait_ge(s["normed"].sem, s["normed"].at(j - 1))
                waits_apart(g, passed_pool)
                mean, var = mv[:, :, 0], mv[:, :, 1]
                ve, rstd, t1, t2, t3, r1, m1, m2 = (lt[:, n, :] for n in range(8))
                n = [0]

                if is_last(j):
                    do_rms(j, mean, var)
                    return

                def do(ins):
                    n[0] += 1
                    ins.then_inc(s["ln_step"].sem, 1)

                def after_all():
                    g.wait_ge(s["ln_step"].sem, s["ln_step"].at(j, n[0]))
                    waits_apart(g, passed_pool)

                keep = lnk[:, bass.ds(j * 2 * TILES, 2 * TILES)]
                do(nc.gpsimd.tensor_scalar(ve, var, EPS, 1.0, ALU.add, ALU.mult))
                after_all()
                do(nc.gpsimd.tensor_tensor(rstd, ve, mhalf[:, :], ALU.pow))
                after_all()
                do(nc.gpsimd.tensor_tensor(t1, var, rstd, ALU.mult))
                do(nc.gpsimd.tensor_tensor(m1, mean, rstd, ALU.mult))
                after_all()
                do(nc.gpsimd.tensor_tensor(t2, t1, rstd, ALU.mult))
                do(nc.gpsimd.tensor_scalar(m2, m1, -1.0, 1.0, ALU.mult, ALU.mult))
                after_all()
                do(nc.gpsimd.tensor_scalar(t3, t2, EPS, 1.0, ALU.add, ALU.mult))
                do(nc.gpsimd.tensor_copy(keep[:, 0:TILES], rstd))
                after_all()
                do(nc.gpsimd.tensor_tensor(r1, t3, mhalf[:, :], ALU.pow))
                do(nc.gpsimd.tensor_copy(keep[:, TILES:2 * TILES], m2))
                after_all()
                do(nc.gpsimd.tensor_tensor(lz[:, 0, :], rstd, r1, ALU.mult))
                nc.gpsimd.tensor_tensor(lz[:, 1, :], m2, r1, ALU.mult).then_inc(s["ln_scale"].sem, 1)

            def decays(i, q):
                u = ORDER[q]
                hs = slice(u * HEADS, (u + 1) * HEADS)
                if q == 0:
                    g.wait_ge(s["dt_ready"].sem, s["dt_ready"].at(i))
                g.wait_ge(s["cs_ps"].sem, s["cs_ps"].at(i, q))
                nc.gpsimd.tensor_tensor(r_hi[:, :, :], over_heads(upper[:, :]), per_head(a_hi[:, hs].bitcast(F32)), ALU.mult)
                nc.gpsimd.tensor_tensor(r_lo[:, :, :], over_heads(upper[:, :]), per_head(a_lo[:, hs]), ALU.mult)\
                    .then_inc(s["r_made"].sem, 1)

            def prepare(i, q):
                u = ORDER[q]
                hs = slice(u * HEADS, (u + 1) * HEADS)
                g.wait_ge(s["t1"].sem, s["t1"].at(i, q))
                nc.gpsimd.tensor_tensor(mdt[:, :, :], over_heads(upper[:, :]), per_head(dtv[:, hs]), ALU.mult)\
                    .then_inc(s["mdt_made"].sem, 1)
                g.wait_ge(s["b_hi_made"].sem, s["b_hi_made"].at(i, q + 1))
                nc.gpsimd.tensor_tensor(b_lo[:, :], xb32[:, 1, :], b_hi[:, :].bitcast(F32), ALU.subtract)\
                    .then_inc(s["b_lo_made"].sem, 1)
                g.wait_ge(s["c_hi_made"].sem, s["c_hi_made"].at(i, q + 1))
                waits_apart(g, passed_pool)
                nc.gpsimd.tensor_tensor(c_lo[:, :, :], c_of(i, u), c_hi[:, :, :].bitcast(F32), ALU.subtract)\
                    .then_inc(s["c_lo_made"].sem, 1)

            def front(i, q):
                u = ORDER[q]
                g.wait_ge(s["ecs_made"].sem, s["ecs_made"].at(i, q + 1))
                g.wait_ge(s["cp_hi_made"].sem, s["cp_hi_made"].at(i, q))
                waits_apart(g, passed_pool)
                nc.gpsimd.tensor_tensor(cp32[:, :, :], c_of(i, u), ecs[:, :, :], ALU.mult).then_inc(s["cp_made"].sem, 1)
                g.wait_ge(s["xs_hi_made"].sem, s["xs_hi_made"].at(i, q + 1))
                nc.gpsimd.tensor_tensor(flat(xs_lo[:, :, :]), flat(xs32[:, :, :]), flat(xs_hi[:, :, :].bitcast(F32)),
                                        ALU.subtract).then_inc(s["xs_lo_made"].sem, 1)
                g.wait_ge(s["cp_hi_made"].sem, s["cp_hi_made"].at(i, q + 1))
                nc.gpsimd.tensor_tensor(flat(cp_lo[:, q % 2, :, :]), flat(cp32[:, :, :]),
                                        flat(cp_hi[:, q % 2, :, :].bitcast(F32)), ALU.subtract)\
                                            .then_inc(s["cp_lo_made"].sem, 1)
                if q + 1 < TILES:
                    decays(i, q + 1)
                g.wait_ge(s["att_hi_made"].sem, s["att_hi_made"].at(i, q + 1))
                nc.gpsimd.tensor_tensor(flat(att_lo[:, q % 2, :, :]), flat(att32[:, :, :]),
                                        flat(att_hi[:, q % 2, :, :].bitcast(F32)), ALU.subtract)\
                                            .then_inc(s["att_lo_made"].sem, 1)
                g.wait_ge(s["s_lo_made"].sem, s["s_lo_made"].at(i, q + 1))
                decay = ecs[:, :, P - 1:P].broadcast_to([P, HEADS, P])
                nc.gpsimd.tensor_tensor(state[:, u // CPB, :, :], state[:, u // CPB, :, :], decay, ALU.mult)\
                    .then_inc(s["s_decayed"].sem, 1)

            def body(i, first, more):
                if not first:
                    front(i - 1, 3)
                    decays(i, 0)
                    prepare(i, 0)
                norm_scales(i + 1)
                front(i, 0)
                prepare(i, 1)
                front(i, 1)
                prepare(i, 2)
                front(i, 2)
                prepare(i, 3)

            g.wait_ge(consts.sem, consts.at(0, 5))
            norm_scales(0)
            wv = cx[:, 0:KD * D_PROJ].rearrange("p (k n) -> p k n", k=KD)
            for k in range(1, KD, 2):
                g.wait_ge(wi_hi_made.sem, wi_hi_made.at(0, k + 1))
                nc.gpsimd.tensor_tensor(wi_lo[:, k, :], wv[:, k, 0:NW], wi_hi[:, k, :].bitcast(F32), ALU.subtract)\
                    .then_inc(wi_lo_pool.sem, 1)
            g.wait_ge(wo_hi_made.sem, wo_hi_made.at(0, 1))
            nc.gpsimd.tensor_tensor(wo_flat[1], zs[:, ZS:ZS + HEADS * D_MODEL], wo_flat[0].bitcast(F32), ALU.subtract)\
                .then_inc(wo_lo_made.sem, 1)
            decays(0, 0)
            prepare(0, 0)
            body(0, True, True)
            with nc.gpsimd.Fori(1, BLOCKS - 1) as i:
                body(i, False, True)
            body(BLOCKS - 1, False, False)
            front(BLOCKS - 1, 3)

        @block.vector
        def _(v):
            for e in dve.values():
                e.seed(v)

            def stats(j):
                v.wait_ge(x_in.sem, x_in.at(j, 16) if is_last(j) else x_in.at(j))
                v.wait_ge(s["ln_scale"].sem, s["ln_scale"].at(j - 1))
                for u in range(TILES):
                    nc.vector.bn_stats(bn[:, u, :], xin[:, u, :]).then_inc(s["bn_made"].sem, 1)
                for u in range(TILES):
                    v.wait_ge(s["bn_made"].sem, s["bn_made"].at(j, u + 1))
                    waits_apart(v, passed_vector)
                    nc.vector.bn_aggr(mv[:, u, :], bn[:, u, :]).then_inc(s["mean_var"].sem, 1)

            def normalise(j):
                v.wait_ge(s["ln_scale"].sem, s["ln_scale"].at(j))
                for u in range(TILES):
                    if is_last(j):
                        nc.vector.tensor_scalar(xin[:, u, :], xin[:, u, :], lz[:, 0, u:u + 1], None, ALU.mult)\
                            .then_inc(s["normed"].sem, 1)
                        continue
                    nc.vector.tensor_scalar(xin[:, u, :], xin[:, u, :], lz[:, 0, u:u + 1], lz[:, 1, u:u + 1],
                                            ALU.mult, ALU.add).then_inc(s["normed"].sem, 1)

            def turn(j):
                for u in range(TILES):
                    v.wait_ge(s["zt_hi_made"].sem, s["zt_hi_made"].at(j, u + 1))
                    cols = slice(u * P, (u + 1) * P)
                    nc.vector.tensor_tensor(zt_lo[:, :, cols], turn_banks[u][:, :].rearrange("p (k t) -> p k t", k=KD),
                                            zt_hi[:, :, cols].bitcast(F32), ALU.subtract)\
                                                .then_inc(s["zt_lo_made"].sem, 1)

            def convolve(j, groups):
                for g in groups:
                    n = IN_GROUPS[g][2]
                    acc = cxs(j, n * BT, BT).rearrange("p (b t) -> p b t", b=BATCH)
                    v.wait_ge(s["in_out"].sem, s["in_out"].at(j, g + 1))
                    if g == 1:
                        v.wait_ge(s["cp_made"].sem, s["cp_made"].at(j - 2))
                    waits_apart(v, passed_vector)
                    nc.vector.tensor_scalar(acc, raw[:, n, :, 0:CW], cw_sb[:, n, 0:1], cb_sb[:, n:n + 1],
                                            ALU.mult, ALU.add).then_inc(s["tap"].sem, 1)
                    for k in range(1, TAPS):
                        v.wait_ge(s["tap"].sem, s["tap"].at(j, (g - 1) * TAPS + k))
                        waits_apart(v, passed_vector)
                        nc.vector.scalar_tensor_tensor(out=acc, in0=raw[:, n, :, k:k + CW], scalar=cw_sb[:, n, k:k + 1],
                                                       in1=acc, op0=ALU.mult, op1=ALU.add).then_inc(s["tap"].sem, 1)

            def keep_history(j):
                v.wait_ge(s["tap"].sem, s["tap"].at(j))
                nc.vector.tensor_copy(raw[:, :, :, 0:TAPS - 1].rearrange("p n b t -> p (n b) t"),
                                      raw[:, :, :, CW:].rearrange("p n b t -> p (n b) t")).then_inc(s["hist"].sem, 1)

            xd, ax, ed, t3, t4, t5, t6, t7 = (dtt[:, n, :] for n in range(8))
            dt_tail = s["dt_tail"]

            def chain(j, n, ins):
                ins.then_inc(s["dt_step"].sem, 1)
                v.wait_ge(s["dt_step"].sem, s["dt_step"].at(j, n))

            def dt_start(j):
                v.wait_ge(s["dt_turned"].sem, s["dt_turned"].at(j))
                x3 = xd.rearrange("p (u h) -> p u h", u=TILES)
                bias = head_sb[:, 2:3, :].broadcast_to([P, TILES, HEADS])
                chain(j, 1, nc.vector.tensor_tensor(x3, dt_ps[:, :, 0:HEADS], bias, ALU.add))
                chain(j, 2, nc.vector.tensor_tensor(x3, dt_ps[:, :, HEADS:], x3, ALU.add))
                nc.vector.scalar_tensor_tensor(out=ax, in0=xd, scalar=-1.0, in1=xd, op0=ALU.mult, op1=ALU.max)\
                    .then_inc(s["dt_abs"].sem, 1)

            def dt_finish(j):
                v.wait_ge(s["dt_exp"].sem, s["dt_exp"].at(j))
                chain(j, 3, nc.vector.tensor_scalar(t3, ed, 2.0, None, ALU.add))
                chain(j, 4, nc.vector.reciprocal(t4, t3))
                chain(j, 5, nc.vector.tensor_tensor(t5, ed, t4, ALU.mult))
                chain(j, 6, nc.vector.tensor_tensor(t6, t5, t5, ALU.mult))
                terms = [1.0 / (2 * k + 1) for k in range(1, 8)]
                nc.vector.tensor_scalar(t7, t6, terms[-1], None, ALU.mult).then_inc(s["dt_step"].sem, 1)
                n = 7
                for c in reversed(terms[:-1]):
                    v.wait_ge(s["dt_step"].sem, s["dt_step"].at(j, n))
                    nc.vector.scalar_tensor_tensor(out=t7, in0=t7, scalar=c, in1=t6, op0=ALU.add, op1=ALU.mult)\
                        .then_inc(s["dt_step"].sem, 1)
                    n += 1
                v.wait_ge(s["dt_step"].sem, s["dt_step"].at(j, n))
                nc.vector.scalar_tensor_tensor(out=t7, in0=t7, scalar=1.0, in1=t5, op0=ALU.add, op1=ALU.mult)\
                    .then_inc(s["dt_step"].sem, 1)
                v.wait_ge(s["dt_step"].sem, s["dt_step"].at(j, n + 1))
                assert n + 1 == s["dt_step"].per

            def dt_write(j):
                v.wait_ge(s["mdt_made"].sem, s["mdt_made"].at(j - 1))
                v.wait_ge(s["wd_made"].sem, s["wd_made"].at(j - 1))
                nc.vector.tensor_scalar(t3, xd, 0.0, None, ALU.max).then_inc(dt_tail.sem, 1)
                v.wait_ge(dt_tail.sem, dt_tail.at(j, 1))
                nc.vector.scalar_tensor_tensor(out=dtv[:, :], in0=t7, scalar=2.0, in1=t3, op0=ALU.mult, op1=ALU.add)\
                    .then_inc(dt_tail.sem, 1)
                v.wait_ge(dt_tail.sem, dt_tail.at(j, 2))
                nc.vector.scalar_tensor_tensor(
                    out=t4.rearrange("p (u h) -> p u h", u=TILES), in0=dtv[:, :].rearrange("p (u h) -> p u h", u=TILES),
                    scalar=-1.0, in1=neg_a[:, :].rearrange("p (o h) -> p o h", o=1).broadcast_to([P, TILES, HEADS]),
                    op0=ALU.mult, op1=ALU.mult).then_inc(dt_tail.sem, 1)
                v.wait_ge(dt_tail.sem, dt_tail.at(j, 3))
                nc.vector.tensor_copy(a_hi[:, :], t4).then_inc(dt_tail.sem, 1)
                v.wait_ge(dt_tail.sem, dt_tail.at(j, 4))
                nc.vector.tensor_tensor(a_lo[:, :], t4, a_hi[:, :].bitcast(F32), ALU.subtract)\
                    .then_inc(s["dt_ready"].sem, 1)

            def prepare(i, q):
                u = ORDER[q]
                if q == 0:
                    v.wait_ge(s["silu_made"].sem, s["silu_made"].at(i, 2))
                v.wait_ge(s["tr_ps"].sem, s["tr_ps"].at(i, q))
                v.wait_ge(s["b_lo_made"].sem, s["b_lo_made"].at(i, q))
                waits_apart(v, passed_vector)
                nc.vector.tensor_copy(xb32[:, :, :], cxs(i, 0, 2 * BT).rearrange("p (n t) -> p n t", n=2)[:, :, u * P:(u + 1) * P])\
                    .then_inc(s["xb_copied"].sem, 1)

            def take_state(i, q):
                v.wait_ge(s["s_hi_made"].sem, s["s_hi_made"].at(i, q + 1))
                nc.vector.tensor_tensor(flat(s_lo[:, q % 2, :, :]), flat(state[:, ORDER[q] // CPB, :, :]),
                                        flat(s_hi[:, q % 2, :, :].bitcast(F32)), ALU.subtract)\
                                            .then_inc(s["s_lo_made"].sem, 1)

            def front(i, q):
                u = ORDER[q]
                v.wait_ge(s["xb_hi_made"].sem, s["xb_hi_made"].at(i, q + 1))
                nc.vector.tensor_tensor(xb_lo[:, q % 2, :, :].rearrange("p n t -> p (n t)"), p_tr[:, 0:2 * P],
                                        xb_hi[:, q % 2, :, :].rearrange("p n t -> p (n t)").bitcast(F32), ALU.subtract)\
                    .then_inc(s["xb_lo_made"].sem, 1)
                v.wait_ge(s["dec_made"].sem, s["dec_made"].at(i, q + 1))
                v.wait_ge(s["dt_ready"].sem, s["dt_ready"].at(i))
                v.wait_ge(s["xs_made"].sem, s["xs_made"].at(i, q))
                nc.vector.tensor_tensor(wd[:, :], dec[:, :, P - 1], dtv[:, u * HEADS:(u + 1) * HEADS], ALU.mult)\
                    .then_inc(s["wd_made"].sem, 1)
                v.wait_ge(s["wd_made"].sem, s["wd_made"].at(i, q + 1))
                v.wait_ge(s["xs_lo_made"].sem, s["xs_lo_made"].at(i, q))
                nc.vector.tensor_tensor(xs32[:, :, :], over_heads(p_tr[:, 0:P]), per_head(wd[:, :]), ALU.mult)\
                    .then_inc(s["xs_made"].sem, 1)
                v.wait_ge(s["mdt_made"].sem, s["mdt_made"].at(i, q + 1))
                v.wait_ge(s["att_lo_made"].sem, s["att_lo_made"].at(i, q))
                nc.vector.tensor_tensor(flat(att32[:, :, :]), flat(dec[:, :, :]), flat(mdt[:, :, :]), ALU.mult)\
                    .then_inc(s["t1"].sem, 1)
                v.wait_ge(s["t1"].sem, s["t1"].at(i, q + 1))
                v.wait_ge(s["sc_ps"].sem, s["sc_ps"].at(i, q + 1))
                nc.vector.tensor_tensor(flat(att32[:, :, :]), p_s[:, :], flat(att32[:, :, :]), ALU.mult)\
                    .then_inc(s["t2"].sem, 1)
                v.wait_ge(s["t2"].sem, s["t2"].at(i, q + 1))
                for h in range(HEADS):
                    ins = nc.vector.scalar_tensor_tensor(out=att32[:, h, :], in0=ident[:, :], scalar=head_sb[:, 1, h:h + 1],
                                                         in1=att32[:, h, :], op0=ALU.mult, op1=ALU.add)
                ins.then_inc(s["att_made"].sem, 1)

            def back(i, q):
                b = ORDER[q] // CPB
                v.wait_ge(s["st_ps"].sem, s["st_ps"].at(i, q + 1))
                v.wait_ge(s["s_decayed"].sem, s["s_decayed"].at(i, q + 1))
                sv = flat(state[:, b, :, :])
                nc.vector.tensor_tensor(sv, p_st[:, :], sv, ALU.add).then_inc(s["s_updated"].sem, 1)
                v.wait_ge(s["y_ps"].sem, s["y_ps"].at(i, q + 1))
                v.wait_ge(s["y_hi_made"].sem, s["y_hi_made"].at(i, q))
                v.wait_ge(s["y_lo_made"].sem, s["y_lo_made"].at(i, q))
                waits_apart(v, passed_vector)
                j, u = (i, ORDER[q]) if q >= 0 else (i - 1, ORDER[q + TILES])
                nc.vector.tensor_tensor(y32[:, :, :], p_y[:, :].rearrange("p (h t) -> p h t", h=HEADS), z_of(j, u), ALU.mult)\
                    .then_inc(s["y_gated"].sem, 1)

            def low_y(i, q):
                v.wait_ge(s["y_hi_made"].sem, s["y_hi_made"].at(i, q + 1))
                nc.vector.tensor_tensor(flat(y_lo[:, :, :]), flat(y32[:, :, :]), flat(y_hi[:, :, :].bitcast(F32)),
                                        ALU.subtract).then_inc(s["y_lo_made"].sem, 1)

            def output(i, q):
                j, n = (i, q) if q >= 0 else (i - 1, q + TILES)
                u = ORDER[n]
                v.wait_ge(xr_in[u].sem, xr_in[u].at(j))
                waits_apart(v, passed_vector)
                keep = lnk[:, bass.ds(j * 2 * TILES, 2 * TILES)]
                nc.vector.tensor_scalar(xr[:, u, :], xr[:, u, :], keep[:, u:u + 1], keep[:, TILES + u:TILES + u + 1],
                                        ALU.mult, ALU.add).then_inc(s["xhat"].sem, 1)
                v.wait_ge(s["xhat"].sem, s["xhat"].at(i, q + 1))
                v.wait_ge(s["o_ps"].sem, s["o_ps"].at(i, q + 1))
                nc.vector.tensor_tensor(xr[:, u, :], p_o[:, :], xr[:, u, :], ALU.add).then_inc(s["h_made"].sem, 1)

            def rest(i, q, before=2):
                if before:
                    back(i, q - 1)
                if before > 1:
                    output(i, q - 2)
                if before:
                    low_y(i, q - 1)

            def body(i, first, more):
                if not first:
                    take_state(i - 1, 3)
                    front(i - 1, 3)
                    rest(i - 1, 3)
                    dt_write(i)
                    convolve(i, CONV_AT[3][:-1])
                    prepare(i, 0)
                    convolve(i, CONV_AT[3][-1:])
                    keep_history(i)
                stats(i + 1)
                if not first:
                    back(i, -1)
                take_state(i, 0)
                front(i, 0)
                normalise(i + 1)
                if not first:
                    low_y(i, -1)
                    output(i, -2)
                prepare(i, 1)
                turn(i + 1)
                take_state(i, 1)
                front(i, 1)
                if more:
                    dt_start(i + 1)
                if more:
                    rest(i, 1, 1 if first else 2)
                prepare(i, 2)
                if not more:
                    rest(i, 1)
                if more:
                    dt_finish(i + 1)
                    convolve(i + 1, CONV_AT[1])
                take_state(i, 2)
                front(i, 2)
                if more:
                    rest(i, 2)
                prepare(i, 3)
                if not more:
                    rest(i, 2)
                if more:
                    convolve(i + 1, CONV_AT[2])

            nc.vector.memset(raw[:, :, :, 0:TAPS - 1], 0.0).then_inc(zeroed.sem, 1)
            nc.vector.memset(state[:, :, :, :], 0.0).then_inc(zeroed.sem, 1)
            stats(0)
            v.wait_ge(ln1_in.sem, ln1_in.at(0, 16))
            wv = cx[:, 0:KD * D_PROJ].rearrange("p (k n) -> p k n", k=KD)

            def scale_w(k):
                v.wait_ge(win_in[k].sem, win_in[k].at(0, 16))
                nc.vector.tensor_scalar(wv[:, k, :], wv[:, k, :], ln1_sb[:, k:k + 1], None, ALU.mult)\
                    .then_inc(win_scaled.sem, 1)

            def low_w(k):
                v.wait_ge(wi_hi_made.sem, wi_hi_made.at(0, k + 1))
                if k % 2 == 0:
                    nc.vector.tensor_tensor(wi_lo[:, k, :], wv[:, k, 0:NW], wi_hi[:, k, :].bitcast(F32), ALU.subtract)
                nc.vector.tensor_tensor(wdt[:, k, HEADS:], wv[:, k, NW:D_PROJ], wdt[:, k, 0:HEADS].bitcast(F32), ALU.subtract)\
                    .then_inc(wi_lo_made.sem, 1)

            scale_w(0)
            scale_w(1)
            low_w(0)
            scale_w(2)
            scale_w(3)
            normalise(0)
            low_w(1)
            low_w(2)
            low_w(3)
            turn(0)
            v.wait_ge(par_in.sem, par_in.at(0, 5 * 16))
            dt_start(0)
            v.wait_ge(neg_a_made.sem, neg_a_made.at(0, 1))
            v.wait_ge(zeroed.sem, zeroed.at(0, 2))
            v.wait_ge(wi_lo_made.sem, wi_lo_made.at(0, KD))
            v.wait_ge(wi_lo_pool.sem, wi_lo_pool.at(0, 2))
            dt_finish(0)
            dt_write(0)
            convolve(0, range(1, CONV))
            prepare(0, 0)
            convolve(0, [CONV])
            keep_history(0)
            body(0, True, True)
            with nc.vector.Fori(1, BLOCKS - 1) as i:
                body(i, False, True)
            body(BLOCKS - 1, False, False)
            last = BLOCKS - 1
            take_state(last, 3)
            front(last, 3)
            rest(last, 3)
            v.wait_ge(first_w_in.sem, first_w_in.at(0, 3 * 16))
            for k in range(KD):
                nc.vector.tensor_scalar(xin[:, k, :], xin[:, k, :], ln2_first[:, k:k + 1], None, ALU.mult)\
                    .then_inc(first_w_scaled.sem, 1)
            back(last, 3)
            output(last, 2)
            low_y(last, 3)
            for f in range(2):
                for w in range(2):
                    v.wait_ge(first_w_hi.sem, first_w_hi.at(0, 2 * f + w + 1))
                    nc.vector.tensor_tensor(gu[1][:, f, :, w, :], first_w[:, :, w, f * P:(f + 1) * P],
                                            gu[0][:, f, :, w, :].bitcast(F32), ALU.subtract)
            output(last, 3)


def mlp_phase(nc, x, ln2, gate, up, down, lora_a, lora_b, w_ffn, ffn_bias, lora_coef, h_scratch, out, turned, split,
              gu):
    with ExitStack() as ctx:
        def sb(name, shape, dt=F32):
            return ctx.enter_context(nc.sbuf_tensor(name, shape, dt))

        def psum(name):
            return ctx.enter_context(nc.psum_tensor(name, [P, 512], F32))

        def sig(name, per, seeded=True):
            return Signal(nc, ctx, name, per, seeded)

        D = D_MODEL
        PIECE = 2
        PIECES = FT // PIECE
        w_gu = sb("w_gu", [P, KD, 2, INTER])
        w_dn = sb("w_dn", [P, FT, D])
        gu_hi, gu_lo = gu
        dn_hi, dn_lo = (v[:, 8 * KD * P:8 * KD * P + 2 * D].rearrange("p (f d) -> p f d", f=2) for v in split)
        ZT = KD * BT
        zt_hi, zt_lo = turned
        hz = sb("hz", [P, 2, D])
        g32, m32 = sb("g32", [P, BT]), sb("m32", [P, BT])
        m_hi, m_lo = sb("m_hi", [P, 2, BT], F32R), sb("m_lo", [P, 2, BT], F32R)
        hr = sb("hr", [P, TILES, D])
        x1 = sb("x1", [P, TILES, D])
        z3 = sb("z3", [P, D])
        z3t_hi, z3t_lo = sb("z3t_hi", [P, KD, P], F32R), sb("z3t_lo", [P, KD, P], F32R)
        fo = sb("fo", [P, D])
        we_hi, we_lo = (split[1][:, n * KD * D:(n + 1) * KD * D].rearrange("p (k d) -> p k d", k=KD) for n in range(2))
        bias = sb("bias", [P, D])
        ident = sb("ident2", [P, P])
        ln2_sb, coef = sb("ln2_sb", [P, KD]), sb("coef", [P, 1])
        mhalf = sb("mhalf2", [P, TILES])
        bn = sb("bn2", [P, 4, TILES, 6])
        mv = sb("mv2", [P, 4, TILES, 2])
        tmp = sb("tmp", [P, 4, 4, TILES])
        scl = sb("scl", [P, 4, 2, TILES])

        p_g, p_u, p_x, p_f = (psum(n) for n in ("p_g", "p_u", "p_x", "p_f"))
        p_m = [psum(f"p_m{u}") for u in range(TILES)]

        par_in, lora_in, wt_in = (sig(n, 1, False) for n in ("par2_in", "lora_in", "wt_in"))
        piece_in = [sig(f"piece_in{c}", 1, False) for c in range(PIECES)]
        hz_in = [sig(f"hz_in{n}", 16 * TILES // 2, False) for n in range(2)]
        hr_in, x1_in = sig("hr_in", 16, False), sig("x1_in", 32, False)
        out_done = sig("out_done", 16 * TILES)
        consts, ident_zero = sig("consts2", 1, False), sig("ident_zero", 1, False)
        w_scaled, lora_scaled, lora_ps, lora_added, we_hi_made, we_lo_made = (
            sig(n, 1, False) for n in ("w_scaled", "lora_scaled", "lora_ps", "lora_added", "we_hi_made", "we_lo_made"))
        pe = {n: sig(n, per) for n, per in dict(
            g_ps=FT, u_ps=FT, dn_ps=FT, z2_ps=TILES, z3_ps=TILES, f_ps=TILES).items()}
        act = {n: sig(n, per) for n, per in dict(
            silu_made=FT, m_hi_made=FT, gu_hi_made=FT, dn_hi_made=FT, z2_hi_made=TILES, z3_hi_made=TILES).items()}
        dve = {n: sig(n, per) for n, per in dict(
            m_made=FT, m_lo_made=FT, dn_lo_made=FT, z2_lo_made=TILES, z3_lo_made=TILES,
            bn_h=TILES, mv_h=TILES, z2_made=TILES,
            h2_made=TILES, bn_1=TILES, mv_1=TILES, n1_made=TILES, bn_2=TILES, mv_2=TILES, z3_made=TILES,
            f_made=TILES, bn_3=TILES, mv_3=TILES, n3_made=TILES).items()}
        pool = {n: sig(n, per) for n, per in dict(
            gu_lo_made=FT, st_h=3 * TILES, sc_h=TILES, st_1=3, sc_1=1, st_2=3, sc_2=1, st_3=3 * TILES, sc_3=TILES,
            x1_made=TILES, out_made=TILES).items()}
        s = {**pe, **act, **dve, **pool}
        last_out = sig("last_out", 1, False)
        TURNED_ALREADY = ("z2_ps", "z2_hi_made", "z2_lo_made", "z2_made", "bn_h", "mv_h", "st_h", "sc_h")

        passed_pool, passed_vector = (ctx.enter_context(nc.semaphore(n)) for n in ("passed_pool", "passed_vector"))

        block = ctx.enter_context(nc.Block())
        x_blocks = x.rearrange("(b i c p) d -> b i p c d", b=BATCH, i=BLOCKS, c=CPB)
        o_tiles = out.rearrange("(b i c p) d -> b i c p d", b=BATCH, i=BLOCKS, c=CPB)

        def zts(t, j, first, count):
            return t[:, bass.ds((j % 2) * ZT + first, count)]

        def zt_tile(t, j, u):
            return zts(t, j, 0, ZT).rearrange("p (k t) -> p k t", k=KD)[:, :, u * P:(u + 1) * P]

        end_z3 = [w_gu[:, u, 0, 0:D] for u in range(TILES)]
        end_fo = [w_gu[:, u, 1, 0:D] for u in range(TILES)]
        end_hi = [gu_hi[:, u // 2, :, u % 2, :] for u in range(TILES)]
        end_lo = [gu_lo[:, u // 2, :, u % 2, :] for u in range(TILES)]
        end_turned = [p_x, p_g, p_u, p_m[0]]
        end_linear = [p_f, p_m[1], p_m[2], p_m[3]]
        HALF = TILES // 2
        LAST = BLOCKS - 1

        Z3_AT = {3 + 2 * u: u for u in range(TILES)}
        F_AT = {4 + 2 * u: u for u in range(TILES)}
        OUT_AT = {5 + 2 * u: u for u in range(TILES)}
        STORE_AT = {6 + 2 * u: u for u in range(TILES)}
        LORA_AT = {2 + k: k for k in range(KD)}

        @block.sync
        def _(sp):
            def load_tile(j, u):
                sp.wait_ge(s["z2_ps"].sem, s["z2_ps"].at(j, u - 1))
                sp.dma_start(hz[:, u % 2, :], h_scratch[bass.ds(j * TILES + u, 1)].rearrange("o p d -> (o p) d"))\
                    .then_inc(hz_in[u % 2].sem, 16)

            def load_hr(j):
                sp.dma_start(hr[:, :, :], h_scratch[bass.ds(j * TILES, TILES)].rearrange("u p d -> p u d"))\
                    .then_inc(hr_in.sem, 16)

            def load_x1(j):
                for b in range(BATCH):
                    sp.dma_start(x1[:, b * CPB:(b + 1) * CPB, :], x_blocks[b, bass.ds(j, 1)].rearrange("o p c d -> (o p) c d"))\
                        .then_inc(x1_in.sem, 16)

            def store(t, u):
                sp.wait_ge(s["out_made"].sem, s["out_made"].at(t, u + 1))
                sp.dma_start(o_tiles[u // CPB, bass.ds(t, 1), u % CPB].rearrange("o p d -> (o p) d"), fo[:, :])\
                    .then_inc(out_done.sem, 16)

            def load_piece(c):
                cols = slice(c * PIECE * P, (c + 1) * PIECE * P)
                for n, w in enumerate((gate, up)):
                    sp.dma_start(w_gu[:, :, n, cols], w[:, cols].rearrange("(k p) f -> p k f", p=P))\
                        .then_inc(piece_in[c].sem, 16)
                sp.dma_start(w_dn[:, c * PIECE:(c + 1) * PIECE, :],
                             down[cols, :].rearrange("(f p) d -> p f d", p=P)).then_inc(piece_in[c].sem, 16)

            out_done.seed(sp)
            sp.dma_start(ln2_sb[:, :], ln2).then_inc(par_in.sem, 16)
            load_piece(0)
            load_piece(1)
            for dst, src in ((z3, lora_a), (fo, lora_b), (coef, lora_coef), (bias, ffn_bias)):
                sp.dma_start(dst[:, :], src).then_inc(lora_in.sem, 16)
            sp.dma_start(x1[:, :, :], w_ffn.rearrange("(k p) o -> p k o", p=P)).then_inc(wt_in.sem, 16)
            for c in range(2, PIECES):
                load_piece(c)

            def body(j, tail, more):
                if tail:
                    sp.wait_ge(s["x1_made"].sem, s["x1_made"].at(j - 1))
                load_hr(j)
                if more:
                    load_tile(j + 1, 0)
                for u in range(TILES):
                    if more and u + 1 < TILES:
                        load_tile(j + 1, u + 1)
                    if tail:
                        store(j - 1, u)
                if not tail:
                    sp.wait_ge(we_lo_made.sem, we_lo_made.at(0, 1))
                load_x1(j)

            body(0, False, True)
            with nc.sync.Fori(1, BLOCKS - 1) as j:
                body(j, True, True)
            body(BLOCKS - 1, True, False)
            for u in range(TILES):
                if u < TILES - 1:
                    sp.wait_ge(s["out_made"].sem, s["out_made"].at(LAST, u + 1))
                else:
                    sp.wait_ge(last_out.sem, last_out.at(0))
                sp.dma_start(o_tiles[u // CPB, BLOCKS - 1, u % CPB], end_fo[u]).then_inc(out_done.sem, 16)
            sp.wait_ge(out_done.sem, out_done.at(BLOCKS - 1))

        @block.tensor
        def _(t):
            for n, v in pe.items():
                v.seed(t, n in TURNED_ALREADY)

            def turn_z2(j, u):
                t.wait_ge(s["z2_made"].sem, s["z2_made"].at(j, u + 1))
                t.wait_ge(s["z2_lo_made"].sem, s["z2_lo_made"].at(j, u))
                for k in range(KD):
                    ins = nc.tensor.transpose(p_x[:, k * P:(k + 1) * P], hz[:, u % 2, k * P:(k + 1) * P], ident[:, :])
                ins.then_inc(s["z2_ps"].sem, 1)

            def turn_z3(j, u, more):
                t.wait_ge(s["z3_made"].sem, s["z3_made"].at(j, u + 1))
                t.wait_ge(s["z3_lo_made"].sem, s["z3_lo_made"].at(j, u))
                if more:
                    t.wait_ge(s["z2_lo_made"].sem, s["z2_lo_made"].at(j + 2, u))
                for k in range(KD):
                    ins = nc.tensor.transpose(p_x[:, k * P:(k + 1) * P], z3[:, k * P:(k + 1) * P], ident[:, :])
                ins.then_inc(s["z3_ps"].sem, 1)

            def linear(j, u):
                t.wait_ge(s["z3_lo_made"].sem, s["z3_lo_made"].at(j, u + 1))
                t.wait_ge(s["f_made"].sem, s["f_made"].at(j, u))
                n = 0
                for k in range(KD):
                    for l, r in split_passes(z3t_hi, z3t_lo, we_hi, we_lo):
                        ins = nc.tensor.matmul(p_f[:, :], l[:, k, :], r[:, k, :], start=(n == 0), stop=(n == 3 * KD - 1))
                        n += 1
                ins.then_inc(s["f_ps"].sem, 1)

            def gate_up(j, f, which):
                n = 0
                bank = (p_g, p_u)[which]
                for k in range(KD):
                    for l, r in split_passes(gu_hi, gu_lo, zt_hi, zt_lo):
                        ins = nc.tensor.matmul(bank[:, :], l[:, f % 2, k, which, :], zts(r, j, k * BT, BT),
                                               start=(n == 0), stop=(n == 3 * KD - 1))
                        n += 1
                return ins

            def down_part(j, f, last=False):
                t.wait_ge(s["m_hi_made"].sem, s["m_hi_made"].at(j, f + 1))
                t.wait_ge(s["m_lo_made"].sem, s["m_lo_made"].at(j, f + 1))
                t.wait_ge(s["dn_hi_made"].sem, s["dn_hi_made"].at(j, f + 1))
                t.wait_ge(s["dn_lo_made"].sem, s["dn_lo_made"].at(j, f + 1))
                if f == 0:
                    t.wait_ge(s["h2_made"].sem, s["h2_made"].at(j - 1))
                for u in range(TILES):
                    for n, (l, r) in enumerate(split_passes(m_hi, m_lo, dn_hi, dn_lo)):
                        ins = nc.tensor.matmul(p_m[u][:, :], l[:, f % 2, u * P:(u + 1) * P], r[:, f % 2, :],
                                               start=(f == 0 and n == 0), stop=(f == FT - 1 and n == 2))
                    if last:
                        ins.then_inc(s["dn_ps"].sem, 1)
                if not last:
                    ins.then_inc(s["dn_ps"].sem, 1)

            def body(j, tail, more):
                t.wait_ge(s["z2_lo_made"].sem, s["z2_lo_made"].at(j))
                for f in range(FT):
                    t.wait_ge(s["gu_hi_made"].sem, s["gu_hi_made"].at(j, f + 1))
                    t.wait_ge(s["gu_lo_made"].sem, s["gu_lo_made"].at(j, f + 1))
                    t.wait_ge(s["silu_made"].sem, s["silu_made"].at(j, f))
                    gate_up(j, f, 0).then_inc(s["g_ps"].sem, 1)
                    t.wait_ge(s["m_made"].sem, s["m_made"].at(j, f))
                    gate_up(j, f, 1).then_inc(s["u_ps"].sem, 1)
                    if f:
                        down_part(j, f - 1)
                    if not tail and f in LORA_AT:
                        k = LORA_AT[f]
                        t.wait_ge(lora_scaled.sem, lora_scaled.at(0, 1))
                        if k:
                            t.wait_ge(lora_added.sem, lora_added.at(0, k))
                        nc.tensor.matmul(p_f[:, :], z3[:, k * P:(k + 1) * P], fo[:, :], start=True, stop=True)\
                            .then_inc(lora_ps.sem, 1)
                    if tail and f in Z3_AT:
                        turn_z3(j - 1, Z3_AT[f], more)
                    if tail and f in F_AT:
                        linear(j - 1, F_AT[f])
                    if more and f in F_AT:
                        if tail:
                            t.wait_ge(s["z3_lo_made"].sem, s["z3_lo_made"].at(j - 1, F_AT[f] + 1))
                        turn_z2(j + 1, F_AT[f])
                down_part(j, FT - 1, not more)

            t.wait_ge(consts.sem, consts.at(0, 2))
            body(0, False, True)
            with nc.tensor.Fori(1, BLOCKS - 1) as j:
                body(j, True, True)
            body(BLOCKS - 1, True, False)

            def end_turn(u):
                t.wait_ge(s["z3_made"].sem, s["z3_made"].at(LAST, u + 1))
                for k in range(KD):
                    ins = nc.tensor.transpose(end_turned[u][:, k * P:(k + 1) * P], end_z3[u][:, k * P:(k + 1) * P],
                                              ident[:, :])
                ins.then_inc(s["z3_ps"].sem, 1)

            def end_product(u):
                t.wait_ge(s["z3_lo_made"].sem, s["z3_lo_made"].at(LAST, u + 1))
                n = 0
                for k in range(KD):
                    for l, r in split_passes(end_hi[u], end_lo[u], we_hi, we_lo):
                        ins = nc.tensor.matmul(end_linear[u][:, :], l[:, k, :], r[:, k, :], start=(n == 0),
                                               stop=(n == 3 * KD - 1))
                        n += 1
                ins.then_inc(s["f_ps"].sem, 1)

            for u in range(HALF):
                end_turn(u)
            end_product(0)
            for u in range(HALF, TILES):
                end_turn(u)
            for u in range(1, TILES):
                end_product(u)

        @block.scalar
        def _(a):
            for n, v in act.items():
                v.seed(a, n in TURNED_ALREADY)

            def split_gu(j, n, f):
                cols = slice(f * P, (f + 1) * P)
                a.wait_ge(w_scaled.sem, w_scaled.at(0, (f // PIECE + 1) * KD))
                a.wait_ge(s["u_ps"].sem, s["u_ps"].at(j, n))
                for w in range(2):
                    ins = nc.scalar.copy(gu_hi[:, f % 2, :, w, :], w_gu[:, :, w, cols])
                ins.then_inc(s["gu_hi_made"].sem, 1)

            def split_dn(j, f):
                a.wait_ge(w_scaled.sem, w_scaled.at(0, (f // PIECE + 1) * KD))
                a.wait_ge(s["dn_ps"].sem, s["dn_ps"].at(j, f - 1))
                nc.scalar.copy(dn_hi[:, f % 2, :], w_dn[:, f, :]).then_inc(s["dn_hi_made"].sem, 1)

            def turn_z2(j, u):
                a.wait_ge(s["z2_ps"].sem, s["z2_ps"].at(j, u + 1))
                a.wait_ge(s["u_ps"].sem, s["u_ps"].at(j - 2))
                nc.scalar.copy(zt_tile(zt_hi, j, u), p_x[:, :].rearrange("p (k t) -> p k t", k=KD))\
                    .then_inc(s["z2_hi_made"].sem, 1)

            def turn_z3(j, u):
                a.wait_ge(s["z3_ps"].sem, s["z3_ps"].at(j, u + 1))
                a.wait_ge(s["f_ps"].sem, s["f_ps"].at(j, u))
                nc.scalar.copy(z3t_hi[:, :, :].rearrange("p k t -> p (k t)"), p_x[:, :])\
                    .then_inc(s["z3_hi_made"].sem, 1)

            def body(j, tail, more):
                for f in range(FT):
                    if f < FT - 1:
                        if f or tail:
                            split_gu(j, f, f + 1)
                    elif more:
                        split_gu(j, f, 0)
                    if f or tail:
                        split_dn(j, f)
                    if tail and f - 1 in Z3_AT:
                        turn_z3(j - 1, Z3_AT[f - 1])
                    if more and f - 1 in F_AT:
                        turn_z2(j + 1, F_AT[f - 1])
                    a.wait_ge(s["g_ps"].sem, s["g_ps"].at(j, f + 1))
                    a.wait_ge(s["m_made"].sem, s["m_made"].at(j, f))
                    nc.scalar.activation(g32[:, :], p_g[:, :], ACT.Silu).then_inc(s["silu_made"].sem, 1)
                    a.wait_ge(s["m_made"].sem, s["m_made"].at(j, f + 1))
                    a.wait_ge(s["dn_ps"].sem, s["dn_ps"].at(j, f - 1))
                    nc.scalar.copy(m_hi[:, f % 2, :], m32[:, :]).then_inc(s["m_hi_made"].sem, 1)
                    if not (f or tail):
                        split_dn(j, f)
                    if not tail and f == FT - 3:
                        a.wait_ge(lora_added.sem, lora_added.at(0, KD))
                        nc.scalar.copy(we_hi[:, :, :], x1[:, :, :]).then_inc(we_hi_made.sem, 1)

            a.sem_inc(s["gu_hi_made"].sem, 2)
            body(0, False, True)
            with nc.scalar.Fori(1, BLOCKS - 1) as j:
                body(j, True, True)
            body(BLOCKS - 1, True, False)
            for u in range(TILES):
                a.wait_ge(s["z3_ps"].sem, s["z3_ps"].at(LAST, u + 1))
                nc.scalar.copy(end_hi[u], end_turned[u][:, :].rearrange("p (k t) -> p k t", k=KD))\
                    .then_inc(s["z3_hi_made"].sem, 1)

        H, N1, N2, N3 = range(4)

        @block.gpsimd
        def _(g):
            for n, v in pool.items():
                v.seed(g, n in TURNED_ALREADY)
            nc.gpsimd.memset(mhalf[:, :], -0.5).then_inc(consts.sem, 1)
            nc.gpsimd.memset(ident[:, :], 0.0).then_inc(ident_zero.sem, 1)
            g.wait_ge(ident_zero.sem, ident_zero.at(0, 1))
            nc.gpsimd.affine_select(out=ident[:, :], in_=ident[:, :], compare_op=ALU.not_equal, fill=1.0, base=0,
                                    pattern=[[-1, P]], channel_multiplier=1).then_inc(consts.sem, 1)
            g.wait_ge(consts.sem, consts.at(0, 2))

            def chain(step, made, j, n0, row, cols, rms):
                mean, var = mv[:, row, cols, 0], mv[:, row, cols, 1]
                t0, t1, t2, t3 = (tmp[:, row, n, cols] for n in range(4))

                def then(n, ins):
                    ins.then_inc(step.sem, 1)
                    g.wait_ge(step.sem, step.at(j, n0 + n))
                    waits_apart(g, passed_pool)

                if rms:
                    then(1, nc.gpsimd.tensor_tensor(t0, mean, mean, ALU.mult))
                    then(2, nc.gpsimd.tensor_tensor(t1, t0, var, ALU.add))
                    then(3, nc.gpsimd.tensor_scalar(t2, t1, EPS, 1.0, ALU.add, ALU.mult))
                    nc.gpsimd.tensor_tensor(scl[:, row, 0, cols], t2, mhalf[:, cols], ALU.pow).then_inc(made.sem, 1)
                else:
                    then(1, nc.gpsimd.tensor_scalar(t2, var, EPS, 1.0, ALU.add, ALU.mult))
                    then(2, nc.gpsimd.tensor_tensor(scl[:, row, 0, cols], t2, mhalf[:, cols], ALU.pow))
                    then(3, nc.gpsimd.tensor_tensor(t0, mean, scl[:, row, 0, cols], ALU.mult))
                    nc.gpsimd.tensor_scalar(scl[:, row, 1, cols], t0, -1.0, 1.0, ALU.mult, ALU.mult)\
                        .then_inc(made.sem, 1)

            def split_lo(j, n, f):
                cols = slice(f * P, (f + 1) * P)
                g.wait_ge(s["gu_hi_made"].sem, s["gu_hi_made"].at(j, n))
                for w in range(2):
                    ins = nc.gpsimd.tensor_tensor(gu_lo[:, f % 2, :, w, :], w_gu[:, :, w, cols],
                                                  gu_hi[:, f % 2, :, w, :].bitcast(F32), ALU.subtract)
                ins.then_inc(s["gu_lo_made"].sem, 1)

            def norm_h(j, u):
                g.wait_ge(s["mv_h"].sem, s["mv_h"].at(j, u + 1))
                g.wait_ge(s["z2_made"].sem, s["z2_made"].at(j, u))
                waits_apart(g, passed_pool)
                chain(s["st_h"], s["sc_h"], j, 3 * u, H, slice(u, u + 1), True)

            def end(j, u):
                g.wait_ge(s["n3_made"].sem, s["n3_made"].at(j, u + 1))
                nc.gpsimd.tensor_tensor(fo[:, :], fo[:, :], x1[:, u, :], ALU.add).then_inc(s["out_made"].sem, 1)

            def norm_3(j, u):
                g.wait_ge(s["mv_3"].sem, s["mv_3"].at(j, u + 1))
                waits_apart(g, passed_pool)
                chain(s["st_3"], s["sc_3"], j, 3 * u, N3, slice(u, u + 1), False)

            def norm_1(j):
                g.wait_ge(s["mv_1"].sem, s["mv_1"].at(j))
                g.wait_ge(s["n1_made"].sem, s["n1_made"].at(j - 1))
                waits_apart(g, passed_pool)
                chain(s["st_1"], s["sc_1"], j, 0, N1, slice(0, TILES), False)

            def first_sum(j):
                g.wait_ge(x1_in.sem, x1_in.at(j))
                for u in range(TILES):
                    g.wait_ge(s["n1_made"].sem, s["n1_made"].at(j, u + 1))
                    nc.gpsimd.tensor_tensor(x1[:, u, :], x1[:, u, :], hr[:, u, :], ALU.add)\
                        .then_inc(s["x1_made"].sem, 1)

            def norm_2(j):
                g.wait_ge(s["mv_2"].sem, s["mv_2"].at(j))
                g.wait_ge(s["z3_made"].sem, s["z3_made"].at(j - 1))
                waits_apart(g, passed_pool)
                chain(s["st_2"], s["sc_2"], j, 0, N2, slice(0, TILES), False)

            def body(j, tail, more):
                for f in range(FT):
                    if f < FT - 1:
                        if f or tail:
                            split_lo(j, f + 2, f + 1)
                    elif more:
                        split_lo(j, FT + 1, 0)
                    if tail:
                        if f in STORE_AT:
                            end(j - 1, STORE_AT[f])
                        if f == 0:
                            norm_1(j - 1)
                        if f == 1:
                            first_sum(j - 1)
                        if f == 2:
                            norm_2(j - 1)
                        if f in OUT_AT:
                            norm_3(j - 1, OUT_AT[f])
                    if more and f in Z3_AT:
                        norm_h(j + 1, Z3_AT[f])

            g.sem_inc(s["gu_lo_made"].sem, 2)
            body(0, False, True)
            with nc.gpsimd.Fori(1, BLOCKS - 1) as j:
                body(j, True, True)
            body(BLOCKS - 1, True, False)
            for row, n in ((N1, "1"), (N2, "2")):
                for half in range(2):
                    g.wait_ge(s["mv_" + n].sem, s["mv_" + n].at(LAST, HALF * (half + 1)))
                    waits_apart(g, passed_pool)
                    chain(s["st_" + n], s["sc_" + n], LAST, 3 * half, row, slice(HALF * half, HALF * (half + 1)), False)

            def end_sum(u):
                g.wait_ge(s["n3_made"].sem, s["n3_made"].at(LAST, u + 1))
                nc.gpsimd.tensor_tensor(end_fo[u], end_fo[u], x1[:, u, :], ALU.add).then_inc(s["out_made"].sem, 1)

            for u in range(TILES):
                g.wait_ge(s["mv_3"].sem, s["mv_3"].at(LAST, u + 1))
                waits_apart(g, passed_pool)
                chain(s["st_3"], s["sc_3"], LAST, 3 * u, N3, slice(u, u + 1), False)
                if u < TILES - 1:
                    end_sum(u)

        @block.vector
        def _(v):
            for n, signal in dve.items():
                signal.seed(v, n in TURNED_ALREADY)

            def stats(src, row, u, bn_sig, mv_sig, j):
                nc.vector.bn_stats(bn[:, row, u, :], src).then_inc(bn_sig.sem, 1)
                v.wait_ge(bn_sig.sem, bn_sig.at(j, u + 1))
                waits_apart(v, passed_vector)
                nc.vector.bn_aggr(mv[:, row, u, :], bn[:, row, u, :]).then_inc(mv_sig.sem, 1)

            def scaled(dst, src, row, u):
                return nc.vector.tensor_scalar(dst, src, scl[:, row, 0, u:u + 1], scl[:, row, 1, u:u + 1], ALU.mult, ALU.add)

            def scale_weights(c):
                v.wait_ge(piece_in[c].sem, piece_in[c].at(0, 48))
                v.wait_ge(par_in.sem, par_in.at(0, 16))
                cols = slice(c * PIECE * P, (c + 1) * PIECE * P)
                for k in range(KD):
                    nc.vector.tensor_scalar(w_gu[:, k, :, cols], w_gu[:, k, :, cols], ln2_sb[:, k:k + 1], None, ALU.mult)\
                        .then_inc(w_scaled.sem, 1)

            def split_dn(j, f):
                v.wait_ge(s["dn_hi_made"].sem, s["dn_hi_made"].at(j, f + 1))
                nc.vector.tensor_tensor(dn_lo[:, f % 2, :], w_dn[:, f, :], dn_hi[:, f % 2, :].bitcast(F32), ALU.subtract)\
                    .then_inc(s["dn_lo_made"].sem, 1)

            def norm_h(j, u):
                v.wait_ge(hz_in[u % 2].sem, hz_in[u % 2].at(j - 1, 16 * (u // 2 + 1)))
                v.wait_ge(s["sc_h"].sem, s["sc_h"].at(j - 1, u + 1))
                stats(hz[:, u % 2, :], H, u, s["bn_h"], s["mv_h"], j)

            def make_z2(j, u):
                v.wait_ge(s["sc_h"].sem, s["sc_h"].at(j, u + 1))
                nc.vector.tensor_scalar(hz[:, u % 2, :], hz[:, u % 2, :], scl[:, H, 0, u:u + 1], None, ALU.mult)\
                    .then_inc(s["z2_made"].sem, 1)

            def turn_z2(j, u):
                v.wait_ge(s["z2_hi_made"].sem, s["z2_hi_made"].at(j, u + 1))
                nc.vector.tensor_tensor(zt_tile(zt_lo, j, u), p_x[:, :].rearrange("p (k t) -> p k t", k=KD),
                                        zt_tile(zt_hi, j, u).bitcast(F32), ALU.subtract)\
                                            .then_inc(s["z2_lo_made"].sem, 1)

            def sums(j):
                v.wait_ge(hr_in.sem, hr_in.at(j))
                v.wait_ge(s["dn_ps"].sem, s["dn_ps"].at(j))
                v.wait_ge(s["sc_1"].sem, s["sc_1"].at(j - 1))
                for u in range(TILES):
                    nc.vector.tensor_tensor(hr[:, u, :], p_m[u][:, :], hr[:, u, :], ALU.add)\
                        .then_inc(s["h2_made"].sem, 1)

            def first_stats(j):
                for u in range(TILES):
                    v.wait_ge(s["h2_made"].sem, s["h2_made"].at(j, u + 1))
                    stats(hr[:, u, :], N1, u, s["bn_1"], s["mv_1"], j)

            def first_norm(j):
                v.wait_ge(s["sc_1"].sem, s["sc_1"].at(j))
                for u in range(TILES):
                    scaled(hr[:, u, :], hr[:, u, :], N1, u).then_inc(s["n1_made"].sem, 1)

            def second_stats(j):
                v.wait_ge(s["sc_2"].sem, s["sc_2"].at(j - 1))
                for u in range(TILES):
                    v.wait_ge(s["x1_made"].sem, s["x1_made"].at(j, u + 1))
                    stats(x1[:, u, :], N2, u, s["bn_2"], s["mv_2"], j)

            def make_z3(j, u):
                v.wait_ge(s["sc_2"].sem, s["sc_2"].at(j))
                v.wait_ge(s["z3_ps"].sem, s["z3_ps"].at(j, u))
                scaled(z3[:, :], x1[:, u, :], N2, u).then_inc(s["z3_made"].sem, 1)

            def turn_z3(j, u):
                v.wait_ge(s["z3_hi_made"].sem, s["z3_hi_made"].at(j, u + 1))
                nc.vector.tensor_tensor(z3t_lo[:, :, :].rearrange("p k t -> p (k t)"), p_x[:, :],
                                        z3t_hi[:, :, :].rearrange("p k t -> p (k t)").bitcast(F32), ALU.subtract)\
                    .then_inc(s["z3_lo_made"].sem, 1)

            def linear(j, u):
                v.wait_ge(s["f_ps"].sem, s["f_ps"].at(j, u + 1))
                v.wait_ge(out_done.sem, out_done.at(j, 16 * u))
                nc.vector.tensor_tensor(fo[:, :], p_f[:, :], bias[:, :], ALU.add).then_inc(s["f_made"].sem, 1)
                v.wait_ge(s["f_made"].sem, s["f_made"].at(j, u + 1))
                v.wait_ge(s["sc_3"].sem, s["sc_3"].at(j - 1, u + 1))
                stats(fo[:, :], N3, u, s["bn_3"], s["mv_3"], j)

            def last_norm(j, u):
                v.wait_ge(s["sc_3"].sem, s["sc_3"].at(j, u + 1))
                scaled(fo[:, :], fo[:, :], N3, u).then_inc(s["n3_made"].sem, 1)

            def body(j, tail, more):
                for f in range(FT):
                    if f or tail:
                        split_dn(j, f)
                    if tail:
                        if f == 0:
                            sums(j - 1)
                        if f == 1:
                            first_norm(j - 1)
                        if f == 2:
                            second_stats(j - 1)
                        if f - 1 in Z3_AT:
                            turn_z3(j - 1, Z3_AT[f - 1])
                        if f - 1 in F_AT:
                            linear(j - 1, F_AT[f - 1])
                    if more and f - 1 in F_AT:
                        turn_z2(j + 1, F_AT[f - 1])
                    v.wait_ge(s["u_ps"].sem, s["u_ps"].at(j, f + 1))
                    v.wait_ge(s["silu_made"].sem, s["silu_made"].at(j, f + 1))
                    v.wait_ge(s["m_hi_made"].sem, s["m_hi_made"].at(j, f))
                    v.wait_ge(s["m_lo_made"].sem, s["m_lo_made"].at(j, f))
                    nc.vector.tensor_tensor(m32[:, :], p_u[:, :], g32[:, :], ALU.mult).then_inc(s["m_made"].sem, 1)
                    v.wait_ge(s["m_hi_made"].sem, s["m_hi_made"].at(j, f + 1))
                    nc.vector.tensor_tensor(m_lo[:, f % 2, :], m32[:, :], m_hi[:, f % 2, :].bitcast(F32), ALU.subtract)\
                        .then_inc(s["m_lo_made"].sem, 1)
                    if not tail:
                        if f == 0:
                            scale_weights(0)
                        if f % PIECE == 0 and f // PIECE + 1 < PIECES:
                            scale_weights(f // PIECE + 1)
                        if f == 0:
                            split_dn(j, f)
                        if f == 1:
                            v.wait_ge(lora_in.sem, lora_in.at(0, 64))
                            nc.vector.tensor_scalar(fo[:, :], fo[:, :], coef[:, :], LORA_SCALE, ALU.mult, ALU.mult)\
                                .then_inc(lora_scaled.sem, 1)
                        if f in LORA_AT:
                            k = LORA_AT[f]
                            v.wait_ge(lora_ps.sem, lora_ps.at(0, k + 1))
                            v.wait_ge(wt_in.sem, wt_in.at(0, 16))
                            nc.vector.tensor_tensor(x1[:, k, :], p_f[:, :], x1[:, k, :], ALU.add)\
                                .then_inc(lora_added.sem, 1)
                        if f == FT - 2:
                            v.wait_ge(we_hi_made.sem, we_hi_made.at(0, 1))
                            nc.vector.tensor_tensor(we_lo[:, :, :], x1[:, :, :], we_hi[:, :, :].bitcast(F32), ALU.subtract)\
                                .then_inc(we_lo_made.sem, 1)
                    if tail:
                        if f == 0:
                            first_stats(j - 1)
                        if f == 2:
                            make_z3(j - 1, 0)
                        if f in F_AT and F_AT[f] + 1 < TILES:
                            make_z3(j - 1, F_AT[f] + 1)
                        if f in OUT_AT:
                            last_norm(j - 1, OUT_AT[f])
                    if more:
                        if f + 1 in Z3_AT:
                            norm_h(j + 1, Z3_AT[f + 1])
                        if f in Z3_AT:
                            make_z2(j + 1, Z3_AT[f])

            body(0, False, True)
            with nc.vector.Fori(1, BLOCKS - 1) as j:
                body(j, True, True)
            body(BLOCKS - 1, True, False)
            v.wait_ge(hr_in.sem, hr_in.at(BLOCKS - 1))
            for half in range(2):
                tiles = range(HALF * half, HALF * (half + 1))
                for u in tiles:
                    v.wait_ge(s["dn_ps"].sem, s["dn_ps"].at(LAST, FT + u))
                    nc.vector.tensor_tensor(hr[:, u, :], p_m[u][:, :], hr[:, u, :], ALU.add)\
                        .then_inc(s["h2_made"].sem, 1)
                for u in tiles:
                    v.wait_ge(s["h2_made"].sem, s["h2_made"].at(LAST, u + 1))
                    stats(hr[:, u, :], N1, u, s["bn_1"], s["mv_1"], LAST)
            v.wait_ge(x1_in.sem, x1_in.at(BLOCKS - 1))
            for half in range(2):
                tiles = range(HALF * half, HALF * (half + 1))
                v.wait_ge(s["sc_1"].sem, s["sc_1"].at(LAST, half + 1))
                for u in tiles:
                    scaled(hr[:, u, :], hr[:, u, :], N1, u).then_inc(s["n1_made"].sem, 1)
                for u in tiles:
                    v.wait_ge(s["n1_made"].sem, s["n1_made"].at(LAST, u + 1))
                    nc.vector.tensor_tensor(x1[:, u, :], x1[:, u, :], hr[:, u, :], ALU.add)\
                        .then_inc(s["x1_made"].sem, 1)
                for u in tiles:
                    v.wait_ge(s["x1_made"].sem, s["x1_made"].at(LAST, u + 1))
                    stats(x1[:, u, :], N2, u, s["bn_2"], s["mv_2"], LAST)

            def end_low(u):
                v.wait_ge(s["z3_hi_made"].sem, s["z3_hi_made"].at(LAST, u + 1))
                nc.vector.tensor_tensor(end_lo[u], end_turned[u][:, :].rearrange("p (k t) -> p k t", k=KD),
                                        end_hi[u].bitcast(F32), ALU.subtract).then_inc(s["z3_lo_made"].sem, 1)

            def end_add(u):
                v.wait_ge(s["f_ps"].sem, s["f_ps"].at(LAST, u + 1))
                nc.vector.tensor_tensor(end_fo[u], end_linear[u][:, :], bias[:, :], ALU.add)\
                    .then_inc(s["f_made"].sem, 1)
                v.wait_ge(s["f_made"].sem, s["f_made"].at(LAST, u + 1))
                stats(end_fo[u], N3, u, s["bn_3"], s["mv_3"], LAST)

            def end_norm(u):
                v.wait_ge(s["sc_3"].sem, s["sc_3"].at(LAST, u + 1))
                scaled(end_fo[u], end_fo[u], N3, u).then_inc(s["n3_made"].sem, 1)

            for half in range(2):
                tiles = range(HALF * half, HALF * (half + 1))
                v.wait_ge(s["sc_2"].sem, s["sc_2"].at(LAST, half + 1))
                for u in tiles:
                    scaled(end_z3[u], x1[:, u, :], N2, u).then_inc(s["z3_made"].sem, 1)
                for u in tiles:
                    end_low(u)
            end_add(0)
            for u in range(1, TILES):
                end_add(u)
                end_norm(u - 1)
            end_norm(TILES - 1)
            last = TILES - 1
            v.wait_ge(s["n3_made"].sem, s["n3_made"].at(LAST))
            nc.vector.tensor_tensor(end_fo[last], end_fo[last], x1[:, last, :], ALU.add).then_inc(last_out.sem, 1)


def kernel(**inputs):
    import numpy as np
    import concourse.bacc as _bacc
    from concourse.bass_utils import run_bass_kernel_spmd as _run

    a = {k.replace("L0_attn_", "").replace("L0_ffn_", "ffn_"): np.asarray(v) for k, v in inputs.items()}
    columns = lambda w, n: w.reshape(n, P).T
    every = lambda w: np.broadcast_to(w, (P, w.size))
    arrays = {
        "x": a["hidden_states"].reshape(BATCH * SEQ, D_MODEL),
        "w_in": a["w_in"].T,
        "w_out": a["w_out"].T,
        "conv_w": a["conv_w"].reshape(CONV, P, TAPS).transpose(1, 0, 2),
        "conv_b": columns(a["conv_b"], CONV),
        "a_log": every(a["A_log"]), "d_skip": every(a["D"]), "dt_bias": every(a["dt_bias"]),
        "ln1": columns(a["ln1_w"], KD), "ln2": columns(a["ln2_w"], KD),
        "gate": a["gate_w"].T, "up": a["up_w"].T, "down": a["down_w"].T,
        "lora_a": a["ffn_lora_A"].reshape(RANKS, D_MODEL),
        "lora_b": a["ffn_lora_B"].transpose(0, 2, 1).reshape(RANKS, D_MODEL),
        "w_ffn": a["ffn_W"].T,
        "ffn_bias": every(a["ffn_bias"]),
        "lora_coef": np.repeat(a["ffn_lora_weights"], RANKS // a["ffn_lora_weights"].size).reshape(RANKS, 1),
    }
    nc = _bacc.Bacc("TRN2", target_bir_lowering=False, num_devices=1)
    arrays = {n: np.ascontiguousarray(v) for n, v in arrays.items()}
    aps = {n: nc.dram_tensor(n, v.shape, F32, kind="ExternalInput").ap() for n, v in arrays.items()}
    h_scratch = nc.dram_tensor("h_scratch", (BLOCKS * TILES, P, D_MODEL), F32, kind="Internal").ap()
    out = nc.dram_tensor("out", (BATCH, SEQ, D_MODEL), F32, kind="ExternalOutput").ap()
    sandwich_program(nc, h_scratch=h_scratch, out=out.rearrange("b s d -> (b s) d"), **aps)
    r = _run(nc, [arrays], core_ids=[0])
    return r.results[0]["out"]
```
